# Optimizing a Trainium2 kernel written in Bass

```python
import numpy as np
import jax
import jax.numpy as jnp

def _softmax(x, axis=-1):
    return jax.nn.softmax(x, axis=axis)

def _gelu(x):
    return jax.nn.gelu(x, approximate=True)

def _silu(x):
    return jax.nn.silu(x)

def _sigmoid(x):
    return jax.nn.sigmoid(x)

def _layernorm(x, axis=-1, eps=1e-05):
    m = jnp.mean(x, axis=axis, keepdims=True)
    v = jnp.var(x, axis=axis, keepdims=True)
    return (x - m) / jnp.sqrt(v + eps)

def _scatter_add(tgt, idx, src, axis=0):
    return tgt.at[idx].add(src)

def _segment_sum(src, seg, n):
    return jax.ops.segment_sum(src, seg, n)
kernel_name = 'mk_adaln_d1_jaxref_r4_23e56a'

def setup_inputs(seed: int=0):
    np.random.seed(seed)
    _w = jnp.asarray

    def _L0_attn_setup():
        import jax, jax.numpy as jnp
        import numpy as np
        B, N, D, H, DH, M = (4, 1024, 256, 16, 64, 64)
        EPS = 0.0001

        def softmax_kernel(data, P, is_query):
            dn = data.shape[-1] ** (-0.25)
            ratio = P.shape[0] ** (-0.5)
            dd = jnp.einsum('bhnd,md->bhnm', dn * data, P)
            diag = (jnp.sum(data * data, axis=-1) * 0.5 * dn * dn)[..., None]
            if is_query:
                mx = jnp.max(dd, axis=-1, keepdims=True)
            else:
                mx = jnp.max(dd)
            return ratio * (jnp.exp(dd - diag - mx) + EPS)
        key = jax.random.key(seed)
        ks = jax.random.split(key, 6)
        s = 1.0 / np.sqrt(D).astype(np.float32)
        x = jax.random.normal(ks[0], (B, N, D), jnp.float32)
        Wq = jax.random.normal(ks[1], (D, H * DH), jnp.float32) * s
        Wk = jax.random.normal(ks[2], (D, H * DH), jnp.float32) * s
        Wv = jax.random.normal(ks[3], (D, H * DH), jnp.float32) * s
        Wo = jax.random.normal(ks[4], (H * DH, D), jnp.float32) * s
        bo = jnp.zeros((D,), jnp.float32)
        P = jax.random.normal(ks[5], (M, DH), jnp.float32)
        return {'x': x, 'Wq': Wq, 'Wk': Wk, 'Wv': Wv, 'Wo': Wo, 'bo': bo, 'P': P}
    _L0_attn_in = _L0_attn_setup()

    def _L0_ffn_setup():
        import jax, jax.numpy as jnp
        import numpy as np
        D_MODEL, D_FF, NUM_EXPERTS, RANK, TOP_K = (256, 1024, 8, 16, 2)
        B, S = (8, 512)

        def _expert_ffn(h, wi_w, wo_w, A, Bm):
            inter = jnp.einsum('bsd,fd->bsf', h, wi_w)
            lora = jnp.einsum('bsr,fr->bsf', jnp.einsum('bsd,rd->bsr', h, A), Bm)
            inter = jax.nn.relu(inter + lora)
            return jnp.einsum('bsf,df->bsd', inter, wo_w)
        key = jax.random.key(seed)
        ks = jax.random.split(key, 8)
        hidden_states = jax.random.normal(ks[0], (B, S, D_MODEL), dtype=jnp.float32)
        wi_w = jax.random.normal(ks[1], (D_FF, D_MODEL), dtype=jnp.float32) * (1.0 / np.sqrt(D_MODEL))
        wo_w = jax.random.normal(ks[2], (D_MODEL, D_FF), dtype=jnp.float32) * (1.0 / np.sqrt(D_FF))
        lora_As = jax.random.uniform(ks[3], (NUM_EXPERTS, RANK, D_MODEL), dtype=jnp.float32, minval=-1.0, maxval=1.0) / np.sqrt(D_MODEL)
        lora_Bs = jax.random.normal(ks[4], (NUM_EXPERTS, D_FF, RANK), dtype=jnp.float32) * 0.02
        top_k_indices = jnp.arange(TOP_K, dtype=jnp.int32)
        top_k_values = jax.random.uniform(ks[5], (TOP_K,), dtype=jnp.float32)
        return {'hidden_states': hidden_states, 'wi_w': wi_w, 'wo_w': wo_w, 'lora_As': lora_As, 'lora_Bs': lora_Bs, 'top_k_indices': top_k_indices, 'top_k_values': top_k_values}
    _L0_ffn_in = _L0_ffn_setup()
    _L0_c = _w((lambda *s: np.random.randn(*s).astype(np.float32) * 0.05)(8, 256))
    _L0_wmod = _w((lambda *s: np.random.randn(*s).astype(np.float32) * 0.05)(256, 6 * 256) * 256 ** (-0.5))
    _d = {'L0_attn_x': _L0_attn_in['x'], 'L0_attn_Wq': _L0_attn_in['Wq'], 'L0_attn_Wk': _L0_attn_in['Wk'], 'L0_attn_Wv': _L0_attn_in['Wv'], 'L0_attn_Wo': _L0_attn_in['Wo'], 'L0_attn_bo': _L0_attn_in['bo'], 'L0_attn_P': _L0_attn_in['P'], 'L0_ffn_wi_w': _L0_ffn_in['wi_w'], 'L0_ffn_wo_w': _L0_ffn_in['wo_w'], 'L0_ffn_lora_As': _L0_ffn_in['lora_As'], 'L0_ffn_lora_Bs': _L0_ffn_in['lora_Bs'], 'L0_ffn_top_k_indices': _L0_ffn_in['top_k_indices'], 'L0_ffn_top_k_values': _L0_ffn_in['top_k_values'], 'L0_c': _L0_c, 'L0_wmod': _L0_wmod}
    _x0 = _d['L0_attn_x']
    _d['L0_attn_x'] = jax.random.normal(jax.random.fold_in(jax.random.key(seed), 1), (8, 512, 256), dtype=_x0.dtype)
    del _x0
    return _d

def reference(L0_attn_x, L0_attn_Wq, L0_attn_Wk, L0_attn_Wv, L0_attn_Wo, L0_attn_bo, L0_attn_P, L0_ffn_wi_w, L0_ffn_wo_w, L0_ffn_lora_As, L0_ffn_lora_Bs, L0_ffn_top_k_indices, L0_ffn_top_k_values, L0_c, L0_wmod):

    def _L0_attn_ref(x, Wq, Wk, Wv, Wo, bo, P):
        import jax, jax.numpy as jnp
        import numpy as np
        B, N, D, H, DH, M = (4, 1024, 256, 16, 64, 64)
        EPS = 0.0001

        def softmax_kernel(data, P, is_query):
            dn = data.shape[-1] ** (-0.25)
            ratio = P.shape[0] ** (-0.5)
            dd = jnp.einsum('bhnd,md->bhnm', dn * data, P)
            diag = (jnp.sum(data * data, axis=-1) * 0.5 * dn * dn)[..., None]
            if is_query:
                mx = jnp.max(dd, axis=-1, keepdims=True)
            else:
                mx = jnp.max(dd)
            return ratio * (jnp.exp(dd - diag - mx) + EPS)
        b, n, _ = x.shape

        def proj(W):
            return (x @ W).reshape(b, n, H, DH).transpose(0, 2, 1, 3)
        q, k, v = (proj(Wq), proj(Wk), proj(Wv))
        qp = softmax_kernel(q, P, is_query=True)
        kp = softmax_kernel(k, P, is_query=False)
        k_cumsum = kp.sum(axis=-2)
        D_inv = 1.0 / jnp.einsum('bhnm,bhm->bhn', qp, k_cumsum)
        ctx = jnp.einsum('bhnm,bhne->bhme', kp, v)
        out = jnp.einsum('bhme,bhnm,bhn->bhne', ctx, qp, D_inv)
        out = out.transpose(0, 2, 1, 3).reshape(b, n, H * DH)
        return out @ Wo + bo

    def _L0_ffn_ref(hidden_states, wi_w, wo_w, lora_As, lora_Bs, top_k_indices, top_k_values):
        import jax, jax.numpy as jnp
        import numpy as np
        D_MODEL, D_FF, NUM_EXPERTS, RANK, TOP_K = (256, 1024, 8, 16, 2)
        B, S = (8, 512)

        def _expert_ffn(h, wi_w, wo_w, A, Bm):
            inter = jnp.einsum('bsd,fd->bsf', h, wi_w)
            lora = jnp.einsum('bsr,fr->bsf', jnp.einsum('bsd,rd->bsr', h, A), Bm)
            inter = jax.nn.relu(inter + lora)
            return jnp.einsum('bsf,df->bsd', inter, wo_w)
        out = jnp.zeros_like(hidden_states)
        for k in range(top_k_values.shape[0]):
            A = jnp.take(lora_As, top_k_indices[k], axis=0)
            Bm = jnp.take(lora_Bs, top_k_indices[k], axis=0)
            out = out + top_k_values[k] * _expert_ffn(hidden_states, wi_w, wo_w, A, Bm)
        return out
    x = L0_attn_x
    mod = (_silu(L0_c) @ L0_wmod).reshape(L0_c.shape[0], 6, 1, -1)
    sa, ca, ga, sb, cb, gb = (mod[:, 0], mod[:, 1], mod[:, 2], mod[:, 3], mod[:, 4], mod[:, 5])
    ga = (2 * (ga >= 0) - 1) * jnp.maximum(jnp.abs(ga), 0.25)
    gb = (2 * (gb >= 0) - 1) * jnp.maximum(jnp.abs(gb), 0.25)
    h = _layernorm(x, axis=-1) * (1 + ca) + sa
    x = x + ga * _L0_attn_ref(h, L0_attn_Wq, L0_attn_Wk, L0_attn_Wv, L0_attn_Wo, L0_attn_bo, L0_attn_P)
    h = _layernorm(x, axis=-1) * (1 + cb) + sb
    x = x + gb * _L0_ffn_ref(h, L0_ffn_wi_w, L0_ffn_wo_w, L0_ffn_lora_As, L0_ffn_lora_Bs, L0_ffn_top_k_indices, L0_ffn_top_k_values)
    return x

_drawn_inputs = setup_inputs


def setup_inputs(seed=0):
    import zlib

    import numpy as np

    out = dict(_drawn_inputs(seed))
    spreads = {'L0_attn_bo': (0.0, 0.33)}
    factors = {'L0_attn_Wq': 8.0,
     'L0_attn_Wk': 8.0,
     'L0_attn_P': 8.0,
     'L0_ffn_lora_As': 7.458,
     'L0_ffn_lora_Bs': 7.471,
     'L0_ffn_top_k_values': 8.0,
     'L0_attn_Wv': 2.793,
     'L0_attn_Wo': 2.868}
    for name, (base, spread) in spreads.items():
        noise = np.random.default_rng([zlib.crc32(name.encode()), seed]).standard_normal(out[name].shape)
        drawn = base * np.exp(spread * noise) if base else spread * noise
        out[name] = jnp.asarray(drawn.astype(out[name].dtype))
    for name, factor in factors.items():
        out[name] = (out[name] * factor).astype(out[name].dtype)
    return out
```

```python
import math
from contextlib import ExitStack

import concourse.bass as bass
from concourse import mybir

F32 = mybir.dt.float32
F16 = mybir.dt.float16
I32 = mybir.dt.int32
ALU = mybir.AluOpType
ACT = mybir.ActivationFunctionType
AX = mybir.AxisListType
RMAX = bass.bass_isa.ReduceOp.max

B, T, D = 8, 512, 256
H, DH, M = 16, 64, 64
F, R, EXP, TOPK = 1024, 16, 8, 2
P = 128
DC = D // P
TC = T // P
PR = H * DH // P
FC = F // P
EPS = 1e-4
LN_EPS = 1e-5
DN = float(DH) ** -0.25
LAST = B - 1
W_UP = 256.0
SQ_UP = 1.0 / 256
KEY_UP = 14
KEY_SHIFT = KEY_UP * math.log(2.0)
ATT_UP = 1024.0
HI, LO = 0, 1
PARTS = ((HI, HI), (HI, LO), (LO, HI))
ZR = 3 * TOPK * R
KEY_BANKS = ((0, 1), (2, 3), 4)
QUERY_BANKS = ((0, 0), (1, 1), 2)


def build(nc, x, wq, wk, wv, wo, bo, pT, wiT, woT, laT, lbT, idx, val, cT, wmod, out):
    with ExitStack() as ctx:
        def sb(name, shape, dt=F32):
            return ctx.enter_context(nc.sbuf_tensor(name, shape, dt))

        def sem(name):
            return ctx.enter_context(nc.semaphore(name))

        wq_s = sb("wq_s", [P, 2, DC, H * DH], F16)
        wk_s = sb("wk_s", [P, 2, DC, H * DH], F16)
        wi_s = sb("wi_s", [P, 2, DC, F], F16)
        wo2_s = sb("wo2_s", [P, 2, FC, D], F16)
        wv_s = sb("wv_s", [P, DC, H * DH])
        wo_s = sb("wo_s", [P, PR, D])
        lora_a_f = sb("lora_a_f", [P, DC, TOPK * R])
        lora_a = sb("lora_a", [P, 2, DC, 3, TOPK * R], F16)
        lora_first = sb("lora_first", [ZR, F], F16)
        lora_delta = sb("lora_delta", [ZR, F], F16)
        lora_sign = sb("lora_sign", [ZR, 1])
        pfeat_f = sb("pfeat_f", [P, P])
        pfeat = sb("pfeat", [P, 2, P], F16)
        ident = sb("ident", [P, P])
        ones = sb("ones", [P, 1], F16)
        head_sel = sb("head_sel", [P, 4, 8])
        head_back = sb("head_back", [8, 4, P])
        head_half = sb("head_half", [P, 2], F16)
        neg_half = sb("neg_half", [P, TC])
        idx_s = sb("idx_s", [1, TOPK], I32)
        val_s = sb("val_s", [P, TOPK])
        val_down = sb("val_down", [P, TOPK])
        c_s = sb("c_s", [P, DC, B])
        silu_a = sb("silu_a", [P, DC, B])
        silu_b = sb("silu_b", [P, DC, B])
        silu_c = sb("silu_c", [P, DC, B])
        modT = sb("modT", [P, B, 12])
        sa_v = sb("sa_v", [P, PR, B])

        hT = sb("hT", [P, B, 2, DC, T], F16)
        ctx_raw = sb("ctx_raw", [P, B, PR, M])
        k_raw = sb("k_raw", [P, B, PR])
        v_in = sb("v_in", [P, DC, 2, B])
        v_raw = sb("v_raw", [P, B, PR])
        mref = sb("mref", [P, B])
        scale_all = sb("scale_all", [P, B])
        gmax = sb("gmax", [P, 1])

        x_in = sb("x_in", [P, TC, D])
        xhat = sb("xhat", [P, TC, D])
        xhat2 = [sb(f"xhat2{i}", [P, 2, TC, D], F16) for i in range(2)]
        stats = sb("stats", [P, TC, 6])
        meanvar = sb("meanvar", [P, TC, 2])
        var_eps = sb("var_eps", [P, TC])
        rstd = sb("rstd", [P, TC])
        mod_cur = sb("mod_cur", [P, 4])
        ca_cur = sb("ca_cur", [P, DC])
        h_f = sb("h_f", [P, DC, T])
        proj = [sb(f"proj{i}", [P, 2, T], F16) for i in range(2)]
        sq_f = [sb(f"sq_f{i}", [P, T]) for i in range(2)]
        sq = [sb(f"sq{i}", [P, 2, T], F16) for i in range(2)]
        mx = sb("mx", [P, PR, 2 * TC])
        shift = [sb(f"shift{i}", [P, 2 * TC]) for i in range(2)]
        bmax = sb("bmax", [P, 1])
        bmax_all = sb("bmax_all", [P, 1])
        pool_pad = sb("pool_pad", [P, 1])
        neg_ref = sb("neg_ref", [P, 1])
        scores = sb("scores", [P, PR, TC, P])
        kexp = sb("kexp", [P, 2, PR, TC, P], F16)
        featT = sb("featT", [P, DC, H * M])
        attw = scores[:, :, :, :].rearrange("p a b c -> p (a b c)").bitcast(F16).rearrange("p (s a t) -> p s a t", s=2, a=PR)
        relu_sum = kexp[:, :, :, :, :].rearrange("p s a b c -> p s a (b c)")
        g_s = featT[:, :, :].rearrange("p a b -> p (a b)").bitcast(F16).rearrange("p (s a d) -> p s a d", s=2, d=D)
        scale_cur = sb("scale_cur", [P, 1])
        v_cur = sb("v_cur", [P, PR])
        k_cur = sb("k_cur", [P, PR])
        k_rec = sb("k_rec", [P, PR])
        k_eps = sb("k_eps", [P, PR])
        ctx_bd = sb("ctx_bd", [P, PR, P])
        wv_flat = wv_s[:, :, :].rearrange("p c n -> p (c n)")
        qexp = [wv_flat[:, T * i:T * (i + 1)].rearrange("p (a b) -> p a b", b=P) for i in range(2)]
        qk = sb("qk", [P, PR, T])
        den_rec = sb("den_rec", [8, 2, T])
        w_f = sq_f
        wk_flat = wk_s[:, :, :, :].rearrange("p s c n -> p (s c n)").bitcast(F32)
        relu0 = [wk_flat[:, T * i:T * (i + 1)] for i in range(2)]
        sum_f = [wk_flat[:, T * (2 + i):T * (3 + i)] for i in range(2)]
        h2T = xhat2[0][:, :, :, :].rearrange("p s a b -> p s (a b)").rearrange("p s (c t) -> p s c t", c=DC)
        z_s = sb("z_s", [ZR, T], F16)
        x_rest = x_in
        x1 = wv_flat[:, 2 * T:4 * T].rearrange("p (a b) -> p a b", b=D)
        row_a = sb("row_a", [P, 2, D])
        row_g = sb("row_g", [P, D])
        o_s = xhat2[1][:, :, :, :].rearrange("p s a b -> p (s a b)").bitcast(F32).rearrange("p (a b) -> p a b", b=D)
        wmod_s = scores[:, :, :, :].rearrange("p a b c -> p (a b c)")[:, 0:DC * 6 * D].rearrange("p (a b) -> p a b", a=DC)
        wk_f = featT
        e_flat = kexp[:, :, :, :, :].rearrange("p s a b c -> p (s a b c)").bitcast(F32)
        wq_f = e_flat[:, 0:DC * H * DH].rearrange("p (c n) -> p c n", c=DC)
        wi_f = e_flat[:, DC * H * DH:2 * DC * H * DH].rearrange("p (c n) -> p c n", c=DC)
        wo2_f = qk[:, 0:4, :].rearrange("p a t -> p (a t)").rearrange("p (c n) -> p c n", c=FC)
        lora_b_f = qk[0:ZR, 4:8, :].rearrange("p a t -> p (a t)").rearrange("p (k f) -> p k f", k=2)
        gates_raw = row_a[0:B, :, :]
        bo_s = row_g[0:B, :]
        gate_row = qk[0:B, 6:8, :].rearrange("p a t -> p (a t)").rearrange("p (a d) -> p a d", d=D)[:, 0:3, :]
        gates = qk[0:B, 4, :].rearrange("p (a d) -> p a d", d=D)
        gate_abs = qk[0:B, 5, :].rearrange("p (a d) -> p a d", d=D)
        rows_dram = nc.dram_tensor("rows_scratch", (B, 3, D), F32, kind="Internal").ap()

        bank = [ctx.enter_context(nc.psum_tensor(f"bank{i}", [P, 512], F32)) for i in range(8)]

        s_small = sem("small_loaded")
        s_wk = sem("wk_loaded")
        s_wv = sem("wv_loaded")
        s_rest = [sem(f"{k}_loaded") for k in ("wq", "wi", "wo2", "lora")]
        s_pre = sem("features_loaded")
        s_idx = sem("index_loaded")
        s_x = sem("x_loaded")
        s_rowa = sem("row_a_loaded")
        s_rowg = sem("row_g_loaded")
        s_out = sem("out_stored")
        c_pool = sem("pool_constants_ready")
        c_dve = sem("dve_constants_ready")
        c_id0 = sem("ident_zeroed")
        p_exp = sem("silu_exp")
        p_dve = sem("silu_steps")
        p_mod = sem("mod_mm")
        p_modT = sem("modT_ready")
        p_sav = sem("sa_v_mm")
        p_savs = sem("sa_v_ready")
        p_r = sem("row_mm")
        p_gate = sem("gate_steps")
        p_rows = sem("rows_ready")
        p_pf = sem("pfeat_steps")
        p_lora = sem("lora_steps")
        w_hi = sem("weight_hi")
        w_lo = sem("weight_lo")
        s_stat = sem("stats_done")
        s_agg = sem("aggregated")
        s_var = sem("variance_ready")
        s_rstd = sem("rstd_ready")
        s_xhat = sem("xhat_ready")
        s_xh = sem("xhat_hi")
        s_xl = sem("xhat_lo")
        s_modc = sem("mod_current")
        s_tr = sem("hT_mm")
        s_hh = sem("hT_hi")
        s_hT = sem("hT_ready")
        s_pm = sem("proj_mm")
        s_pe = sem("proj_read_by_act")
        s_pl = sem("proj_lo")
        s_sl = sem("square_lo")
        s_dd = sem("scores_mm")
        s_dg = sem("diag_mm")
        s_mx = sem("max_ready")
        s_sh = sem("shift_ready")
        s_ss = sem("scores_shifted")
        s_bm = sem("batch_max")
        s_bma = sem("batch_max_all")
        s_nr = sem("neg_ref_ready")
        s_ke = sem("key_exp")
        s_kh = sem("key_exp_hi")
        s_kl = sem("key_exp_lo")
        s_sum = sem("sums_mm")
        s_sume = sem("sums_ready")
        s_ft = sem("feat_mm")
        s_fte = sem("feat_ready")
        s_cx = sem("ctx_mm")
        s_cxe = sem("ctx_ready")
        s_sv = sem("v_raw_mm")
        s_sve = sem("v_raw_ready")
        s_gm = sem("gmax_ready")
        s_sc = sem("scale_ready")
        s_cur = sem("current_ready")
        s_cur_a = sem("current_steps")
        s_bd = sem("ctx_bd_ready")
        s_g = sem("g_mm")
        s_gh = sem("g_hi")
        s_ge = sem("g_ready")
        s_qe = sem("query_exp")
        s_qt = sem("query_tr")
        s_qk = sem("qk_ready")
        s_dn = sem("den_mm")
        s_dr = sem("den_rec_ready")
        s_db = sem("den_rec_spread")
        s_wf = sem("attw_float")
        s_wh = sem("attw_hi")
        s_w = sem("attw_ready")
        s_xr = sem("x_rest_ready")
        s_y = sem("y_mm")
        s_yg = sem("y_gated")
        s_yr = sem("y_read")
        s_x1 = sem("x1_ready")
        s_z = sem("z_mm")
        s_vin = sem("v_in_ready")
        s_zh = sem("z_hi")
        s_ze = sem("z_ready")
        s_f0 = sem("ffn_first_mm")
        s_r0 = sem("relu0_ready")
        s_f1 = sem("ffn_second_mm")
        s_r1 = sem("relu1_ready")
        s_rf = sem("relu_sum_float")
        s_rh = sem("relu_sum_hi")
        s_rs = sem("relu_sum_ready")
        s_o = sem("out_mm")
        s_og = sem("out_gated")
        s_of = sem("out_ready")

        block = ctx.enter_context(nc.Block())
        xv = x.rearrange("b (p t) d -> b p t d", t=TC)
        ov = out.rearrange("b (p t) d -> b p t d", t=TC)

        @block.sync
        def _(sp):
            sp.dma_start(x_in[:, :, :], xv[0]).then_inc(s_x, 16)
            sp.dma_start(idx_s[:, :], idx.rearrange("(a n) -> a n", a=1)).then_inc(s_idx, 16)
            sp.dma_start(c_s[:, :, :], cT.rearrange("(c p) b -> p c b", p=P)).then_inc(s_small, 16)
            sp.dma_start(wmod_s, wmod.rearrange("(c p) n -> p c n", p=P)).then_inc(s_small, 16)
            sp.dma_start(wk_f[:, :, :], wk.rearrange("(c p) n -> p c n", p=P)).then_inc(s_wk, 16)
            sp.wait_ge(c_pool, 1)
            sp.dma_start(pfeat_f[0:DH, 0:M], pT).then_inc(s_pre, 16)
            sp.dma_start(pfeat_f[DH:P, M:P], pT).then_inc(s_pre, 16)
            sp.dma_start(wq_f, wq.rearrange("(c p) n -> p c n", p=P)).then_inc(s_rest[0], 16)
            sp.dma_start(wi_f, wiT.rearrange("(c p) n -> p c n", p=P)).then_inc(s_rest[1], 16)
            sp.dma_start(wo2_f, woT.rearrange("(c p) n -> p c n", p=P)).then_inc(s_rest[2], 16)
            sp.wait_ge(s_idx, 16)
            expert = [sp.value_load(idx_s[0:1, k:k + 1], min_val=0, max_val=EXP - 1) for k in range(TOPK)]
            lb = [lbT[bass.ds(e, 1)].rearrange("o r f -> (o r) f") for e in expert]
            for g in range(3):
                r = g * TOPK * R
                sp.dma_start(lora_b_f[r:r + R, 0, :], lb[0]).then_inc(s_rest[3], 16)
                for k in range(TOPK):
                    sp.dma_start(lora_b_f[r + k * R:r + (k + 1) * R, 1, :], lb[k]).then_inc(s_rest[3], 16)
            for k in range(TOPK):
                sp.dma_start(lora_a_f[:, :, k * R:(k + 1) * R],
                             laT[bass.ds(expert[k], 1)].rearrange("o (c p) r -> p (o c) r", p=P)).then_inc(s_rest[3], 16)
            sp.dma_start(val_s[:, :], val.rearrange("(a n) -> a n", a=1).to_broadcast([P, TOPK])).then_inc(s_rest[3], 16)
            sp.dma_start(wv_s[:, :, :], wv.rearrange("(c p) n -> p c n", p=P)).then_inc(s_wv, 16)
            sp.dma_start(wo_s[:, :, :], wo.rearrange("(c p) n -> p c n", p=P)).then_inc(s_wv, 16)
            sp.dma_start(bo_s[:, :], bo.rearrange("(a n) -> a n", a=1).to_broadcast([B, D])).then_inc(s_wv, 16)
            with sp.Fori(1, B) as b:
                sp.wait_ge(s_xhat, b)
                sp.dma_start(x_in[:, :, :], xv[b]).then_inc(s_x, 16)
            sp.wait_ge(p_rows, 1)
            sp.dma_start(rows_dram, gate_row).then_inc(s_out, 16)
            sp.wait_ge(s_out, 16)

            def load_att(i, first):
                sp.wait_ge(s_xhat, B) if first else sp.wait_ge(s_yr, 2 * i)
                sp.dma_start(x_in[:, :, :], xv[i]).then_inc(s_x, 16)
                sp.dma_start(row_a[:, :, :].rearrange("p a d -> p (a d)"),
                             rows_dram[bass.ds(i, 1), 0:2, :].rearrange("o a d -> o (a d)").to_broadcast([P, 2 * D])).then_inc(s_rowa, 16)

            def load_gate(i, first=False):
                if not first:
                    sp.wait_ge(s_of, 2 * (i - 1))
                sp.dma_start(row_g[:, :], rows_dram[bass.ds(i - 1, 1), 2, :].to_broadcast([P, D])).then_inc(s_rowg, 16)

            def store(i):
                sp.wait_ge(s_of, 2 * i)
                sp.dma_start(ov[i - 1], o_s).then_inc(s_out, 16)

            load_att(0, True)
            load_att(1, False)
            load_gate(1, first=True)
            store(1)
            with sp.Fori(2, B) as i:
                load_att(i, False)
                load_gate(i)
                store(i)
            load_gate(B)
            store(B)
            sp.wait_ge(s_out, 16 * (B + 1))

        @block.gpsimd
        def _(pool):
            pool.memset(pfeat_f[:, :], 0.0)
            pool.memset(lora_b_f, 0.0).then_inc(c_pool, 1)
            pool.memset(head_back[:, :, :], 0.0)
            pool.memset(neg_half[:, :], -0.5)
            pool.memset(ctx_bd[:, :, :], 0.0)
            pool.memset(ident[:, :], 0.0).then_inc(c_id0, 1)
            pool.wait_ge(c_id0, 1)
            pool.affine_select(out=ident[:, :], in_=ident[:, :], compare_op=ALU.not_equal, fill=1.0,
                               base=0, pattern=[[-1, P]], channel_multiplier=1).then_inc(c_pool, 1)
            pool.affine_select(out=head_back[:, :, :], in_=head_back[:, :, :], compare_op=ALU.not_equal, fill=ATT_UP,
                               base=0, pattern=[[-2, 4], [-1, 2], [0, DH]], channel_multiplier=1).then_inc(c_pool, 1)
            pool.wait_ge(c_pool, 3)

            def lower(out, value, hi):
                return pool.tensor_tensor(out, value, hi, ALU.subtract)

            def ln_power(n):
                pool.wait_ge(s_var, n + 1)
                pool.tensor_tensor(rstd[:, :], var_eps[:, :], neg_half[:, :], ALU.pow).then_inc(s_rstd, 1)

            def h_lower(n, c, dst, first=False):
                if c == 0 and not first:
                    pool.wait_ge(s_pm, 1)
                pool.wait_ge(s_hh, 4 * n + 2 * c + 2)
                lower(dst[LO][c], h_f[:, c, :], dst[HI][c]).then_inc(s_hT, 1)

            def x_lower(n, par):
                pool.wait_ge(s_xh, n + 1)
                lower(xhat2[par][:, LO, :, :], xhat[:, :, :], xhat2[par][:, HI, :, :]).then_inc(s_xl, 1)

            def square_lower(n, p, early):
                pool.wait_ge(s_pe, 3 * n + 3)
                if not early:
                    pool.wait_ge(s_dg, n - 1)
                lower(sq[p % 2][:, LO, :], sq_f[p % 2][:, :], sq[p % 2][:, HI, :]).then_inc(s_sl, 1)

            def key_lower(u, q):
                pool.wait_ge(s_kh, 4 * u + q + 1)
                lower(kexp[:, LO, 2 * q:2 * q + 2, :, :], scores[:, 2 * q:2 * q + 2, :, :], kexp[:, HI, 2 * q:2 * q + 2, :, :]).then_inc(s_kl, 1)

            def batch_max(b):
                pool.wait_ge(s_bm, b + 1)
                pool.tensor_tensor(pool_pad[:, :], neg_half[:, 0:1], neg_half[:, 0:1], ALU.mult)
                pool.partition_all_reduce(bmax_all[:, :], bmax[:, :], P, RMAX).then_inc(s_bma, 1)

            def hT_of(b):
                return [[hT[:, b, s, c, :] for c in range(DC)] for s in range(2)]

            def keys(b, par, has_u, has_next):
                for s in range(PR + 1):
                    if s < PR:
                        square_lower(8 * b + s, s, early=not has_u and s < 2)
                    if has_u and s < 4:
                        key_lower(b - 1, s)
                    if has_next and s == 3:
                        ln_power(b + 1)
                    if has_next and s == 7:
                        h_lower(b + 1, 0, hT_of(b + 1))
                batch_max(b)
                if has_next:
                    h_lower(b + 1, 1, hT_of(b + 1))
                    x_lower(b + 1, 1 - par)

            ln_power(0)
            h_lower(0, 0, hT_of(0), first=True)
            h_lower(0, 1, hT_of(0))
            x_lower(0, 0)
            keys(0, 0, False, True)
            with pool.Fori(0, B // 2 - 1) as h:
                keys(2 * h + 1, 1, True, True)
                keys(2 * h + 2, 0, True, True)
            keys(LAST, 1, True, False)
            for q in range(4):
                key_lower(LAST, q)

            h2 = [[h2T[:, s, c, :] for c in range(DC)] for s in range(2)]

            def weight_lower(i, p):
                pool.wait_ge(s_wh, 8 * i + p + 1)
                lower(attw[:, LO, p, :], w_f[p % 2][:, :], attw[:, HI, p, :]).then_inc(s_w, 1)

            def batch(i, att, ffn):
                n0 = 8 * B + 8 * i
                for s in range(PR + 4):
                    if att and s < PR:
                        square_lower(n0 + s, s, early=False)
                    if ffn and s == 1:
                        for c in range(DC):
                            h_lower(B + i - 1, c, h2)
                    if att and s == 2:
                        pool.wait_ge(s_x, 16 * (B + i + 1))
                        pool.wait_ge(s_rowa, 16 * (i + 1))
                        for j in range(TC):
                            op = pool.tensor_tensor(x_rest[:, j, :], x_in[:, j, :], row_a[:, 1, :], ALU.add)
                        op.then_inc(s_xr, 1)
                    if ffn and 4 <= s < 12:
                        f = s - 4
                        pool.wait_ge(s_rh, 8 * (i - 1) + f + 1)
                        lower(relu_sum[:, LO, f, :], sum_f[f % 2], relu_sum[:, HI, f, :]).then_inc(s_rs, 1)
                    if att and s >= PR:
                        weight_lower(i, s - PR)
                if att:
                    for p in range(4, PR):
                        weight_lower(i, p)
                    ln_power(B + i)

            batch(0, True, False)
            with pool.Fori(1, B) as i:
                batch(i, True, True)
            batch(B, False, True)

        @block.tensor
        def _(pe):
            def transpose_x(c, dst):
                for j in range(TC):
                    op = pe.transpose(dst[:, j * P:(j + 1) * P], xhat[:, j, c * P:(c + 1) * P], ident[:, :])
                op.then_inc(s_tr, 1)

            def project(n, p, b, w, banks):
                for a in range(3):
                    st, mv = PARTS[a]
                    for c in range(DC):
                        op = pe.matmul(bank[banks[0][p % 2]][:, :], w[:, st, c, p * P:(p + 1) * P], hT[:, b, mv, c, :],
                                       start=(a == 0 and c == 0), stop=(a == 2 and c == DC - 1))
                op.then_inc(s_pm, 1)

            def score(n, p, banks):
                pe.wait_ge(s_pl, n + 1)
                for j in range(TC):
                    for a in range(3):
                        st, mv = PARTS[a]
                        op = pe.matmul(bank[banks[1][p % 2]][:, j * P:(j + 1) * P], proj[p % 2][:, st, j * P:(j + 1) * P], pfeat[:, mv, :],
                                       start=(a == 0), stop=(a == 2))
                op.then_inc(s_dd, 1)

            def diag(n, p, banks, first):
                pe.wait_ge(s_sl, n + 1)
                if not first:
                    pe.wait_ge(s_sh, n)
                for j in range(TC):
                    for a in (HI, LO):
                        op = pe.matmul(bank[banks[2]][:, 2 * j:2 * j + 2], sq[p % 2][:, a, j * P:(j + 1) * P], head_half[:, :], start=(a == HI), stop=(a == LO))
                op.then_inc(s_dg, 1)

            def features(u, par, k):
                half, c = k // 2, k % 2
                if c == 0:
                    pe.wait_ge(s_kl, 4 * u + 2 * (half + 1))
                if k == 0:
                    pe.wait_ge(s_xl, u + 1)
                if k > 0:
                    pe.wait_ge(s_fte, 4 * u + k)
                for a in range(3):
                    st, mv = PARTS[a]
                    for j in range(TC):
                        op = pe.matmul(bank[7][:, :], xhat2[par][:, st, j, c * P:(c + 1) * P], kexp[:, mv, 4 * half:4 * half + 4, j, :],
                                       start=(a == 0 and j == 0), stop=(a == 2 and j == TC - 1))
                op.then_inc(s_ft, 1)

            def sums(u, par):
                pe.wait_ge(s_kl, 4 * u + 4)
                for p in range(PR):
                    for a in (HI, LO):
                        for j in range(TC):
                            pe.matmul(bank[5][:, p:p + 1], kexp[:, a, p, j, :], ones[:, :], start=(a == HI and j == 0), stop=(a == LO and j == TC - 1))
                for c in range(DC):
                    for a in (HI, LO):
                        for j in range(TC):
                            op = pe.matmul(bank[5][:, PR + c:PR + c + 1], xhat2[par][:, a, j, c * P:(c + 1) * P], ones[:, :],
                                           start=(a == HI and j == 0), stop=(a == LO and j == TC - 1))
                op.then_inc(s_sum, 1)

            def contexts(u):
                pe.wait_ge(s_fte, 4 * u + 4)
                pe.wait_ge(s_sume, u + 1)
                for p in range(PR):
                    for c in range(DC):
                        op = pe.matmul(bank[(7, 5)[p // 4]][:, p % 4 * P:(p % 4 + 1) * P], wv_s[:, c, p * P:(p + 1) * P],
                                       featT[:, c, p * P:(p + 1) * P], start=(c == 0), stop=(c == DC - 1))
                op.then_inc(s_cx, 1)

            pe.wait_ge(p_dve, 3)
            pe.wait_ge(s_small, 32)
            for ch in (0, 1, 2, 3, 6, 7, 8, 9):
                for c in range(DC):
                    op = pe.matmul(bank[6][:, ch * B:(ch + 1) * B], wmod_s[:, c, ch * P:(ch + 1) * P], silu_c[:, c, :], start=(c == 0), stop=(c == DC - 1))
            op.then_inc(p_mod, 1)
            for g, col in enumerate((2 * D, 5 * D)):
                for c in range(DC):
                    op = pe.matmul(bank[7][0:B, g * D:(g + 1) * D], silu_c[:, c, :], wmod_s[:, c, col:col + D], start=(c == 0), stop=(c == DC - 1))
            op.then_inc(p_mod, 1)
            pe.wait_ge(c_pool, 2)
            pe.wait_ge(s_xhat, 1)
            pe.wait_ge(p_modT, 1)
            transpose_x(0, bank[6])
            pe.wait_ge(s_hh, 2)
            transpose_x(1, bank[6])
            pe.wait_ge(w_lo, 1)
            pe.wait_ge(p_pf, 3)
            pe.wait_ge(c_dve, 2)

            def keys(b, par, has_u, has_next):
                pe.wait_ge(s_hT, 2 * (b + 1))
                for s in range(PR + 1):
                    n = 8 * b + s
                    if s < PR:
                        if has_u or s >= 2:
                            pe.wait_ge(s_pl, n - 1)
                        project(n, s, b, wk_s, KEY_BANKS)
                    if s >= 1:
                        if has_u or s >= 3:
                            pe.wait_ge(s_ss, n - 2)
                        score(n - 1, s - 1, KEY_BANKS)
                        diag(n - 1, s - 1, KEY_BANKS, first=not has_u and s == 1)
                    if has_u:
                        u = b - 1
                        if 3 <= s < 7:
                            features(u, 1 - par, s - 3)
                        if s == 4:
                            sums(u, 1 - par)
                        if s == 7:
                            contexts(u)
                    if has_next and s == 6:
                        pe.wait_ge(s_xhat, b + 2)
                        transpose_x(0, bank[6])
                    if has_next and s == 7:
                        pe.wait_ge(s_hh, 4 * (b + 1) + 2)
                        transpose_x(1, bank[6])
                if has_u:
                    pe.wait_ge(s_cxe, b)

            keys(0, 0, False, True)
            pe.wait_ge(s_wv, 48)
            with pe.Fori(0, B // 2 - 1) as h:
                keys(2 * h + 1, 1, True, True)
                keys(2 * h + 2, 0, True, True)
            keys(LAST, 1, True, False)
            for k in range(4):
                features(LAST, 1, k)
            sums(LAST, 1)
            contexts(LAST)
            pe.wait_ge(s_vin, 1)
            for p in range(PR):
                for c in range(DC):
                    op = pe.matmul(bank[6][:, p * 2 * B:(p + 1) * 2 * B], wv_s[:, c, p * P:(p + 1) * P], v_in[:, c, :, :], start=(c == 0), stop=(c == DC - 1))
            op.then_inc(s_sv, 1)
            pe.wait_ge(s_sve, 1)
            for p in range(PR):
                op = pe.matmul(bank[6][0:B, 0:D], sa_v[:, p, :], wo_s[:, p, :], start=(p == 0), stop=(p == PR - 1))
            op.then_inc(p_r, 1)

            def g_mm(i, k):
                if k >= 2:
                    pe.wait_ge(s_ge, 8 * i + 2 * (k - 1))
                for q in range(2):
                    p = 2 * k + q
                    op = pe.matmul(bank[(7, 3)[k % 2]][:, q * D:(q + 1) * D], ctx_bd[:, p, :], wo_s[:, p, :], start=True, stop=True)
                op.then_inc(s_g, 1)

            def query_transposes(i, p):
                pe.wait_ge(s_qe, 8 * i + p + 1)
                pe.wait_ge(s_ge, 8 * i + 8) if p == 0 else pe.wait_ge(s_qk, 8 * i + p)
                for j in range(TC):
                    op = pe.transpose(bank[3][:, j * P:(j + 1) * P], qexp[p % 2][:, j, :], ident[:, :])
                op.then_inc(s_qt, 1)

            def denominator(i, p, first):
                q, half = p % 4, p // 4
                pe.wait_ge(s_qk, 8 * i + p + 1)
                if q == 0 and not (first and half == 0):
                    pe.wait_ge(s_dr, 2 * i + half)
                op = pe.matmul(bank[4][0:8, :], head_sel[:, q, :], qk[:, p, :], start=(q == 0), stop=(q == 3))
                if q == 3:
                    op.then_inc(s_dn, 1)

            def spread(i, p):
                q, half = p % 4, p // 4
                pe.wait_ge(s_dr, 2 * i + half + 1)
                n_end = 8 * B + 8 * i + 8
                if p == 0:
                    pe.wait_ge(s_pl, n_end)
                elif p == 1:
                    pe.wait_ge(s_ss, n_end)
                else:
                    pe.wait_ge(s_wf, 8 * i + p - 1)
                pe.matmul(bank[p % 2][:, :], head_back[:, q, :], den_rec[:, half, :], start=True, stop=True).then_inc(s_db, 1)

            def lora_in(i):
                pe.wait_ge(s_hT, 2 * (B + i))
                for a in range(3):
                    st, mv = PARTS[a]
                    for c in range(DC):
                        op = pe.matmul(bank[7][0:ZR, :], lora_a[:, st, c, :, :].rearrange("p g r -> p (g r)"), h2T[:, mv, c, :],
                                       start=(a == 0 and c == 0), stop=(a == 2 and c == DC - 1))
                op.then_inc(s_z, 1)

            def ffn_first(i, f):
                if f == 0:
                    pe.wait_ge(s_ze, i)
                if f >= 2:
                    pe.wait_ge(s_rf, 8 * (i - 1) + f - 1)
                dst = bank[5 + f % 2]
                for a in range(3):
                    st, mv = PARTS[a]
                    for c in range(DC):
                        pe.matmul(dst[:, :], wi_s[:, st, c, f * P:(f + 1) * P], h2T[:, mv, c, :], start=(a == 0 and c == 0), stop=False)
                pe.matmul(dst[:, :], lora_first[:, f * P:(f + 1) * P], z_s[:, :], start=False, stop=True).then_inc(s_f0, 1)

            def ffn_second(i, f):
                pe.wait_ge(s_r0, 8 * (i - 1) + f + 1)
                pe.matmul(bank[5 + f % 2][:, :], lora_delta[:, f * P:(f + 1) * P], z_s[:, :], start=False, stop=True, skip_group_check=True).then_inc(s_f1, 1)

            def ffn_out(i, k):
                if k == 0:
                    pe.wait_ge(s_rs, 8 * i)
                for j in (2 * k, 2 * k + 1):
                    for f in range(FC):
                        for a in range(3):
                            st, mv = PARTS[a]
                            op = pe.matmul(bank[(7, 5)[k]][:, (j % 2) * D:(j % 2 + 1) * D], relu_sum[:, st, f, j * P:(j + 1) * P], wo2_s[:, mv, f, :],
                                           start=(f == 0 and a == 0), stop=(f == FC - 1 and a == 2))
                op.then_inc(s_o, 1)

            def attention_out(i):
                for k in range(2):
                    for j in (2 * k, 2 * k + 1):
                        for p in range(PR):
                            if j == 0:
                                pe.wait_ge(s_w, 8 * i + p + 1)
                            for a in range(3):
                                st, mv = PARTS[a]
                                op = pe.matmul(bank[(3, 2)[k]][:, (j % 2) * D:(j % 2 + 1) * D], attw[:, st, p, j * P:(j + 1) * P], g_s[:, mv, p, :],
                                               start=(p == 0 and a == 0), stop=(p == PR - 1 and a == 2))
                    op.then_inc(s_y, 1)

            def batch(i, att, ffn, first=False):
                n0 = 8 * B + 8 * i
                for s in range(PR + 4):
                    n = n0 + s
                    if ffn and 4 <= s < 12:
                        ffn_second(i, s - 4)
                    if att and s < PR:
                        pe.wait_ge(s_pl, n)
                        if s == 0 and not first:
                            pe.wait_ge(s_yr, 2 * i)
                        project(n, s, i, wq_s, QUERY_BANKS)
                    if att and s == 0:
                        pe.wait_ge(s_bd, i + 1)
                        for k in range(4):
                            g_mm(i, k)
                    if ffn and s == 1:
                        pe.wait_ge(s_ge, 8 * i + 6) if att else pe.wait_ge(s_yr, 2 * i)
                        pe.wait_ge(s_xhat, B + i)
                        transpose_x(0, bank[7])
                        transpose_x(1, bank[6])
                    if ffn and s == 2:
                        lora_in(i)
                    if att and 0 <= s - 1 < PR:
                        pe.wait_ge(s_ss, n - 1)
                        score(n - 1, s - 1, QUERY_BANKS)
                    if att and 0 <= s - 3 < PR:
                        query_transposes(i, s - 3)
                    if att and 0 <= s - 4 < PR:
                        denominator(i, s - 4, first)
                    if att and 0 <= s - 1 < PR:
                        diag(n - 1, s - 1, QUERY_BANKS, False)
                    if att and s >= PR:
                        spread(i, s - PR)
                    if ffn and 3 <= s < 11:
                        ffn_first(i, s - 3)
                if ffn:
                    ffn_out(i, 0)
                if att:
                    spread(i, 4)
                    spread(i, 5)
                if ffn:
                    ffn_out(i, 1)
                if att:
                    spread(i, 6)
                    spread(i, 7)
                    attention_out(i)

            pe.wait_ge(w_lo, 4)
            pe.wait_ge(p_lora, 2)
            pe.wait_ge(s_cxe, B)
            batch(0, True, False, first=True)
            with pe.Fori(1, B) as i:
                batch(i, True, True)
            batch(B, False, True)

        @block.scalar
        def _(act):
            act.wait_ge(s_small, 32)
            act.activation(silu_a[:, :, :], c_s[:, :, :], ACT.Exp, scale=-1.0).then_inc(p_exp, 1)

            def weight_hi(src, w, loaded):
                act.wait_ge(loaded, 16)
                act.activation(w, src, ACT.Copy, scale=W_UP).then_inc(w_hi, 1)

            def h_copy(n, c, dst, src, first=False):
                if c == 0:
                    act.wait_ge(s_modc, n + 1)
                    if not first:
                        act.wait_ge(s_hT, 2 * n)
                act.wait_ge(s_tr, 2 * n + c + 1)
                act.activation(dst[HI][c], src[:, :], ACT.Identity, bias=mod_cur[:, c:c + 1], scale=mod_cur[:, 2 + c:3 + c]).then_inc(s_hh, 1)
                act.activation(h_f[:, c, :], src[:, :], ACT.Identity, bias=mod_cur[:, c:c + 1], scale=mod_cur[:, 2 + c:3 + c]).then_inc(s_hh, 1)

            def hT_of(b):
                return [[hT[:, b, s, c, :] for c in range(DC)] for s in range(2)]

            def projection(n, p, banks, early):
                src = bank[banks[0][p % 2]]
                act.wait_ge(s_pm, n + 1)
                if not early:
                    act.wait_ge(s_dd, n - 1)
                act.activation(proj[p % 2][:, HI, :], src[:, :], ACT.Copy, scale=1.0 / W_UP).then_inc(s_pe, 1)
                if not early:
                    act.wait_ge(s_sl, n - 1)
                act.activation(sq_f[p % 2][:, :], src[:, :], ACT.Square, scale=math.sqrt(SQ_UP) / W_UP).then_inc(s_pe, 1)
                if not early:
                    act.wait_ge(s_dg, n - 1)
                act.activation(sq[p % 2][:, HI, :], src[:, :], ACT.Square, scale=math.sqrt(SQ_UP) / W_UP).then_inc(s_pe, 1)

            def key_exp(u, q):
                if q == 0:
                    act.wait_ge(s_nr, u + 1)
                part = scores[:, 2 * q:2 * q + 2, :, :]
                act.activation(part, part, ACT.Exp, bias=neg_ref[:, :]).then_inc(s_ke, 1)

            def feature_copy(u, k):
                half, c = k // 2, k % 2
                act.wait_ge(s_ft, 4 * u + k + 1)
                act.activation(featT[:, c, 512 * half:512 * (half + 1)], bank[7][:, :], ACT.Copy, scale=ca_cur[:, c:c + 1]).then_inc(s_fte, 1)

            def keys(b, par, has_u, has_next):
                for s in range(PR + 1):
                    if s < PR:
                        projection(8 * b + s, s, KEY_BANKS, early=not has_u and s < 2)
                    if has_u and s < 4:
                        key_exp(b - 1, s)
                    if not has_u and s in (2, 4, 6):
                        src, w, loaded = ((wq_f, wq_s, s_rest[0]), (wi_f, wi_s, s_rest[1]), (wo2_f, wo2_s, s_rest[2]))[s // 2 - 1]
                        weight_hi(src, w[:, HI, :, :], loaded)
                    if has_u and 3 <= s < 7:
                        feature_copy(b - 1, s - 3)
                    if has_next and s in (6, 7):
                        h_copy(b + 1, s - 6, hT_of(b + 1), bank[6])

            weight_hi(wk_f[:, :, :], wk_s[:, HI, :, :], s_wk)
            h_copy(0, 0, hT_of(0), bank[6], first=True)
            h_copy(0, 1, hT_of(0), bank[6], first=True)
            keys(0, 0, False, True)
            with act.Fori(0, B // 2 - 1) as h:
                keys(2 * h + 1, 1, True, True)
                keys(2 * h + 2, 0, True, True)
            keys(LAST, 1, True, False)
            for q in range(4):
                key_exp(LAST, q)
            for k in range(4):
                feature_copy(LAST, k)
            act.wait_ge(s_gm, 1)
            act.activation(scale_all[:, :], mref[:, :], ACT.Exp, bias=gmax[:, :]).then_inc(s_sc, 1)

            def attw_hi(i, p):
                act.wait_ge(s_wf, 8 * i + p + 1)
                act.activation(attw[:, HI, p, :], w_f[p % 2][:, :], ACT.Copy).then_inc(s_wh, 1)

            h2 = [[h2T[:, s, c, :] for c in range(DC)] for s in range(2)]

            def batch(i, att, ffn, first=False):
                n0 = 8 * B + 8 * i
                for s in range(PR + 4):
                    if att and s < PR:
                        projection(n0 + s, s, QUERY_BANKS, early=False)
                    if att and s == 0:
                        act.wait_ge(s_cur, i + 1)
                        if not first:
                            act.wait_ge(s_y, 2 * i)
                        for p in range(PR):
                            if p % 2 == 0:
                                act.wait_ge(s_g, 4 * i + p // 2 + 1)
                            act.activation(g_s[:, HI, p, :], bank[(7, 3)[p // 2 % 2]][:, (p % 2) * D:(p % 2 + 1) * D], ACT.Copy,
                                           scale=k_rec[:, p:p + 1]).then_inc(s_gh, 1)
                    if ffn and s == 1:
                        h_copy(B + i - 1, 0, h2, bank[7])
                        h_copy(B + i - 1, 1, h2, bank[6])
                    if ffn and s == 2:
                        act.wait_ge(s_z, i)
                        act.activation(z_s[:, :], bank[7][0:ZR, :], ACT.Copy, scale=1.0 / W_UP).then_inc(s_zh, 1)
                    if att and 0 <= s - 1 < PR:
                        p = s - 1
                        act.wait_ge(s_ss, n0 + p + 1)
                        act.activation(qexp[p % 2][:, :, :], qexp[p % 2][:, :, :], ACT.Exp).then_inc(s_qe, 1)
                    if att and 0 <= s - 3 < PR:
                        p = s - 3
                        act.wait_ge(s_qt, 8 * i + p + 1)
                        if first and p == 4:
                            act.wait_ge(s_out, 16)
                        act.activation(qk[:, p, :], bank[3][:, :], ACT.Identity, bias=k_eps[:, p:p + 1], scale=k_cur[:, p:p + 1]).then_inc(s_qk, 1)
                    if ffn and 4 <= s < 12:
                        f = s - 4
                        act.wait_ge(s_rf, 8 * (i - 1) + f + 1)
                        act.activation(relu_sum[:, HI, f, :], sum_f[f % 2], ACT.Copy).then_inc(s_rh, 1)
                    if att and s >= PR:
                        attw_hi(i, s - PR)
                    if ffn and 3 <= s < 11:
                        f = s - 3
                        act.wait_ge(s_f0, 8 * (i - 1) + f + 1)
                        if f >= 2:
                            act.wait_ge(s_rf, 8 * (i - 1) + f - 1)
                        act.activation(relu0[f % 2], bank[5 + f % 2][:, :], ACT.Relu, scale=1.0 / W_UP).then_inc(s_r0, 1)
                if att:
                    for p in range(4, PR):
                        attw_hi(i, p)

            batch(0, True, False, first=True)
            with act.Fori(1, B) as i:
                batch(i, True, True)
            batch(B, False, True)

        @block.vector
        def _(dve):
            def ln_stats(n, src, mod, first=False):
                for j in range(TC):
                    op = dve.bn_stats(stats[:, j, :], src[:, j, :])
                op.then_inc(s_stat, 1)
                if not first:
                    dve.wait_ge(s_hh, 4 * n)
                dve.wait_ge(s_stat, n + 1)
                dve.tensor_copy(mod_cur[:, :], mod).then_inc(s_modc, 1)
                for j in range(TC):
                    op = dve.bn_aggr(meanvar[:, j, :], stats[:, j, :])
                op.then_inc(s_agg, 1)
                dve.wait_ge(s_agg, n + 1)
                dve.tensor_scalar(var_eps[:, :], meanvar[:, :, 1], LN_EPS, None, ALU.add).then_inc(s_var, 1)

            def ln_apply(n, src, first=False):
                if not first:
                    dve.wait_ge(s_tr, 2 * n)
                dve.wait_ge(s_rstd, n + 1)
                for j in range(TC):
                    op = dve.tensor_scalar(xhat[:, j, :], src[:, j, :], meanvar[:, j, 0:1], rstd[:, j:j + 1], ALU.subtract, ALU.mult)
                op.then_inc(s_xhat, 1)

            def xhat_hi(n, par):
                dve.wait_ge(s_xhat, n + 1)
                dve.tensor_copy(xhat2[par][:, HI, :, :], xhat[:, :, :]).then_inc(s_xh, 1)

            def heads(ap):
                return ap.rearrange("p (a m) -> p a m", m=M)

            def weight_lo(src, w, k):
                dve.wait_ge(w_hi, k + 1)
                dve.scalar_tensor_tensor(out=w[:, LO, :, :], in0=src, scalar=W_UP, in1=w[:, HI, :, :], op0=ALU.mult, op1=ALU.subtract).then_inc(w_lo, 1)

            def projection_lo(n, p, banks):
                dve.wait_ge(s_pe, 3 * n + 3)
                dve.scalar_tensor_tensor(out=proj[p % 2][:, LO, :], in0=bank[banks[0][p % 2]][:, :], scalar=1.0 / W_UP, in1=proj[p % 2][:, HI, :],
                                         op0=ALU.mult, op1=ALU.subtract).then_inc(s_pl, 1)

            def shifted_scores(n, p, dst, banks, query):
                dd = bank[banks[1][p % 2]]
                dg = bank[banks[2]][:, 0:2 * TC]
                dve.wait_ge(s_dd, n + 1)
                dve.tensor_reduce(mx[:, p, :], heads(dd[:, :]), AX.X, ALU.max).then_inc(s_mx, 1)
                dve.wait_ge(s_dg, n + 1)
                if query:
                    dve.wait_ge(s_mx, n + 1)
                    dve.tensor_tensor(shift[p % 2][:, :], dg, mx[:, p, :], ALU.add).then_inc(s_sh, 1)
                else:
                    dve.tensor_copy(shift[p % 2][:, :], dg).then_inc(s_sh, 1)
                dve.wait_ge(s_sh, n + 1)
                dve.tensor_tensor(dst.rearrange("p t (a m) -> p (t a) m", m=M), heads(dd[:, :]),
                                  shift[p % 2][:, :].unsqueeze(2).to_broadcast([P, 2 * TC, M]), ALU.subtract).then_inc(s_ss, 1)

            def batch_max(b):
                dve.wait_ge(s_mx, 8 * b + 8)
                dve.tensor_reduce(bmax[:, :], mx[:, :, :].rearrange("p a b -> p (a b)"), AX.X, ALU.max).then_inc(s_bm, 1)

            def reference_max(u):
                dve.wait_ge(s_bma, u + 1)
                dve.tensor_copy(ca_cur[:, :], modT[:, u, 2:4])
                dve.tensor_copy(mref[:, u:u + 1] if isinstance(u, int) else mref[:, bass.ds(u, 1)], bmax_all[:, :])
                dve.tensor_scalar(neg_ref[:, :], bmax_all[:, :], -1.0, KEY_SHIFT, ALU.mult, ALU.add).then_inc(s_nr, 1)

            def key_hi(u, q):
                dve.wait_ge(s_ke, 4 * u + q + 1)
                dve.tensor_copy(kexp[:, HI, 2 * q:2 * q + 2, :, :], scores[:, 2 * q:2 * q + 2, :, :]).then_inc(s_kh, 1)

            def sums_copy(u):
                dve.wait_ge(s_sum, u + 1)
                dve.tensor_copy(k_raw[:, u, :], bank[5][:, 0:PR])
                at = v_in[:, :, 0, u:u + 1] if isinstance(u, int) else v_in[:, :, 0, bass.ds(u, 1)]
                dve.tensor_tensor(at, bank[5][:, PR:PR + DC].unsqueeze(2), ca_cur[:, :].unsqueeze(2), ALU.mult).then_inc(s_sume, 1)

            def ctx_copy(u):
                dve.wait_ge(s_cx, u + 1)
                for q in range(2):
                    for g in range(2):
                        op = dve.tensor_copy(ctx_raw[g * DH:(g + 1) * DH, u, 4 * q:4 * q + 4, :],
                                             bank[(7, 5)[q]][g * DH:(g + 1) * DH, :].rearrange("p (a m) -> p a m", m=P)[:, :, g * M:(g + 1) * M])
                op.then_inc(s_cxe, 1)

            dve.memset(ones[:, :], 1.0)
            dve.memset(head_sel[:, :, :], 0.0)
            dve.memset(head_half[:, :], 0.0)
            dve.memset(lora_sign[:, :], W_UP).then_inc(c_dve, 1)
            dve.wait_ge(c_dve, 1)
            for g in range(2):
                for q in range(4):
                    dve.memset(head_sel[g * DH:(g + 1) * DH, q, 2 * q + g:2 * q + g + 1], 1.0)
                dve.memset(head_half[g * DH:(g + 1) * DH, g:g + 1], 0.5 * DN * DN / SQ_UP)
            for g in range(3):
                op = dve.memset(lora_sign[g * TOPK * R:g * TOPK * R + R, :], -W_UP)
            op.then_inc(c_dve, 1)
            dve.wait_ge(p_exp, 1)
            dve.tensor_scalar(silu_b[:, :, :], silu_a[:, :, :], 1.0, None, ALU.add).then_inc(p_dve, 1)
            dve.wait_ge(p_dve, 1)
            dve.reciprocal(silu_a[:, :, :], silu_b[:, :, :]).then_inc(p_dve, 1)
            dve.wait_ge(p_dve, 2)
            dve.tensor_tensor(silu_c[:, :, :], c_s[:, :, :], silu_a[:, :, :], ALU.mult).then_inc(p_dve, 1)
            dve.wait_ge(p_mod, 1)
            mod_ps = bank[6][:, 0:12 * B].rearrange("p (k b) -> p b k", b=B)
            for k in (0, 3):
                dve.tensor_copy(modT[:, :, 2 * k:2 * k + 2], mod_ps[:, :, 2 * k:2 * k + 2])
                op = dve.tensor_scalar(modT[:, :, 2 * k + 2:2 * k + 4], mod_ps[:, :, 2 * k + 2:2 * k + 4], 1.0, None, ALU.add)
            op.then_inc(p_modT, 1)
            dve.wait_ge(p_modT, 1)
            dve.wait_ge(s_x, 16)
            ln_stats(0, x_in, modT[:, 0, 0:4], first=True)
            ln_apply(0, x_in, first=True)
            xhat_hi(0, 0)
            dve.tensor_copy(v_in[:, :, 1, :], modT[:, :, 0:2].rearrange("p b c -> p c b"))
            dve.wait_ge(p_mod, 2)
            dve.tensor_copy(gates_raw[:, :, :], bank[7][0:B, :].rearrange("p (a d) -> p a d", a=2)).then_inc(p_gate, 1)
            weight_lo(wk_f[:, :, :], wk_s, 0)
            dve.wait_ge(s_pre, 32)
            dve.tensor_scalar(pfeat_f[:, :], pfeat_f[:, :], DN, None, ALU.mult).then_inc(p_pf, 1)
            dve.wait_ge(p_pf, 1)
            dve.tensor_copy(pfeat[:, HI, :], pfeat_f[:, :]).then_inc(p_pf, 1)
            dve.wait_ge(p_pf, 2)
            dve.tensor_tensor(pfeat[:, LO, :], pfeat_f[:, :], pfeat[:, HI, :], ALU.subtract).then_inc(p_pf, 1)

            def lora_parts():
                dve.wait_ge(s_rest[3], 16 * 12)
                dve.wait_ge(c_dve, 2)
                dve.tensor_scalar(val_down[:, :], val_s[:, :], 1.0 / W_UP, None, ALU.mult)
                dve.tensor_scalar(lora_first[:, :], lora_b_f[:, 0, :], W_UP, None, ALU.mult)
                dve.tensor_scalar(lora_delta[:, :], lora_b_f[:, 1, :], lora_sign[:, 0:1], None, ALU.mult)
                for g in range(3):
                    op = dve.tensor_scalar(lora_a[:, HI, :, g, :], lora_a_f[:, :, :], W_UP, None, ALU.mult)
                op.then_inc(p_lora, 1)
                dve.wait_ge(p_lora, 1)
                r = 2 * TOPK * R
                dve.scalar_tensor_tensor(out=lora_first[r:ZR, :], in0=lora_b_f[r:ZR, 0, :], scalar=W_UP, in1=lora_first[r:ZR, :], op0=ALU.mult, op1=ALU.subtract)
                dve.scalar_tensor_tensor(out=lora_delta[r:ZR, :], in0=lora_b_f[r:ZR, 1, :], scalar=lora_sign[r:ZR, 0:1], in1=lora_delta[r:ZR, :], op0=ALU.mult, op1=ALU.subtract)
                for g in range(3):
                    op = dve.scalar_tensor_tensor(out=lora_a[:, LO, :, g, :], in0=lora_a_f[:, :, :], scalar=W_UP, in1=lora_a[:, HI, :, g, :], op0=ALU.mult, op1=ALU.subtract)
                op.then_inc(p_lora, 1)

            def keys(b, par, has_u, has_next):
                for s in range(PR + 1):
                    n = 8 * b + s
                    if has_u and s == 0:
                        reference_max(b - 1)
                    if s >= 1:
                        if has_u and s == 1:
                            dve.wait_ge(s_bm, b)
                        if has_u:
                            dve.wait_ge(s_kl, 4 * (b - 1) + (s - 1) // 2 + 1)
                        shifted_scores(n - 1, s - 1, scores[:, s - 1, :, :], KEY_BANKS, False)
                    if s < PR:
                        projection_lo(n, s, KEY_BANKS)
                    if has_u and s < 4:
                        key_hi(b - 1, s)
                    if not has_u and s in (2, 4, 6):
                        src, w = ((wq_f, wq_s), (wi_f, wi_s), (wo2_f, wo2_s))[s // 2 - 1]
                        weight_lo(src, w, s // 2)
                    if has_next and s == 3:
                        dve.wait_ge(s_x, 16 * (b + 2))
                        ln_stats(b + 1, x_in, modT[:, b + 1, 0:4])
                    if has_next and s == 4:
                        dve.wait_ge(s_xl, b + 1)
                        ln_apply(b + 1, x_in)
                    if has_u and s == 5:
                        sums_copy(b - 1)
                if has_u:
                    ctx_copy(b - 1)
                batch_max(b)
                if has_next:
                    xhat_hi(b + 1, 1 - par)

            keys(0, 0, False, True)
            lora_parts()
            with dve.Fori(0, B // 2 - 1) as h:
                keys(2 * h + 1, 1, True, True)
                keys(2 * h + 2, 0, True, True)
            keys(LAST, 1, True, False)
            reference_max(LAST)
            for q in range(4):
                key_hi(LAST, q)
            dve.wait_ge(s_nr, B)
            dve.tensor_reduce(gmax[:, :], mref[:, :], AX.X, ALU.max, negate=True).then_inc(s_gm, 1)
            dve.wait_ge(p_gate, 1)
            dve.tensor_scalar(gates, gates_raw[:, :, :], -1.0, None, ALU.mult).then_inc(p_gate, 1)
            dve.wait_ge(p_gate, 2)
            dve.tensor_tensor(gate_abs, gates_raw[:, :, :], gates, ALU.max).then_inc(p_gate, 1)
            dve.wait_ge(p_gate, 3)
            dve.tensor_scalar(gates, gates_raw[:, :, :], 0.0, 2.0, ALU.is_ge, ALU.mult)
            dve.tensor_scalar(gate_abs, gate_abs, 0.25, None, ALU.max).then_inc(p_gate, 1)
            dve.wait_ge(p_gate, 4)
            dve.scalar_tensor_tensor(out=gates_raw[:, :, :], in0=gates, scalar=-1.0, in1=gate_abs, op0=ALU.add, op1=ALU.mult).then_inc(p_gate, 1)
            dve.wait_ge(p_gate, 5)
            dve.wait_ge(p_lora, 2)
            dve.tensor_scalar(gate_row[:, 0, :], gates_raw[:, 0, :], 1.0 / ATT_UP, None, ALU.mult)
            dve.tensor_scalar(gate_row[:, 2, :], gates_raw[:, 1, :], 1.0 / W_UP, None, ALU.mult)
            sums_copy(LAST)
            dve.wait_ge(s_sume, B)
            dve.tensor_copy(v_in[:, :, 0, 0:1], v_in[:, :, 0, 0:1]).then_inc(s_vin, 1)
            dve.wait_ge(s_sc, 1)
            dve.tensor_scalar(scale_all[:, :], scale_all[:, :], 2.0 ** -KEY_UP, None, ALU.mult).then_inc(s_cur_a, 1)
            ctx_copy(LAST)
            dve.wait_ge(s_sv, 1)
            v_ps = bank[6][:, 0:2 * B * PR].rearrange("p (a s b) -> p s a b", s=2, b=B)
            dve.tensor_copy(v_raw[:, :, :].rearrange("p b a -> p a b"), v_ps[:, 0, :, :])
            dve.tensor_copy(sa_v[:, :, :], v_ps[:, 1, :, :]).then_inc(s_sve, 1)
            dve.wait_ge(p_r, 1)
            dve.tensor_tensor(gates[:, 0, :], bank[6][0:B, 0:D], bo_s[:, :], ALU.add).then_inc(p_gate, 1)
            dve.wait_ge(p_gate, 6)
            dve.tensor_tensor(gate_row[:, 1, :], gates[:, 0, :], gates_raw[:, 0, :], ALU.mult).then_inc(p_rows, 1)

            def current(i):
                dve.wait_ge(s_cur_a, 2 * i + 1)
                dve.tensor_copy(scale_cur[:, :], scale_all[:, i:i + 1] if isinstance(i, int) else scale_all[:, bass.ds(i, 1)])
                dve.tensor_scalar(v_cur[:, :], v_raw[:, i, :], EPS, None, ALU.mult)
                dve.tensor_copy(k_cur[:, :], k_raw[:, i, :]).then_inc(s_cur_a, 1)
                dve.wait_ge(s_cur_a, 2 * i + 2)
                dve.tensor_scalar(k_cur[:, :], k_cur[:, :], scale_cur[:, 0:1], T * EPS, ALU.mult, ALU.add).then_inc(s_cur_a, 1)
                dve.wait_ge(s_cur_a, 2 * i + 3)
                dve.tensor_scalar(k_eps[:, :], k_cur[:, :], EPS, None, ALU.mult)
                dve.reciprocal(k_rec[:, :], k_cur[:, :]).then_inc(s_cur, 1)
                for g in range(2):
                    rows = slice(g * DH, (g + 1) * DH)
                    op = dve.scalar_tensor_tensor(out=ctx_bd[rows, :, g * M:(g + 1) * M], in0=ctx_raw[rows, i, :, :], scalar=scale_cur[rows, 0:1],
                                                  in1=v_cur[rows, :].unsqueeze(2).to_broadcast([DH, PR, M]), op0=ALU.mult, op1=ALU.add)
                op.then_inc(s_bd, 1)

            def attw_float(i, p):
                dve.wait_ge(s_db, 8 * i + p + 1)
                if p >= 2:
                    dve.wait_ge(s_w, 8 * i + p - 1)
                else:
                    dve.wait_ge(s_sl, 8 * B + 8 * i + 8)
                dve.tensor_tensor(w_f[p % 2][:, :], qk[:, p, :], bank[p % 2][:, :], ALU.mult).then_inc(s_wf, 1)

            def reciprocals(i, half):
                dve.wait_ge(s_dn, 2 * i + half + 1)
                dve.reciprocal(den_rec[:, half, :], bank[4][0:8, :]).then_inc(s_dr, 1)

            def out_rows(i, k):
                rows = bank[(7, 5)[k]][:, :].rearrange("p (a d) -> p a d", d=D)
                if k == 0:
                    dve.wait_ge(s_rowg, 16 * i)
                    dve.wait_ge(s_out, 16 * i)
                dve.wait_ge(s_o, 2 * (i - 1) + k + 1)
                dve.tensor_tensor(rows, rows, row_g[:, :].unsqueeze(1).to_broadcast([P, 2, D]), ALU.mult).then_inc(s_og, 1)
                dve.wait_ge(s_og, 2 * (i - 1) + k + 1)
                dve.tensor_tensor(o_s[:, 2 * k:2 * k + 2, :], rows, x1[:, 2 * k:2 * k + 2, :], ALU.add).then_inc(s_of, 1)

            def y_rows(i, k, ffn):
                rows = bank[(3, 2)[k]][:, :].rearrange("p (a d) -> p a d", d=D)
                if k == 0:
                    if ffn:
                        dve.wait_ge(s_of, 2 * i)
                    dve.wait_ge(s_rowa, 16 * (i + 1))
                    dve.wait_ge(s_xr, i + 1)
                dve.wait_ge(s_y, 2 * i + k + 1)
                dve.tensor_tensor(rows, rows, row_a[:, 0, :].unsqueeze(1).to_broadcast([P, 2, D]), ALU.mult).then_inc(s_yg, 1)
                dve.wait_ge(s_yg, 2 * i + k + 1)
                dve.tensor_tensor(x1[:, 2 * k:2 * k + 2, :], rows, x_rest[:, 2 * k:2 * k + 2, :], ALU.add).then_inc(s_yr, 1)

            def batch(i, att, ffn, first=False):
                n0 = 8 * B + 8 * i
                if att:
                    current(i)
                for s in range(PR + 4):
                    if ffn and 4 <= s < 12:
                        f = s - 4
                        m = 8 * (i - 1) + f
                        dve.wait_ge(s_f1, m + 1)
                        dve.tensor_scalar(bank[5 + f % 2][:, :], bank[5 + f % 2][:, :], 0.0, val_down[:, 1:2], ALU.max, ALU.mult).then_inc(s_r1, 1)
                        dve.wait_ge(s_r1, m + 1)
                        dve.wait_ge(s_r0, m + 1)
                        if f >= 2:
                            dve.wait_ge(s_rs, m - 1)
                        dve.scalar_tensor_tensor(out=sum_f[f % 2], in0=relu0[f % 2], scalar=val_s[:, 0:1], in1=bank[5 + f % 2][:, :],
                                                 op0=ALU.mult, op1=ALU.add).then_inc(s_rf, 1)
                    if att and s == PR:
                        reciprocals(i, 0)
                    if att and 0 <= s - 1 < PR:
                        p = s - 1
                        if p >= 2:
                            dve.wait_ge(s_qt, 8 * i + p - 1)
                        shifted_scores(n0 + p, p, qexp[p % 2][:, :, :], QUERY_BANKS, True)
                    if att and s < PR:
                        projection_lo(n0 + s, s, QUERY_BANKS)
                    if att and s == 0:
                        for p in range(PR):
                            dve.wait_ge(s_gh, 8 * i + 2 * (p // 2) + 2)
                            dve.scalar_tensor_tensor(out=g_s[:, LO, p, :], in0=bank[(7, 3)[p // 2 % 2]][:, (p % 2) * D:(p % 2 + 1) * D],
                                                     scalar=k_rec[:, p:p + 1], in1=g_s[:, HI, p, :], op0=ALU.mult, op1=ALU.subtract).then_inc(s_ge, 1)
                    if ffn and s == 2:
                        r = TOPK * R
                        dve.wait_ge(s_zh, i)
                        dve.scalar_tensor_tensor(out=z_s[r:2 * r, :], in0=bank[7][r:2 * r, :], scalar=1.0 / W_UP, in1=z_s[r:2 * r, :],
                                                 op0=ALU.mult, op1=ALU.subtract).then_inc(s_ze, 1)
                    if att and s >= PR:
                        attw_float(i, s - PR)
                if att:
                    reciprocals(i, 1)
                if ffn:
                    out_rows(i, 0)
                if att:
                    attw_float(i, 4)
                    attw_float(i, 5)
                if ffn and not att:
                    out_rows(i, 1)
                if att:
                    attw_float(i, 6)
                    attw_float(i, 7)
                    if ffn:
                        out_rows(i, 1)
                    y_rows(i, 0, ffn)
                    y_rows(i, 1, ffn)
                    dve.wait_ge(s_yr, 2 * i + 2)
                    ln_stats(B + i, x1, modT[:, i, 6:10])
                    ln_apply(B + i, x1)

            batch(0, True, False, first=True)
            with dve.Fori(1, B) as i:
                batch(i, True, True)
            batch(B, False, True)


_INS = ["L0_attn_x", "L0_attn_Wq", "L0_attn_Wk", "L0_attn_Wv", "L0_attn_Wo", "L0_attn_bo"]


def kernel(**inputs):
    import numpy as np
    import concourse.bacc as bacc
    from concourse.bass_utils import run_bass_kernel_spmd

    f = "L0_ffn_"
    arrays = {name: np.asarray(inputs[name]) for name in _INS}
    arrays["P_t"] = np.asarray(inputs["L0_attn_P"]).T
    arrays["wi_t"] = np.asarray(inputs[f + "wi_w"]).T
    arrays["wo_t"] = np.asarray(inputs[f + "wo_w"]).T
    arrays["lora_a_t"] = np.asarray(inputs[f + "lora_As"]).transpose(0, 2, 1)
    arrays["lora_b_t"] = np.asarray(inputs[f + "lora_Bs"]).transpose(0, 2, 1)
    arrays["index"] = np.asarray(inputs[f + "top_k_indices"])
    arrays["value"] = np.asarray(inputs[f + "top_k_values"])
    arrays["c_t"] = np.asarray(inputs["L0_c"]).T
    arrays["wmod"] = np.asarray(inputs["L0_wmod"])
    arrays = {"in_" + k: np.ascontiguousarray(a) for k, a in arrays.items()}
    nc = bacc.Bacc("TRN2", target_bir_lowering=False, num_devices=1)
    args = [nc.dram_tensor(k, a.shape, mybir.dt.from_np(a.dtype), kind="ExternalInput").ap() for k, a in arrays.items()]
    args.append(nc.dram_tensor("out_x", (B, T, D), F32, kind="ExternalOutput").ap())
    build(nc, *args)
    return run_bass_kernel_spmd(nc, [arrays], core_ids=[0]).results[0]["out_x"]
```

```python
import math
from contextlib import ExitStack

import concourse.bass as bass
from concourse import mybir

F32 = mybir.dt.float32
F16 = mybir.dt.float16
I32 = mybir.dt.int32
ALU = mybir.AluOpType
ACT = mybir.ActivationFunctionType
AX = mybir.AxisListType
RMAX = bass.bass_isa.ReduceOp.max

B, T, D = 8, 512, 256
H, DH, M = 16, 64, 64
F, R, EXP, TOPK = 1024, 16, 8, 2
P = 128
DC = D // P
TC = T // P
PR = H * DH // P
FC = F // P
EPS = 1e-4
LN_EPS = 1e-5
DN = float(DH) ** -0.25
LAST = B - 1
W_UP = 256.0
SQ_UP = 1.0 / 256
KEY_UP = 14
KEY_SHIFT = KEY_UP * math.log(2.0)
ATT_UP = 1024.0
HI, LO = 0, 1
PARTS = ((HI, HI), (HI, LO), (LO, HI))
ZR = 3 * TOPK * R
KEY_BANKS = ((0, 1), (2, 3), 4)
QUERY_BANKS = ((0, 4), (1, 1), 2)
G_BANKS = (5, 1, 6, 7)


def build(nc, x, wq, wk, wv, wo, bo, pT, wiT, woT, laT, lbT, idx, val, cT, wmod, out):
    with ExitStack() as ctx:
        def sb(name, shape, dt=F32):
            return ctx.enter_context(nc.sbuf_tensor(name, shape, dt))

        def sem(name):
            return ctx.enter_context(nc.semaphore(name))

        wq_s = sb("wq_s", [P, 2, DC, H * DH], F16)
        wk_s = sb("wk_s", [P, 2, DC, H * DH], F16)
        wi_s = sb("wi_s", [P, 2, DC, F], F16)
        wo2_s = sb("wo2_s", [P, 2, FC, D], F16)
        wv_s = sb("wv_s", [P, DC, H * DH])
        wo_s = sb("wo_s", [P, PR, D])
        lora_a_f = sb("lora_a_f", [P, DC, TOPK * R])
        lora_a = sb("lora_a", [P, 2, DC, 3, TOPK * R], F16)
        lora_first = sb("lora_first", [ZR, F], F16)
        lora_delta = sb("lora_delta", [ZR, F], F16)
        lora_sign = sb("lora_sign", [ZR, 1])
        pfeat_f = sb("pfeat_f", [P, P])
        pfeat = sb("pfeat", [P, 2, P], F16)
        ident = sb("ident", [P, P])
        ident16 = sb("ident16", [P, P], F16)
        ones = sb("ones", [P, 1], F16)
        head_half = sb("head_half", [P, 2], F16)
        neg_half = sb("neg_half", [P, TC])
        idx_s = sb("idx_s", [1, TOPK], I32)
        val_s = sb("val_s", [P, TOPK])
        val_neg = sb("val_neg", [P, TOPK])
        val_abs = sb("val_abs", [P, TOPK])
        val_sign = sb("val_sign", [P, TOPK])
        val_pair = sb("val_pair", [P, 1])
        c_s = sb("c_s", [P, DC, B])
        silu_a = sb("silu_a", [P, DC, B])
        silu_b = sb("silu_b", [P, DC, B])
        silu_c = sb("silu_c", [P, DC, B])
        modT = sb("modT", [P, B, 12])
        sa_v = sb("sa_v", [P, PR, B])

        hT = sb("hT", [P, B, 2, DC, T], F16)
        ctx_raw = sb("ctx_raw", [P, B, PR, M])
        k_raw = sb("k_raw", [P, B, PR])
        v_in = sb("v_in", [P, DC, 2, B])
        v_raw = sb("v_raw", [P, B, PR])
        mref = sb("mref", [P, B])
        scale_all = sb("scale_all", [P, B])
        gmax = sb("gmax", [P, 1])

        x_in = sb("x_in", [P, TC, D])
        xhat = sb("xhat", [P, TC, D])
        xhat2 = [sb(f"xhat2{i}", [P, 2, TC, D], F16) for i in range(2)]
        stats = sb("stats", [P, TC, 6])
        meanvar = sb("meanvar", [P, TC, 2])
        var_eps = sb("var_eps", [P, TC])
        rstd = sb("rstd", [P, TC])
        mod_cur = sb("mod_cur", [P, 4])
        ca_cur = sb("ca_cur", [P, DC])
        h_f = sb("h_f", [P, DC, T])
        proj = [sb(f"proj{i}", [P, 2, T], F16) for i in range(2)]
        sq_f = [sb(f"sq_f{i}", [P, T]) for i in range(2)]
        sq = [sb(f"sq{i}", [P, 2, T], F16) for i in range(2)]
        mx = sb("mx", [P, PR, 2 * TC])
        shift = [sb(f"shift{i}", [P, 2 * TC]) for i in range(2)]
        bmax = sb("bmax", [P, 1])
        bmax_all = sb("bmax_all", [P, 1])
        pool_pad = sb("pool_pad", [P, 1])
        neg_ref = sb("neg_ref", [P, 1])
        scores = sb("scores", [P, PR, TC, P])
        kexp = sb("kexp", [P, 2, PR, TC, P], F16)
        featT = sb("featT", [P, DC, H * M])
        attw = scores[:, :, :, :].rearrange("p a b c -> p (a b c)").bitcast(F16).rearrange("p (s a t) -> p s a t", s=2, a=PR)
        relu_sum = kexp[:, :, :, :, :].rearrange("p s a b c -> p s a (b c)")
        g_s = featT[:, :, :].rearrange("p a b -> p (a b)").bitcast(F16).rearrange("p (s a d) -> p s a d", s=2, d=D)
        scale_cur = sb("scale_cur", [P, 1])
        v_cur = sb("v_cur", [P, PR])
        k_cur = sb("k_cur", [P, PR])
        k_rec = sb("k_rec", [P, PR])
        ctx_bd = sb("ctx_bd", [P, PR, P])
        wv_flat = wv_s[:, :, :].rearrange("p c n -> p (c n)")
        qexp = [wv_flat[:, T * i:T * (i + 1)].rearrange("p (a b) -> p a b", b=P) for i in range(2)]
        work = sb("work", [P, 4, T])
        qk = [work[:, i, :] for i in range(2)]
        k_row = work[:, 2:4, :].rearrange("p a t -> p (a t)")
        qsum = [sb(f"qsum{i}", [P, 2 * TC]) for i in range(2)]
        qrec = [sb(f"qrec{i}", [P, 2 * TC]) for i in range(2)]
        w2 = [sb(f"w2{i}", [P, 2, T], F16) for i in range(2)]
        wk_flat = wk_s[:, :, :, :].rearrange("p s c n -> p (s c n)").bitcast(F32)
        relu0 = [wk_flat[:, T * i:T * (i + 1)] for i in range(2)]
        sum_f = [wk_flat[:, T * (2 + i):T * (3 + i)] for i in range(2)]
        h2T = xhat2[0][:, :, :, :].rearrange("p s a b -> p s (a b)").rearrange("p s (c t) -> p s c t", c=DC)
        z_s = sb("z_s", [ZR, T], F16)
        x_rest = x_in
        x1 = wv_flat[:, 2 * T:4 * T].rearrange("p (a b) -> p a b", b=D)
        row_a = sb("row_a", [P, 2, D])
        row_g = sb("row_g", [P, D])
        o_s = xhat2[1][:, :, :, :].rearrange("p s a b -> p (s a b)").bitcast(F32).rearrange("p (a b) -> p a b", b=D)
        wmod_s = scores[:, :, :, :].rearrange("p a b c -> p (a b c)")[:, 0:DC * 6 * D].rearrange("p (a b) -> p a b", a=DC)
        wk_f = featT
        e_flat = kexp[:, :, :, :, :].rearrange("p s a b c -> p (s a b c)").bitcast(F32)
        wq_f = e_flat[:, 0:DC * H * DH].rearrange("p (c n) -> p c n", c=DC)
        wi_f = e_flat[:, DC * H * DH:2 * DC * H * DH].rearrange("p (c n) -> p c n", c=DC)
        wo2_f = featT[:, :, :].rearrange("p a t -> p (a t)").rearrange("p (c n) -> p c n", c=FC)
        lora_b_f = work[0:ZR, :, :].rearrange("p a t -> p (a t)").rearrange("p (k f) -> p k f", k=2)
        gates_raw = row_a[0:B, :, :]
        bo_s = row_g[0:B, :]
        gate_row = work[0:B, 2:4, :].rearrange("p a t -> p (a t)").rearrange("p (a d) -> p a d", d=D)[:, 0:3, :]
        gates = work[0:B, 0, :].rearrange("p (a d) -> p a d", d=D)
        gate_abs = work[0:B, 1, :].rearrange("p (a d) -> p a d", d=D)
        rows_dram = nc.dram_tensor("rows_scratch", (B, 3, D), F32, kind="Internal").ap()

        bank = [ctx.enter_context(nc.psum_tensor(f"bank{i}", [P, 512], F32)) for i in range(8)]
        tr16 = bank[3][:, :].bitcast(F16).rearrange("p (s t) -> p s t", s=2)

        s_small = sem("small_loaded")
        s_wk = sem("wk_loaded")
        s_wv = sem("wv_loaded")
        s_rest = [sem(f"{k}_loaded") for k in ("wq", "wi", "wo2", "lora")]
        s_pre = sem("features_loaded")
        s_idx = sem("index_loaded")
        s_x = sem("x_loaded")
        s_rowa = sem("row_a_loaded")
        s_rowg = sem("row_g_loaded")
        s_out = sem("out_stored")
        c_pool = sem("pool_constants_ready")
        c_dve = sem("dve_constants_ready")
        c_id0 = sem("ident_zeroed")
        p_exp = sem("silu_exp")
        p_dve = sem("silu_steps")
        p_mod = sem("mod_mm")
        p_modT = sem("modT_ready")
        p_sav = sem("sa_v_mm")
        p_savs = sem("sa_v_ready")
        p_r = sem("row_mm")
        p_gate = sem("gate_steps")
        p_rows = sem("rows_ready")
        p_pf = sem("pfeat_steps")
        p_lora = sem("lora_steps")
        w_hi = sem("weight_hi")
        w_lo = sem("weight_lo")
        s_stat = sem("stats_done")
        s_agg = sem("aggregated")
        s_var = sem("variance_ready")
        s_rstd = sem("rstd_ready")
        s_xhat = sem("xhat_ready")
        s_xh = sem("xhat_hi")
        s_xl = sem("xhat_lo")
        s_modc = sem("mod_current")
        s_tr = sem("hT_mm")
        s_hh = sem("hT_hi")
        s_hT = sem("hT_ready")
        s_pm = sem("proj_mm")
        s_pe = sem("proj_read_by_act")
        s_qh = sem("square_hi")
        s_pl = sem("proj_lo")
        s_sl = sem("square_lo")
        s_dd = sem("scores_mm")
        s_dg = sem("diag_mm")
        s_mx = sem("max_ready")
        s_sh = sem("shift_ready")
        s_ss = sem("scores_shifted")
        s_bm = sem("batch_max")
        s_bma = sem("batch_max_all")
        s_nr = sem("neg_ref_ready")
        s_ke = sem("key_exp")
        s_kh = sem("key_exp_hi")
        s_kl = sem("key_exp_lo")
        s_sum = sem("sums_mm")
        s_sume = sem("sums_ready")
        s_ft = sem("feat_mm")
        s_fte = sem("feat_ready")
        s_cx = sem("ctx_mm")
        s_cxe = sem("ctx_ready")
        s_sv = sem("v_raw_mm")
        s_sve = sem("v_raw_ready")
        s_gm = sem("gmax_ready")
        s_sc = sem("scale_ready")
        s_cur = sem("current_ready")
        s_cur_a = sem("current_steps")
        s_bd = sem("ctx_bd_ready")
        s_kr = sem("k_row_mm")
        s_krc = sem("k_row_ready")
        s_g = sem("g_mm")
        s_gh = sem("g_hi")
        s_ge = sem("g_ready")
        s_qe = sem("query_exp")
        s_qk = sem("qk_ready")
        s_qs = sem("query_sums")
        s_qr = sem("query_rec")
        s_wf = sem("weights_float")
        s_wh = sem("weights_hi")
        s_wl = sem("weights_lo")
        s_wt = sem("weights_tr")
        s_w = sem("attw_ready")
        s_xr = sem("x_rest_ready")
        s_y = sem("y_mm")
        s_yg = sem("y_gated")
        s_yr = sem("y_read")
        s_x1 = sem("x1_ready")
        s_z = sem("z_mm")
        s_zh = sem("z_hi")
        s_ze = sem("z_ready")
        s_f0 = sem("ffn_first_mm")
        s_r0 = sem("relu0_ready")
        s_f1 = sem("ffn_second_mm")
        s_r1 = sem("relu1_ready")
        s_rf = sem("relu_sum_float")
        s_rh = sem("relu_sum_hi")
        s_rs = sem("relu_sum_ready")
        s_o = sem("out_mm")
        s_og = sem("out_gated")
        s_of = sem("out_ready")

        block = ctx.enter_context(nc.Block())
        xv = x.rearrange("b (p t) d -> b p t d", t=TC)
        ov = out.rearrange("b (p t) d -> b p t d", t=TC)

        def heads(ap):
            return ap.rearrange("p (a m) -> p a m", m=M)

        @block.sync
        def _(sp):
            sp.dma_start(x_in[:, :, :], xv[0]).then_inc(s_x, 16)
            sp.dma_start(idx_s[:, :], idx.rearrange("(a n) -> a n", a=1)).then_inc(s_idx, 16)
            sp.dma_start(c_s[:, :, :], cT.rearrange("(c p) b -> p c b", p=P)).then_inc(s_small, 16)
            sp.dma_start(wmod_s, wmod.rearrange("(c p) n -> p c n", p=P)).then_inc(s_small, 16)
            sp.dma_start(wk_f[:, :, :], wk.rearrange("(c p) n -> p c n", p=P)).then_inc(s_wk, 16)
            sp.wait_ge(c_pool, 1)
            sp.dma_start(pfeat_f[0:DH, 0:M], pT).then_inc(s_pre, 16)
            sp.dma_start(pfeat_f[DH:P, M:P], pT).then_inc(s_pre, 16)
            sp.dma_start(wq_f, wq.rearrange("(c p) n -> p c n", p=P)).then_inc(s_rest[0], 16)
            sp.dma_start(wi_f, wiT.rearrange("(c p) n -> p c n", p=P)).then_inc(s_rest[1], 16)
            sp.wait_ge(w_lo, 1)
            sp.dma_start(wo2_f, woT.rearrange("(c p) n -> p c n", p=P)).then_inc(s_rest[2], 16)
            sp.wait_ge(s_idx, 16)
            expert = [sp.value_load(idx_s[0:1, k:k + 1], min_val=0, max_val=EXP - 1) for k in range(TOPK)]
            lb = [lbT[bass.ds(e, 1)].rearrange("o r f -> (o r) f") for e in expert]
            for g in range(3):
                r = g * TOPK * R
                sp.dma_start(lora_b_f[r:r + R, 0, :], lb[0]).then_inc(s_rest[3], 16)
                for k in range(TOPK):
                    sp.dma_start(lora_b_f[r + k * R:r + (k + 1) * R, 1, :], lb[k]).then_inc(s_rest[3], 16)
            for k in range(TOPK):
                sp.dma_start(lora_a_f[:, :, k * R:(k + 1) * R],
                             laT[bass.ds(expert[k], 1)].rearrange("o (c p) r -> p (o c) r", p=P)).then_inc(s_rest[3], 16)
            sp.dma_start(val_s[:, :], val.rearrange("(a n) -> a n", a=1).to_broadcast([P, TOPK])).then_inc(s_rest[3], 16)
            sp.dma_start(wv_s[:, :, :], wv.rearrange("(c p) n -> p c n", p=P)).then_inc(s_wv, 16)
            sp.dma_start(wo_s[:, :, :], wo.rearrange("(c p) n -> p c n", p=P)).then_inc(s_wv, 16)
            sp.dma_start(bo_s[:, :], bo.rearrange("(a n) -> a n", a=1).to_broadcast([B, D])).then_inc(s_wv, 16)
            with sp.Fori(1, B) as b:
                sp.wait_ge(s_xhat, b)
                sp.dma_start(x_in[:, :, :], xv[b]).then_inc(s_x, 16)
            sp.wait_ge(p_rows, 1)
            sp.dma_start(rows_dram, gate_row).then_inc(s_out, 16)
            sp.wait_ge(s_out, 16)

            def load_att(i, first):
                sp.wait_ge(s_xhat, B) if first else sp.wait_ge(s_yr, 2 * i)
                sp.dma_start(x_in[:, :, :], xv[i]).then_inc(s_x, 16)
                sp.dma_start(row_a[:, :, :].rearrange("p a d -> p (a d)"),
                             rows_dram[bass.ds(i, 1), 0:2, :].rearrange("o a d -> o (a d)").to_broadcast([P, 2 * D])).then_inc(s_rowa, 16)

            def load_gate(i, first=False):
                if not first:
                    sp.wait_ge(s_of, 2 * (i - 1))
                sp.dma_start(row_g[:, :], rows_dram[bass.ds(i - 1, 1), 2, :].to_broadcast([P, D])).then_inc(s_rowg, 16)

            def store(i):
                sp.wait_ge(s_of, 2 * i)
                sp.dma_start(ov[i - 1], o_s).then_inc(s_out, 16)

            load_att(0, True)
            load_att(1, False)
            load_gate(1, first=True)
            store(1)
            with sp.Fori(2, B) as i:
                load_att(i, False)
                load_gate(i)
                store(i)
            load_gate(B)
            store(B)
            sp.wait_ge(s_out, 16 * (B + 1))

        @block.gpsimd
        def _(pool):
            pool.memset(pfeat_f[:, :], 0.0)
            pool.memset(lora_b_f, 0.0).then_inc(c_pool, 1)
            pool.memset(neg_half[:, :], -0.5)
            pool.memset(ctx_bd[:, :, :], 0.0)
            pool.memset(ident[:, :], 0.0).then_inc(c_id0, 1)
            pool.wait_ge(c_id0, 1)
            pool.affine_select(out=ident[:, :], in_=ident[:, :], compare_op=ALU.not_equal, fill=1.0,
                               base=0, pattern=[[-1, P]], channel_multiplier=1).then_inc(c_pool, 1)
            pool.wait_ge(c_pool, 2)
            pool.tensor_copy(ident16[:, :], ident[:, :]).then_inc(c_pool, 1)

            def lower(out, value, hi):
                return pool.tensor_tensor(out, value, hi, ALU.subtract)

            def ln_power(n):
                pool.wait_ge(s_var, n + 1)
                pool.tensor_tensor(rstd[:, :], var_eps[:, :], neg_half[:, :], ALU.pow).then_inc(s_rstd, 1)

            def h_lower(n, c, dst):
                pool.wait_ge(s_hh, 4 * n + 2 * c + 2)
                lower(dst[LO][c], h_f[:, c, :], dst[HI][c]).then_inc(s_hT, 1)

            def x_lower(n, par):
                pool.wait_ge(s_xh, n + 1)
                lower(xhat2[par][:, LO, :, :], xhat[:, :, :], xhat2[par][:, HI, :, :]).then_inc(s_xl, 1)

            def square_lower(n, p):
                pool.wait_ge(s_qh, n + 1)
                lower(sq[p % 2][:, LO, :], sq_f[p % 2][:, :], sq[p % 2][:, HI, :]).then_inc(s_sl, 1)

            def key_lower(u, q):
                pool.wait_ge(s_kh, 4 * u + q + 1)
                lower(kexp[:, LO, 2 * q:2 * q + 2, :, :], scores[:, 2 * q:2 * q + 2, :, :], kexp[:, HI, 2 * q:2 * q + 2, :, :]).then_inc(s_kl, 1)

            def batch_max(b):
                pool.wait_ge(s_bm, b + 1)
                pool.tensor_tensor(pool_pad[:, :], neg_half[:, 0:1], neg_half[:, 0:1], ALU.mult)
                pool.partition_all_reduce(bmax_all[:, :], bmax[:, :], P, RMAX).then_inc(s_bma, 1)

            def hT_of(b):
                return [[hT[:, b, s, c, :] for c in range(DC)] for s in range(2)]

            def keys(b, par, has_u, has_next):
                for s in range(PR + 1):
                    if s < PR:
                        square_lower(8 * b + s, s)
                    if has_u and s < 4:
                        key_lower(b - 1, s)
                    if has_next and s == 3:
                        ln_power(b + 1)
                    if has_next and s == 7:
                        h_lower(b + 1, 0, hT_of(b + 1))
                batch_max(b)
                if has_next:
                    h_lower(b + 1, 1, hT_of(b + 1))
                    x_lower(b + 1, 1 - par)

            ln_power(0)
            h_lower(0, 0, hT_of(0))
            h_lower(0, 1, hT_of(0))
            x_lower(0, 0)
            keys(0, 0, False, True)
            with pool.Fori(0, B // 2 - 1) as h:
                keys(2 * h + 1, 1, True, True)
                keys(2 * h + 2, 0, True, True)
            keys(LAST, 1, True, False)
            for q in range(4):
                key_lower(LAST, q)

            h2 = [[h2T[:, s, c, :] for c in range(DC)] for s in range(2)]

            def weight_float(i, p):
                pool.wait_ge(s_qr, 8 * i + p + 1)
                pool.tensor_tensor(heads(qk[p % 2]), heads(qk[p % 2]), qrec[p % 2][:, :].unsqueeze(2).to_broadcast([P, 2 * TC, M]),
                                   ALU.mult).then_inc(s_wf, 1)

            def weight_lower(i, p):
                pool.wait_ge(s_wh, 8 * i + p + 1)
                lower(w2[p % 2][:, LO, :], qk[p % 2], w2[p % 2][:, HI, :]).then_inc(s_wl, 1)

            def batch(i, att, ffn):
                n0 = 8 * B + 8 * i
                for s in range(PR + 4):
                    if att and 0 <= s - 3 < PR:
                        weight_lower(i, s - 3)
                    if ffn and 4 <= s < 12:
                        f = s - 4
                        pool.wait_ge(s_rh, 8 * (i - 1) + f + 1)
                        lower(relu_sum[:, LO, f, :], sum_f[f % 2], relu_sum[:, HI, f, :]).then_inc(s_rs, 1)
                    if att and 0 <= s - 2 < PR:
                        weight_float(i, s - 2)
                    if att and s < PR:
                        square_lower(n0 + s, s)
                    if ffn and s == 1:
                        for c in range(DC):
                            h_lower(B + i - 1, c, h2)
                    if att and s == 2:
                        pool.wait_ge(s_x, 16 * (B + i + 1))
                        pool.wait_ge(s_rowa, 16 * (i + 1))
                        for j in range(TC):
                            op = pool.tensor_tensor(x_rest[:, j, :], x_in[:, j, :], row_a[:, 1, :], ALU.add)
                        op.then_inc(s_xr, 1)
                if att:
                    ln_power(B + i)

            batch(0, True, False)
            with pool.Fori(1, B) as i:
                batch(i, True, True)
            batch(B, False, True)

        @block.tensor
        def _(pe):
            def transpose_x(c, dst):
                for j in range(TC):
                    op = pe.transpose(dst[:, j * P:(j + 1) * P], xhat[:, j, c * P:(c + 1) * P], ident[:, :])
                op.then_inc(s_tr, 1)

            def project(n, p, b, w, banks):
                for a in range(3):
                    st, mv = PARTS[a]
                    for c in range(DC):
                        op = pe.matmul(bank[banks[0][p % 2]][:, :], w[:, st, c, p * P:(p + 1) * P], hT[:, b, mv, c, :],
                                       start=(a == 0 and c == 0), stop=(a == 2 and c == DC - 1))
                op.then_inc(s_pm, 1)

            def score(n, p, banks):
                pe.wait_ge(s_pl, n + 1)
                for j in range(TC):
                    for a in range(3):
                        st, mv = PARTS[a]
                        op = pe.matmul(bank[banks[1][p % 2]][:, j * P:(j + 1) * P], proj[p % 2][:, st, j * P:(j + 1) * P], pfeat[:, mv, :],
                                       start=(a == 0), stop=(a == 2))
                op.then_inc(s_dd, 1)

            def diag(n, p, banks, first):
                pe.wait_ge(s_sl, n + 1)
                if not first:
                    pe.wait_ge(s_sh, n)
                for j in range(TC):
                    for a in (HI, LO):
                        op = pe.matmul(bank[banks[2]][:, 2 * j:2 * j + 2], sq[p % 2][:, a, j * P:(j + 1) * P], head_half[:, :], start=(a == HI), stop=(a == LO))
                op.then_inc(s_dg, 1)

            def features(u, par, k):
                half, c = k // 2, k % 2
                if c == 0:
                    pe.wait_ge(s_kl, 4 * u + 2 * (half + 1))
                if k == 0:
                    pe.wait_ge(s_xl, u + 1)
                if k > 0:
                    pe.wait_ge(s_fte, 4 * u + k)
                for a in range(3):
                    st, mv = PARTS[a]
                    for j in range(TC):
                        op = pe.matmul(bank[7][:, :], xhat2[par][:, st, j, c * P:(c + 1) * P], kexp[:, mv, 4 * half:4 * half + 4, j, :],
                                       start=(a == 0 and j == 0), stop=(a == 2 and j == TC - 1))
                op.then_inc(s_ft, 1)

            def sums(u, par):
                pe.wait_ge(s_kl, 4 * u + 4)
                for p in range(PR):
                    for a in (HI, LO):
                        for j in range(TC):
                            pe.matmul(bank[5][:, p:p + 1], kexp[:, a, p, j, :], ones[:, :], start=(a == HI and j == 0), stop=(a == LO and j == TC - 1))
                for c in range(DC):
                    for a in (HI, LO):
                        for j in range(TC):
                            op = pe.matmul(bank[5][:, PR + c:PR + c + 1], xhat2[par][:, a, j, c * P:(c + 1) * P], ones[:, :],
                                           start=(a == HI and j == 0), stop=(a == LO and j == TC - 1))
                op.then_inc(s_sum, 1)

            def contexts(u):
                pe.wait_ge(s_fte, 4 * u + 4)
                pe.wait_ge(s_sume, u + 1)
                for p in range(PR):
                    for c in range(DC):
                        op = pe.matmul(bank[(7, 5)[p // 4]][:, p % 4 * P:(p % 4 + 1) * P], wv_s[:, c, p * P:(p + 1) * P],
                                       featT[:, c, p * P:(p + 1) * P], start=(c == 0), stop=(c == DC - 1))
                op.then_inc(s_cx, 1)

            pe.wait_ge(p_dve, 3)
            pe.wait_ge(s_small, 32)
            for ch in (0, 1, 2, 3, 6, 7, 8, 9):
                for c in range(DC):
                    op = pe.matmul(bank[6][:, ch * B:(ch + 1) * B], wmod_s[:, c, ch * P:(ch + 1) * P], silu_c[:, c, :], start=(c == 0), stop=(c == DC - 1))
            op.then_inc(p_mod, 1)
            for g, col in enumerate((2 * D, 5 * D)):
                for c in range(DC):
                    op = pe.matmul(bank[7][0:B, g * D:(g + 1) * D], silu_c[:, c, :], wmod_s[:, c, col:col + D], start=(c == 0), stop=(c == DC - 1))
            op.then_inc(p_mod, 1)
            pe.wait_ge(c_pool, 2)
            pe.wait_ge(s_xhat, 1)
            pe.wait_ge(p_modT, 1)
            transpose_x(0, bank[6])
            pe.wait_ge(s_hh, 2)
            transpose_x(1, bank[6])
            pe.wait_ge(w_lo, 1)
            pe.wait_ge(p_pf, 3)
            pe.wait_ge(c_dve, 2)

            def keys(b, par, has_u, has_next):
                pe.wait_ge(s_hT, 2 * (b + 1))
                for s in range(PR + 1):
                    n = 8 * b + s
                    if s < PR:
                        if has_u or s >= 2:
                            pe.wait_ge(s_pl, n - 1)
                        project(n, s, b, wk_s, KEY_BANKS)
                    if s >= 1:
                        if has_u or s >= 3:
                            pe.wait_ge(s_ss, n - 2)
                        score(n - 1, s - 1, KEY_BANKS)
                    if s >= 2:
                        diag(n - 2, s - 2, KEY_BANKS, first=not has_u and s == 2)
                    if has_u:
                        u = b - 1
                        if 3 <= s < 7:
                            features(u, 1 - par, s - 3)
                        if s == 4:
                            sums(u, 1 - par)
                        if s == 7:
                            contexts(u)
                    if has_next and s == 6:
                        pe.wait_ge(s_xhat, b + 2)
                        transpose_x(0, bank[6])
                    if has_next and s == 7:
                        pe.wait_ge(s_hh, 4 * (b + 1) + 2)
                        transpose_x(1, bank[6])
                diag(8 * b + 7, 7, KEY_BANKS, False)
                if has_u:
                    pe.wait_ge(s_cxe, b)

            keys(0, 0, False, True)
            pe.wait_ge(s_wv, 48)
            with pe.Fori(0, B // 2 - 1) as h:
                keys(2 * h + 1, 1, True, True)
                keys(2 * h + 2, 0, True, True)
            keys(LAST, 1, True, False)
            for k in range(4):
                features(LAST, 1, k)
            sums(LAST, 1)
            contexts(LAST)
            pe.wait_ge(s_sume, B)
            for p in range(PR):
                for c in range(DC):
                    op = pe.matmul(bank[6][:, p * 2 * B:(p + 1) * 2 * B], wv_s[:, c, p * P:(p + 1) * P], v_in[:, c, :, :], start=(c == 0), stop=(c == DC - 1))
            op.then_inc(s_sv, 1)
            pe.wait_ge(s_sve, 1)
            for p in range(PR):
                op = pe.matmul(bank[6][0:B, 0:D], sa_v[:, p, :], wo_s[:, p, :], start=(p == 0), stop=(p == PR - 1))
            op.then_inc(p_r, 1)

            def k_rows(i, first):
                pe.wait_ge(s_cur, i + 1)
                for half in range(2):
                    for q in range(4):
                        p = 4 * half + q
                        op = pe.matmul(bank[6 + half][:, q * P:(q + 1) * P], k_cur[:, p:p + 1].to_broadcast([P, P]), ident[:, :], start=True, stop=True)
                    op.then_inc(s_kr, 1)

            def g_mm(i, k):
                if k >= 2:
                    pe.wait_ge(s_krc, 2 * i + k - 1)
                if k == 1:
                    pe.wait_ge(s_ss, 8 * B + 8 * i)
                for q in range(2):
                    p = 2 * k + q
                    op = pe.matmul(bank[G_BANKS[k]][:, q * D:(q + 1) * D], ctx_bd[:, p, :], wo_s[:, p, :], start=True, stop=True)
                op.then_inc(s_g, 1)

            def weight_transposes(i, p, first):
                pe.wait_ge(s_wl, 8 * i + p + 1)
                if p == 0 and not first:
                    pe.wait_ge(s_yr, 2 * i)
                if p > 0:
                    pe.wait_ge(s_w, 8 * i + p)
                for part in range(2):
                    for j in range(TC):
                        op = pe.transpose(tr16[:, part, j * P:(j + 1) * P], w2[p % 2][:, part, j * P:(j + 1) * P], ident16[:, :])
                op.then_inc(s_wt, 1)

            def lora_in(i):
                pe.wait_ge(s_hT, 2 * (B + i))
                for a in range(3):
                    st, mv = PARTS[a]
                    for c in range(DC):
                        op = pe.matmul(bank[7][0:ZR, :], lora_a[:, st, c, :, :].rearrange("p g r -> p (g r)"), h2T[:, mv, c, :],
                                       start=(a == 0 and c == 0), stop=(a == 2 and c == DC - 1))
                op.then_inc(s_z, 1)

            def ffn_first(i, f):
                if f == 0:
                    pe.wait_ge(s_ze, i)
                if f >= 2:
                    pe.wait_ge(s_rf, 8 * (i - 1) + f - 1)
                dst = bank[5 + f % 2]
                for a in range(3):
                    st, mv = PARTS[a]
                    for c in range(DC):
                        pe.matmul(dst[:, :], wi_s[:, st, c, f * P:(f + 1) * P], h2T[:, mv, c, :], start=(a == 0 and c == 0), stop=False)
                pe.matmul(dst[:, :], lora_first[:, f * P:(f + 1) * P], z_s[:, :], start=False, stop=True).then_inc(s_f0, 1)

            def ffn_second(i, f):
                pe.wait_ge(s_r0, 8 * (i - 1) + f + 1)
                pe.matmul(bank[5 + f % 2][:, :], lora_delta[:, f * P:(f + 1) * P], z_s[:, :], start=False, stop=True, skip_group_check=True).then_inc(s_f1, 1)

            def ffn_out(i, k):
                if k == 0:
                    pe.wait_ge(s_rs, 8 * i)
                for j in (2 * k, 2 * k + 1):
                    for f in range(FC):
                        for a in range(3):
                            st, mv = PARTS[a]
                            op = pe.matmul(bank[(7, 5)[k]][:, (j % 2) * D:(j % 2 + 1) * D], relu_sum[:, st, f, j * P:(j + 1) * P], wo2_s[:, mv, f, :],
                                           start=(f == 0 and a == 0), stop=(f == FC - 1 and a == 2))
                op.then_inc(s_o, 1)

            def attention_out(i):
                pe.wait_ge(s_w, 8 * i + 8)
                for k in range(2):
                    for j in (2 * k, 2 * k + 1):
                        for p in range(PR):
                            for a in range(3):
                                st, mv = PARTS[a]
                                op = pe.matmul(bank[(3, 2)[k]][:, (j % 2) * D:(j % 2 + 1) * D], attw[:, st, p, j * P:(j + 1) * P], g_s[:, mv, p, :],
                                               start=(p == 0 and a == 0), stop=(p == PR - 1 and a == 2))
                    op.then_inc(s_y, 1)

            def batch(i, att, ffn, first=False):
                n0 = 8 * B + 8 * i
                for s in range(PR + 4):
                    n = n0 + s
                    if ffn and 4 <= s < 12:
                        ffn_second(i, s - 4)
                    if att and s < PR:
                        pe.wait_ge(s_pl, n - 1)
                        project(n, s, i, wq_s, QUERY_BANKS)
                    if att and s == 0:
                        k_rows(i, first)
                        pe.wait_ge(s_bd, i + 1)
                        for k in range(4):
                            g_mm(i, k)
                    if ffn and s == 1:
                        pe.wait_ge(s_xhat, B + i)
                        pe.wait_ge(s_ge, 8 * i + 8) if att else pe.wait_ge(s_yr, 2 * i)
                        transpose_x(0, bank[7])
                        transpose_x(1, bank[6])
                    if ffn and s == 2:
                        lora_in(i)
                    if att and 0 <= s - 1 < PR:
                        pe.wait_ge(s_ss, n - 1)
                        if s == 1:
                            pe.wait_ge(s_ge, 8 * i + 4)
                        score(n - 1, s - 1, QUERY_BANKS)
                    if att and 0 <= s - 4 < PR:
                        weight_transposes(i, s - 4, first)
                    if att and 0 <= s - 1 < PR:
                        if s == 1 and not first:
                            pe.wait_ge(s_yr, 2 * i)
                        diag(n - 1, s - 1, QUERY_BANKS, False)
                    if ffn and 3 <= s < 11:
                        ffn_first(i, s - 3)
                if ffn:
                    ffn_out(i, 0)
                    ffn_out(i, 1)
                if att:
                    attention_out(i)

            pe.wait_ge(w_lo, 4)
            pe.wait_ge(p_lora, 2)
            pe.wait_ge(s_cxe, B)
            pe.wait_ge(s_sh, 8 * B)
            batch(0, True, False, first=True)
            with pe.Fori(1, B) as i:
                batch(i, True, True)
            batch(B, False, True)

        @block.scalar
        def _(act):
            act.wait_ge(s_small, 32)
            act.activation(silu_a[:, :, :], c_s[:, :, :], ACT.Exp, scale=-1.0).then_inc(p_exp, 1)

            def weight_hi(src, w, loaded):
                act.wait_ge(loaded, 16)
                act.activation(w, src, ACT.Copy, scale=W_UP).then_inc(w_hi, 1)

            def h_copy(n, c, dst, src, first=False):
                if c == 0:
                    act.wait_ge(s_modc, n + 1)
                    if not first:
                        act.wait_ge(s_hT, 2 * n)
                act.wait_ge(s_tr, 2 * n + c + 1)
                act.activation(dst[HI][c], src[:, :], ACT.Identity, bias=mod_cur[:, c:c + 1], scale=mod_cur[:, 2 + c:3 + c]).then_inc(s_hh, 1)
                act.activation(h_f[:, c, :], src[:, :], ACT.Identity, bias=mod_cur[:, c:c + 1], scale=mod_cur[:, 2 + c:3 + c]).then_inc(s_hh, 1)

            def hT_of(b):
                return [[hT[:, b, s, c, :] for c in range(DC)] for s in range(2)]

            def projection(n, p, banks, early):
                src = bank[banks[0][p % 2]]
                act.wait_ge(s_pm, n + 1)
                if not early:
                    act.wait_ge(s_dd, n - 1)
                act.activation(proj[p % 2][:, HI, :], src[:, :], ACT.Copy, scale=1.0 / W_UP).then_inc(s_pe, 1)
                if not early:
                    act.wait_ge(s_sl, n - 1)
                act.activation(sq_f[p % 2][:, :], src[:, :], ACT.Square, scale=math.sqrt(SQ_UP) / W_UP).then_inc(s_pe, 1)

            def key_exp(u, q):
                if q == 0:
                    act.wait_ge(s_nr, u + 1)
                part = scores[:, 2 * q:2 * q + 2, :, :]
                act.activation(part, part, ACT.Exp, bias=neg_ref[:, :]).then_inc(s_ke, 1)

            def feature_copy(u, k):
                half, c = k // 2, k % 2
                act.wait_ge(s_ft, 4 * u + k + 1)
                act.activation(featT[:, c, 512 * half:512 * (half + 1)], bank[7][:, :], ACT.Copy, scale=ca_cur[:, c:c + 1]).then_inc(s_fte, 1)

            def keys(b, par, has_u, has_next):
                for s in range(PR + 1):
                    if s < PR:
                        projection(8 * b + s, s, KEY_BANKS, early=not has_u and s < 2)
                    if has_u and s < 4:
                        key_exp(b - 1, s)
                    if not has_u and s in (2, 4, 6):
                        src, w, loaded = ((wq_f, wq_s, s_rest[0]), (wi_f, wi_s, s_rest[1]), (wo2_f, wo2_s, s_rest[2]))[s // 2 - 1]
                        weight_hi(src, w[:, HI, :, :], loaded)
                    if has_u and 3 <= s < 7:
                        feature_copy(b - 1, s - 3)
                    if has_next and s in (6, 7):
                        h_copy(b + 1, s - 6, hT_of(b + 1), bank[6])

            weight_hi(wk_f[:, :, :], wk_s[:, HI, :, :], s_wk)
            h_copy(0, 0, hT_of(0), bank[6], first=True)
            h_copy(0, 1, hT_of(0), bank[6], first=True)
            keys(0, 0, False, True)
            with act.Fori(0, B // 2 - 1) as h:
                keys(2 * h + 1, 1, True, True)
                keys(2 * h + 2, 0, True, True)
            keys(LAST, 1, True, False)
            for q in range(4):
                key_exp(LAST, q)
            for k in range(4):
                feature_copy(LAST, k)
            act.wait_ge(s_gm, 1)
            act.activation(scale_all[:, :], mref[:, :], ACT.Exp, bias=gmax[:, :]).then_inc(s_sc, 1)

            h2 = [[h2T[:, s, c, :] for c in range(DC)] for s in range(2)]

            def batch(i, att, ffn, first=False):
                n0 = 8 * B + 8 * i
                for s in range(PR + 4):
                    f = s - 4
                    if ffn and 0 <= f < FC:
                        act.wait_ge(s_f1, 8 * (i - 1) + f + 1)
                        act.activation(bank[5 + f % 2][:, :], bank[5 + f % 2][:, :], ACT.Relu, scale=val_abs[:, 1:2]).then_inc(s_r1, 1)
                    if att and s < PR:
                        projection(n0 + s, s, QUERY_BANKS, early=False)
                    if att and s == 0:
                        if first:
                            act.wait_ge(s_out, 16)
                        else:
                            act.wait_ge(s_y, 2 * i)
                        for half in range(2):
                            act.wait_ge(s_kr, 2 * i + half + 1)
                            act.activation(k_row[:, 512 * half:512 * (half + 1)], bank[6 + half][:, :], ACT.Copy).then_inc(s_krc, 1)
                        for p in range(PR):
                            if p % 2 == 0:
                                act.wait_ge(s_g, 4 * i + p // 2 + 1)
                            act.activation(g_s[:, HI, p, :], bank[G_BANKS[p // 2]][:, (p % 2) * D:(p % 2 + 1) * D], ACT.Copy,
                                           scale=k_rec[:, p:p + 1]).then_inc(s_gh, 1)
                    if ffn and s == 1:
                        h_copy(B + i - 1, 0, h2, bank[7])
                        h_copy(B + i - 1, 1, h2, bank[6])
                    if ffn and s == 2:
                        act.wait_ge(s_z, i)
                        act.activation(z_s[:, :], bank[7][0:ZR, :], ACT.Copy, scale=1.0 / W_UP).then_inc(s_zh, 1)
                    if att and 0 <= s - 3 < PR:
                        p = s - 3
                        act.wait_ge(s_wf, 8 * i + p + 1)
                        if not (first and p < 2):
                            act.wait_ge(s_wt, 8 * i + p - 1)
                        act.activation(w2[p % 2][:, HI, :], qk[p % 2], ACT.Copy).then_inc(s_wh, 1)
                    if att and 0 <= s - 4 < PR:
                        p = s - 4
                        act.wait_ge(s_wt, 8 * i + p + 1)
                        act.activation(attw[:, :, p, :], tr16, ACT.Copy).then_inc(s_w, 1)
                    if ffn and 0 <= f < FC:
                        act.wait_ge(s_rf, 8 * (i - 1) + f + 1)
                        act.activation(relu_sum[:, HI, f, :], sum_f[f % 2], ACT.Copy).then_inc(s_rh, 1)
                    if ffn and 3 <= s < 11:
                        f = s - 3
                        act.wait_ge(s_f0, 8 * (i - 1) + f + 1)
                        if f >= 2:
                            act.wait_ge(s_rf, 8 * (i - 1) + f - 1)
                        act.activation(relu0[f % 2], bank[5 + f % 2][:, :], ACT.Relu, scale=val_abs[:, 0:1]).then_inc(s_r0, 1)
                    if att and 0 <= s - 1 < PR:
                        p = s - 1
                        act.wait_ge(s_ss, n0 + p + 1)
                        act.activation(qexp[p % 2][:, :, :], qexp[p % 2][:, :, :], ACT.Exp).then_inc(s_qe, 1)

            batch(0, True, False, first=True)
            with act.Fori(1, B) as i:
                batch(i, True, True)
            batch(B, False, True)

        @block.vector
        def _(dve):
            def ln_stats(n, src, mod, first=False):
                for j in range(TC):
                    op = dve.bn_stats(stats[:, j, :], src[:, j, :])
                op.then_inc(s_stat, 1)
                if not first:
                    dve.wait_ge(s_hh, 4 * n)
                dve.wait_ge(s_stat, n + 1)
                dve.tensor_copy(mod_cur[:, :], mod).then_inc(s_modc, 1)
                for j in range(TC):
                    op = dve.bn_aggr(meanvar[:, j, :], stats[:, j, :])
                op.then_inc(s_agg, 1)
                dve.wait_ge(s_agg, n + 1)
                dve.tensor_scalar(var_eps[:, :], meanvar[:, :, 1], LN_EPS, None, ALU.add).then_inc(s_var, 1)

            def ln_apply(n, src, first=False):
                if not first:
                    dve.wait_ge(s_tr, 2 * n)
                dve.wait_ge(s_rstd, n + 1)
                for j in range(TC):
                    op = dve.tensor_scalar(xhat[:, j, :], src[:, j, :], meanvar[:, j, 0:1], rstd[:, j:j + 1], ALU.subtract, ALU.mult)
                op.then_inc(s_xhat, 1)

            def xhat_hi(n, par):
                dve.wait_ge(s_xhat, n + 1)
                dve.tensor_copy(xhat2[par][:, HI, :, :], xhat[:, :, :]).then_inc(s_xh, 1)

            def weight_lo(src, w, k):
                dve.wait_ge(w_hi, k + 1)
                dve.scalar_tensor_tensor(out=w[:, LO, :, :], in0=src, scalar=W_UP, in1=w[:, HI, :, :], op0=ALU.mult, op1=ALU.subtract).then_inc(w_lo, 1)

            def projection_lo(n, p, banks, early):
                dve.wait_ge(s_pe, 2 * n + 2)
                dve.scalar_tensor_tensor(out=proj[p % 2][:, LO, :], in0=bank[banks[0][p % 2]][:, :], scalar=1.0 / W_UP, in1=proj[p % 2][:, HI, :],
                                         op0=ALU.mult, op1=ALU.subtract).then_inc(s_pl, 1)
                if not early:
                    dve.wait_ge(s_dg, n - 1)
                dve.tensor_copy(sq[p % 2][:, HI, :], sq_f[p % 2][:, :]).then_inc(s_qh, 1)

            def score_max(n, p, banks):
                dve.wait_ge(s_dd, n + 1)
                dve.tensor_reduce(mx[:, p, :], heads(bank[banks[1][p % 2]][:, :]), AX.X, ALU.max).then_inc(s_mx, 1)

            def shifted_scores(n, p, dst, banks, query):
                dg = bank[banks[2]][:, 0:2 * TC]
                dve.wait_ge(s_dg, n + 1)
                if query:
                    dve.wait_ge(s_mx, n + 1)
                    dve.tensor_tensor(shift[p % 2][:, :], dg, mx[:, p, :], ALU.add).then_inc(s_sh, 1)
                else:
                    dve.tensor_copy(shift[p % 2][:, :], dg).then_inc(s_sh, 1)
                dve.wait_ge(s_sh, n + 1)
                dve.tensor_tensor(dst.rearrange("p t (a m) -> p (t a) m", m=M), heads(bank[banks[1][p % 2]][:, :]),
                                  shift[p % 2][:, :].unsqueeze(2).to_broadcast([P, 2 * TC, M]), ALU.subtract).then_inc(s_ss, 1)

            def batch_max(b):
                dve.wait_ge(s_mx, 8 * b + 8)
                dve.tensor_reduce(bmax[:, :], mx[:, :, :].rearrange("p a b -> p (a b)"), AX.X, ALU.max).then_inc(s_bm, 1)

            def reference_max(u):
                dve.wait_ge(s_bma, u + 1)
                dve.tensor_copy(ca_cur[:, :], modT[:, u, 2:4])
                dve.tensor_copy(mref[:, u:u + 1] if isinstance(u, int) else mref[:, bass.ds(u, 1)], bmax_all[:, :])
                dve.tensor_scalar(neg_ref[:, :], bmax_all[:, :], -1.0, KEY_SHIFT, ALU.mult, ALU.add).then_inc(s_nr, 1)

            def key_hi(u, q):
                dve.wait_ge(s_ke, 4 * u + q + 1)
                dve.tensor_copy(kexp[:, HI, 2 * q:2 * q + 2, :, :], scores[:, 2 * q:2 * q + 2, :, :]).then_inc(s_kh, 1)

            def sums_copy(u):
                dve.wait_ge(s_sum, u + 1)
                dve.tensor_copy(k_raw[:, u, :], bank[5][:, 0:PR])
                at = v_in[:, :, 0, u:u + 1] if isinstance(u, int) else v_in[:, :, 0, bass.ds(u, 1)]
                dve.tensor_tensor(at, bank[5][:, PR:PR + DC].unsqueeze(2), ca_cur[:, :].unsqueeze(2), ALU.mult).then_inc(s_sume, 1)

            def ctx_copy(u):
                dve.wait_ge(s_cx, u + 1)
                for q in range(2):
                    for g in range(2):
                        op = dve.tensor_copy(ctx_raw[g * DH:(g + 1) * DH, u, 4 * q:4 * q + 4, :],
                                             bank[(7, 5)[q]][g * DH:(g + 1) * DH, :].rearrange("p (a m) -> p a m", m=P)[:, :, g * M:(g + 1) * M])
                op.then_inc(s_cxe, 1)

            dve.memset(ones[:, :], 1.0)
            dve.memset(head_half[:, :], 0.0)
            dve.memset(lora_sign[:, :], W_UP).then_inc(c_dve, 1)
            dve.wait_ge(c_dve, 1)
            for g in range(2):
                dve.memset(head_half[g * DH:(g + 1) * DH, g:g + 1], 0.5 * DN * DN / SQ_UP)
            for g in range(3):
                op = dve.memset(lora_sign[g * TOPK * R:g * TOPK * R + R, :], -W_UP)
            op.then_inc(c_dve, 1)
            dve.wait_ge(p_exp, 1)
            dve.tensor_scalar(silu_b[:, :, :], silu_a[:, :, :], 1.0, None, ALU.add).then_inc(p_dve, 1)
            dve.wait_ge(p_dve, 1)
            dve.reciprocal(silu_a[:, :, :], silu_b[:, :, :]).then_inc(p_dve, 1)
            dve.wait_ge(p_dve, 2)
            dve.tensor_tensor(silu_c[:, :, :], c_s[:, :, :], silu_a[:, :, :], ALU.mult).then_inc(p_dve, 1)
            dve.wait_ge(p_mod, 1)
            mod_ps = bank[6][:, 0:12 * B].rearrange("p (k b) -> p b k", b=B)
            for k in (0, 3):
                dve.tensor_copy(modT[:, :, 2 * k:2 * k + 2], mod_ps[:, :, 2 * k:2 * k + 2])
                op = dve.tensor_scalar(modT[:, :, 2 * k + 2:2 * k + 4], mod_ps[:, :, 2 * k + 2:2 * k + 4], 1.0, None, ALU.add)
            op.then_inc(p_modT, 1)
            dve.wait_ge(p_modT, 1)
            dve.wait_ge(s_x, 16)
            ln_stats(0, x_in, modT[:, 0, 0:4], first=True)
            ln_apply(0, x_in, first=True)
            xhat_hi(0, 0)
            dve.tensor_copy(v_in[:, :, 1, :], modT[:, :, 0:2].rearrange("p b c -> p c b"))
            dve.wait_ge(p_mod, 2)
            dve.tensor_copy(gates_raw[:, :, :], bank[7][0:B, :].rearrange("p (a d) -> p a d", a=2)).then_inc(p_gate, 1)
            weight_lo(wk_f[:, :, :], wk_s, 0)
            dve.wait_ge(s_pre, 32)
            dve.tensor_scalar(pfeat_f[:, :], pfeat_f[:, :], DN, None, ALU.mult).then_inc(p_pf, 1)
            dve.wait_ge(p_pf, 1)
            dve.tensor_copy(pfeat[:, HI, :], pfeat_f[:, :]).then_inc(p_pf, 1)
            dve.wait_ge(p_pf, 2)
            dve.tensor_tensor(pfeat[:, LO, :], pfeat_f[:, :], pfeat[:, HI, :], ALU.subtract).then_inc(p_pf, 1)

            def lora_parts():
                dve.wait_ge(s_rest[3], 16 * 12)
                dve.wait_ge(c_dve, 2)
                dve.tensor_scalar(val_neg[:, :], val_s[:, :], -1.0 / W_UP, None, ALU.mult)
                dve.tensor_scalar(val_sign[:, :], val_s[:, :], 0.0, 2.0, ALU.is_ge, ALU.mult)
                dve.tensor_scalar(lora_first[:, :], lora_b_f[:, 0, :], W_UP, None, ALU.mult)
                dve.tensor_scalar(lora_delta[:, :], lora_b_f[:, 1, :], lora_sign[:, 0:1], None, ALU.mult)
                for g in range(3):
                    op = dve.tensor_scalar(lora_a[:, HI, :, g, :], lora_a_f[:, :, :], W_UP, None, ALU.mult)
                op.then_inc(p_lora, 1)
                dve.wait_ge(p_lora, 1)
                dve.scalar_tensor_tensor(out=val_abs[:, :], in0=val_s[:, :], scalar=1.0 / W_UP, in1=val_neg[:, :], op0=ALU.mult, op1=ALU.max)
                dve.tensor_scalar(val_sign[:, :], val_sign[:, :], -1.0, None, ALU.add)
                r = 2 * TOPK * R
                dve.scalar_tensor_tensor(out=lora_first[r:ZR, :], in0=lora_b_f[r:ZR, 0, :], scalar=W_UP, in1=lora_first[r:ZR, :], op0=ALU.mult, op1=ALU.subtract)
                dve.scalar_tensor_tensor(out=lora_delta[r:ZR, :], in0=lora_b_f[r:ZR, 1, :], scalar=lora_sign[r:ZR, 0:1], in1=lora_delta[r:ZR, :], op0=ALU.mult, op1=ALU.subtract)
                for g in range(3):
                    op = dve.scalar_tensor_tensor(out=lora_a[:, LO, :, g, :], in0=lora_a_f[:, :, :], scalar=W_UP, in1=lora_a[:, HI, :, g, :], op0=ALU.mult, op1=ALU.subtract)
                op.then_inc(p_lora, 1)
                dve.wait_ge(p_lora, 2)
                dve.tensor_tensor(val_pair[:, :], val_sign[:, 0:1], val_sign[:, 1:2], ALU.mult).then_inc(p_lora, 1)

            def keys(b, par, has_u, has_next):
                for s in range(PR + 1):
                    n = 8 * b + s
                    if has_u and s == 0:
                        reference_max(b - 1)
                    if s >= 1:
                        if has_u and s == 1:
                            dve.wait_ge(s_bm, b)
                        score_max(n - 1, s - 1, KEY_BANKS)
                    if s < PR:
                        projection_lo(n, s, KEY_BANKS, early=not has_u and s < 2)
                    else:
                        batch_max(b)
                    if s >= 2:
                        if has_u:
                            dve.wait_ge(s_kl, 4 * (b - 1) + (s - 2) // 2 + 1)
                        shifted_scores(n - 2, s - 2, scores[:, s - 2, :, :], KEY_BANKS, False)
                    if has_u and s < 4:
                        key_hi(b - 1, s)
                    if not has_u and s in (2, 4, 6):
                        src, w = ((wq_f, wq_s), (wi_f, wi_s), (wo2_f, wo2_s))[s // 2 - 1]
                        weight_lo(src, w, s // 2)
                    if has_next and s == 3:
                        dve.wait_ge(s_x, 16 * (b + 2))
                        ln_stats(b + 1, x_in, modT[:, b + 1, 0:4])
                    if has_next and s == 4:
                        dve.wait_ge(s_xl, b + 1)
                        ln_apply(b + 1, x_in)
                    if has_u and s == 5:
                        sums_copy(b - 1)
                shifted_scores(8 * b + 7, 7, scores[:, 7, :, :], KEY_BANKS, False)
                if has_u:
                    ctx_copy(b - 1)
                if has_next:
                    xhat_hi(b + 1, 1 - par)

            keys(0, 0, False, True)
            lora_parts()
            with dve.Fori(0, B // 2 - 1) as h:
                keys(2 * h + 1, 1, True, True)
                keys(2 * h + 2, 0, True, True)
            keys(LAST, 1, True, False)
            reference_max(LAST)
            for q in range(4):
                key_hi(LAST, q)
            dve.wait_ge(s_nr, B)
            dve.tensor_reduce(gmax[:, :], mref[:, :], AX.X, ALU.max, negate=True).then_inc(s_gm, 1)
            dve.wait_ge(p_gate, 1)
            dve.tensor_scalar(gates, gates_raw[:, :, :], -1.0, None, ALU.mult).then_inc(p_gate, 1)
            dve.wait_ge(p_gate, 2)
            dve.tensor_tensor(gate_abs, gates_raw[:, :, :], gates, ALU.max).then_inc(p_gate, 1)
            dve.wait_ge(p_gate, 3)
            dve.tensor_scalar(gates, gates_raw[:, :, :], 0.0, 2.0, ALU.is_ge, ALU.mult)
            dve.tensor_scalar(gate_abs, gate_abs, 0.25, None, ALU.max).then_inc(p_gate, 1)
            dve.wait_ge(p_gate, 4)
            dve.scalar_tensor_tensor(out=gates_raw[:, :, :], in0=gates, scalar=-1.0, in1=gate_abs, op0=ALU.add, op1=ALU.mult).then_inc(p_gate, 1)
            dve.wait_ge(p_gate, 5)
            dve.wait_ge(p_lora, 2)
            dve.tensor_scalar(gate_row[:, 0, :], gates_raw[:, 0, :], 1.0 / ATT_UP, None, ALU.mult)
            dve.tensor_scalar(gate_row[:, 2, :], gates_raw[:, 1, :], val_sign[0:B, 0:1], 1.0 / W_UP, ALU.mult, ALU.mult)
            sums_copy(LAST)
            dve.wait_ge(s_sc, 1)
            dve.tensor_scalar(scale_all[:, :], scale_all[:, :], 2.0 ** -KEY_UP, None, ALU.mult).then_inc(s_cur_a, 1)
            ctx_copy(LAST)
            dve.wait_ge(s_sv, 1)
            v_ps = bank[6][:, 0:2 * B * PR].rearrange("p (a s b) -> p s a b", s=2, b=B)
            dve.tensor_copy(v_raw[:, :, :].rearrange("p b a -> p a b"), v_ps[:, 0, :, :])
            dve.tensor_copy(sa_v[:, :, :], v_ps[:, 1, :, :]).then_inc(s_sve, 1)
            dve.wait_ge(p_r, 1)
            dve.tensor_tensor(gates[:, 0, :], bank[6][0:B, 0:D], bo_s[:, :], ALU.add).then_inc(p_gate, 1)
            dve.wait_ge(p_gate, 6)
            dve.tensor_tensor(gate_row[:, 1, :], gates[:, 0, :], gates_raw[:, 0, :], ALU.mult).then_inc(p_rows, 1)

            def current(i):
                dve.wait_ge(s_cur_a, 2 * i + 1)
                dve.tensor_copy(scale_cur[:, :], scale_all[:, i:i + 1] if isinstance(i, int) else scale_all[:, bass.ds(i, 1)])
                dve.tensor_scalar(v_cur[:, :], v_raw[:, i, :], EPS, None, ALU.mult)
                dve.tensor_copy(k_cur[:, :], k_raw[:, i, :]).then_inc(s_cur_a, 1)
                dve.wait_ge(s_cur_a, 2 * i + 2)
                dve.tensor_scalar(k_cur[:, :], k_cur[:, :], scale_cur[:, 0:1], T * EPS, ALU.mult, ALU.add).then_inc(s_cur_a, 1)
                dve.wait_ge(s_cur_a, 2 * i + 3)
                dve.reciprocal(k_rec[:, :], k_cur[:, :]).then_inc(s_cur, 1)
                for g in range(2):
                    rows = slice(g * DH, (g + 1) * DH)
                    op = dve.scalar_tensor_tensor(out=ctx_bd[rows, :, g * M:(g + 1) * M], in0=ctx_raw[rows, i, :, :], scalar=scale_cur[rows, 0:1],
                                                  in1=v_cur[rows, :].unsqueeze(2).to_broadcast([DH, PR, M]), op0=ALU.mult, op1=ALU.add)
                op.then_inc(s_bd, 1)

            def query_weights(i, p, first):
                dve.wait_ge(s_qe, 8 * i + p + 1)
                if p == 0:
                    dve.wait_ge(s_krc, 2 * i + 2)
                if not (first and p < 2):
                    dve.wait_ge(s_wl, 8 * i + p - 1)
                dve.scalar_tensor_tensor(out=qk[p % 2].rearrange("p (a b) -> p a b", b=P), in0=qexp[p % 2][:, :, :], scalar=EPS,
                                         in1=k_row[:, p * P:(p + 1) * P].unsqueeze(1).to_broadcast([P, TC, P]), op0=ALU.add, op1=ALU.mult).then_inc(s_qk, 1)
                dve.wait_ge(s_qk, 8 * i + p + 1)
                dve.tensor_reduce(qsum[p % 2][:, :], heads(qk[p % 2]), AX.X, ALU.add).then_inc(s_qs, 1)
                dve.wait_ge(s_qs, 16 * i + 2 * p + 1)
                dve.tensor_scalar(qsum[p % 2][:, :], qsum[p % 2][:, :], 1.0 / ATT_UP, None, ALU.mult).then_inc(s_qs, 1)
                dve.wait_ge(s_qs, 16 * i + 2 * p + 2)
                dve.reciprocal(qrec[p % 2][:, :], qsum[p % 2][:, :]).then_inc(s_qr, 1)

            def out_rows(i, k):
                rows = bank[(7, 5)[k]][:, :].rearrange("p (a d) -> p a d", d=D)
                if k == 0:
                    dve.wait_ge(s_rowg, 16 * i)
                    dve.wait_ge(s_out, 16 * i)
                dve.wait_ge(s_o, 2 * (i - 1) + k + 1)
                dve.tensor_tensor(rows, rows, row_g[:, :].unsqueeze(1).to_broadcast([P, 2, D]), ALU.mult).then_inc(s_og, 1)
                dve.wait_ge(s_og, 2 * (i - 1) + k + 1)
                dve.tensor_tensor(o_s[:, 2 * k:2 * k + 2, :], rows, x1[:, 2 * k:2 * k + 2, :], ALU.add).then_inc(s_of, 1)

            def y_rows(i, k, ffn):
                rows = bank[(3, 2)[k]][:, :].rearrange("p (a d) -> p a d", d=D)
                if k == 0:
                    if ffn:
                        dve.wait_ge(s_of, 2 * i)
                    dve.wait_ge(s_rowa, 16 * (i + 1))
                    dve.wait_ge(s_xr, i + 1)
                dve.wait_ge(s_y, 2 * i + k + 1)
                dve.tensor_tensor(rows, rows, row_a[:, 0, :].unsqueeze(1).to_broadcast([P, 2, D]), ALU.mult).then_inc(s_yg, 1)
                dve.wait_ge(s_yg, 2 * i + k + 1)
                dve.tensor_tensor(x1[:, 2 * k:2 * k + 2, :], rows, x_rest[:, 2 * k:2 * k + 2, :], ALU.add).then_inc(s_yr, 1)

            def batch(i, att, ffn, first=False, last=False):
                n0 = 8 * B + 8 * i
                for s in range(PR + 4):
                    if ffn and 4 <= s < 12:
                        f = s - 4
                        m = 8 * (i - 1) + f
                        dve.wait_ge(s_r1, m + 1)
                        if f >= 2:
                            dve.wait_ge(s_rs, m - 1)
                        dve.scalar_tensor_tensor(out=sum_f[f % 2], in0=bank[5 + f % 2][:, :], scalar=val_pair[:, 0:1], in1=relu0[f % 2],
                                                 op0=ALU.mult, op1=ALU.add).then_inc(s_rf, 1)
                    if att and 0 <= s - 2 < PR:
                        query_weights(i, s - 2, first)
                    if att and s < PR:
                        projection_lo(n0 + s, s, QUERY_BANKS, False)
                    if att and s == 0:
                        for p in range(PR):
                            dve.wait_ge(s_gh, 8 * i + 2 * (p // 2) + 2)
                            dve.scalar_tensor_tensor(out=g_s[:, LO, p, :], in0=bank[G_BANKS[p // 2]][:, (p % 2) * D:(p % 2 + 1) * D],
                                                     scalar=k_rec[:, p:p + 1], in1=g_s[:, HI, p, :], op0=ALU.mult, op1=ALU.subtract).then_inc(s_ge, 1)
                    if ffn and s == 2:
                        r = TOPK * R
                        dve.wait_ge(s_zh, i)
                        dve.scalar_tensor_tensor(out=z_s[r:2 * r, :], in0=bank[7][r:2 * r, :], scalar=1.0 / W_UP, in1=z_s[r:2 * r, :],
                                                 op0=ALU.mult, op1=ALU.subtract).then_inc(s_ze, 1)
                    if att and 0 <= s - 1 < PR:
                        p = s - 1
                        score_max(n0 + p, p, QUERY_BANKS)
                        if p >= 2:
                            dve.wait_ge(s_qk, 8 * i + p - 1)
                        shifted_scores(n0 + p, p, qexp[p % 2][:, :, :], QUERY_BANKS, True)
                if ffn:
                    out_rows(i, 0)
                    out_rows(i, 1)
                if att:
                    if not last:
                        current(i + 1)
                    y_rows(i, 0, ffn)
                    y_rows(i, 1, ffn)
                    dve.wait_ge(s_yr, 2 * i + 2)
                    ln_stats(B + i, x1, modT[:, i, 6:10])
                    ln_apply(B + i, x1)

            current(0)
            batch(0, True, False, first=True)
            with dve.Fori(1, LAST) as i:
                batch(i, True, True)
            batch(LAST, True, True, last=True)
            batch(B, False, True)


_INS = ["L0_attn_x", "L0_attn_Wq", "L0_attn_Wk", "L0_attn_Wv", "L0_attn_Wo", "L0_attn_bo"]


def kernel(**inputs):
    import numpy as np
    import concourse.bacc as bacc
    from concourse.bass_utils import run_bass_kernel_spmd

    f = "L0_ffn_"
    arrays = {name: np.asarray(inputs[name]) for name in _INS}
    arrays["P_t"] = np.asarray(inputs["L0_attn_P"]).T
    arrays["wi_t"] = np.asarray(inputs[f + "wi_w"]).T
    arrays["wo_t"] = np.asarray(inputs[f + "wo_w"]).T
    arrays["lora_a_t"] = np.asarray(inputs[f + "lora_As"]).transpose(0, 2, 1)
    arrays["lora_b_t"] = np.asarray(inputs[f + "lora_Bs"]).transpose(0, 2, 1)
    arrays["index"] = np.asarray(inputs[f + "top_k_indices"])
    arrays["value"] = np.asarray(inputs[f + "top_k_values"])
    arrays["c_t"] = np.asarray(inputs["L0_c"]).T
    arrays["wmod"] = np.asarray(inputs["L0_wmod"])
    arrays = {"in_" + k: np.ascontiguousarray(a) for k, a in arrays.items()}
    nc = bacc.Bacc("TRN2", target_bir_lowering=False, num_devices=1)
    args = [nc.dram_tensor(k, a.shape, mybir.dt.from_np(a.dtype), kind="ExternalInput").ap() for k, a in arrays.items()]
    args.append(nc.dram_tensor("out_x", (B, T, D), F32, kind="ExternalOutput").ap())
    build(nc, *args)
    return run_bass_kernel_spmd(nc, [arrays], core_ids=[0]).results[0]["out_x"]
```

```python
import math
from contextlib import ExitStack

import concourse.bass as bass
from concourse import mybir

F32 = mybir.dt.float32
F16 = mybir.dt.float16
I32 = mybir.dt.int32
ALU = mybir.AluOpType
ACT = mybir.ActivationFunctionType
AX = mybir.AxisListType
RMAX = bass.bass_isa.ReduceOp.max

B, T, D = 8, 512, 256
H, DH, M = 16, 64, 64
F, R, EXP, TOPK = 1024, 16, 8, 2
P = 128
DC = D // P
TC = T // P
PR = H * DH // P
FC = F // P
EPS = 1e-4
LN_EPS = 1e-5
DN = float(DH) ** -0.25
LAST = B - 1
W_UP = 256.0
SQ_UP = 1.0 / 256
KEY_UP = 14
KEY_SHIFT = KEY_UP * math.log(2.0)
ATT_UP = 1024.0
HI, LO = 0, 1
PARTS = ((HI, HI), (HI, LO), (LO, HI))
ZR = 3 * TOPK * R
KEY_BANKS = ((0, 1), (2, 3), 4)
QUERY_BANKS = ((0, 4), (1, 1), 2)
K_BANKS = Y_BANKS = H2_BANKS = (6, 5)
G_BANKS = (2, 6, 5, 6)
FFN_BANKS = (5, 7, 6)
Z_BANK = 2
OUT_BANK = 7
END_BANKS = (0, 1)
KEY_STEPS = (1, 2, 4, 5)
UNITS = {5: (0, 1, 2), 6: (3, 4, 5), 7: (6, 7)}


def build(nc, x, wq, wk, wv, wo, bo, pT, wiT, woT, laT, lbT, idx, val, cT, wmod, out):
    with ExitStack() as ctx:
        def sb(name, shape, dt=F32):
            return ctx.enter_context(nc.sbuf_tensor(name, shape, dt))

        def sem(name):
            return ctx.enter_context(nc.semaphore(name))

        wq_s = sb("wq_s", [P, 2, DC, H * DH], F16)
        wk_s = sb("wk_s", [P, 2, DC, H * DH], F16)
        wi_s = sb("wi_s", [P, 2, DC, F], F16)
        wo2_s = sb("wo2_s", [P, 2, FC, D], F16)
        wv_s = sb("wv_s", [P, DC, H * DH])
        wo_s = sb("wo_s", [P, PR, D])
        lora_a_f = sb("lora_a_f", [P, DC, TOPK * R])
        lora_a = sb("lora_a", [P, 2, DC, 3, TOPK * R], F16)
        lora_first = sb("lora_first", [ZR, F], F16)
        lora_delta = sb("lora_delta", [ZR, F], F16)
        lora_sign = sb("lora_sign", [ZR, 1])
        pfeat_f = sb("pfeat_f", [P, P])
        pfeat = sb("pfeat", [P, 2, P], F16)
        ident = sb("ident", [P, P])
        ident16 = sb("ident16", [P, P], F16)
        ones = sb("ones", [P, 1], F16)
        head_half = sb("head_half", [P, 2], F16)
        neg_half = sb("neg_half", [P, TC])
        idx_s = sb("idx_s", [1, TOPK], I32)
        val_s = sb("val_s", [P, TOPK])
        val_neg = sb("val_neg", [P, TOPK])
        val_abs = sb("val_abs", [P, TOPK])
        val_sign = sb("val_sign", [P, TOPK])
        val_pair = sb("val_pair", [P, 1])
        c_s = sb("c_s", [P, DC, B])
        silu_a = sb("silu_a", [P, DC, B])
        silu_b = sb("silu_b", [P, DC, B])
        silu_c = sb("silu_c", [P, DC, B])
        modT = sb("modT", [P, B, 12])
        sa_v = sb("sa_v", [P, PR, B])

        hT = sb("hT", [P, B, 2, DC, T], F16)
        ctx_raw = sb("ctx_raw", [P, B, PR, M])
        k_raw = sb("k_raw", [P, B, PR])
        v_in = sb("v_in", [P, DC, 2, B])
        v_raw = sb("v_raw", [P, B, PR])
        mref = sb("mref", [P, B])
        scale_all = sb("scale_all", [P, B])
        gmax = sb("gmax", [P, 1])

        x_in = sb("x_in", [P, TC, D])
        xhat = sb("xhat", [P, TC, D])
        xhat2 = [sb(f"xhat2{i}", [P, 2, TC, D], F16) for i in range(2)]
        stats = sb("stats", [P, TC, 6])
        meanvar = sb("meanvar", [P, TC, 2])
        var_eps = sb("var_eps", [P, TC])
        rstd = sb("rstd", [P, TC])
        mod_cur = sb("mod_cur", [P, 4])
        ca_cur = sb("ca_cur", [P, DC])
        h_f = sb("h_f", [P, DC, T])
        proj = [sb(f"proj{i}", [P, 2, T], F16) for i in range(2)]
        sq_f = [sb(f"sq_f{i}", [P, T]) for i in range(2)]
        sq = [sb(f"sq{i}", [P, 2, T], F16) for i in range(2)]
        mx = sb("mx", [P, PR, 2 * TC])
        shift = [sb(f"shift{i}", [P, 2 * TC]) for i in range(2)]
        bmax = sb("bmax", [P, 1])
        bmax_all = sb("bmax_all", [P, 1])
        pool_pad = sb("pool_pad", [P, 1])
        neg_ref = sb("neg_ref", [P, 1])
        scores = sb("scores", [P, PR, TC, P])
        kexp = sb("kexp", [P, 2, PR, TC, P], F16)
        featT = sb("featT", [P, DC, H * M])
        attw = scores[:, :, :, :].rearrange("p a b c -> p (a b c)").bitcast(F16).rearrange("p (s a t) -> p s a t", s=2, a=PR)
        relu_sum = kexp[:, :, :, :, :].rearrange("p s a b c -> p s a (b c)")
        g_s = featT[:, :, :].rearrange("p a b -> p (a b)").bitcast(F16).rearrange("p (s a d) -> p s a d", s=2, d=D)
        scale_cur = sb("scale_cur", [P, 1])
        v_cur = sb("v_cur", [P, PR])
        k_cur = sb("k_cur", [P, PR])
        k_rec = sb("k_rec", [P, PR])
        ctx_bd = sb("ctx_bd", [P, PR, P])
        wv_flat = wv_s[:, :, :].rearrange("p c n -> p (c n)")
        qexp = [sb(f"qexp{i}", [P, TC, P]) for i in range(2)]
        work = sb("work", [P, 4, T])
        qk = [work[:, i, :] for i in range(2)]
        k_row = work[:, 2:4, :].rearrange("p a t -> p (a t)")
        qsum = [sb(f"qsum{i}", [P, 2 * TC]) for i in range(2)]
        qrec = [sb(f"qrec{i}", [P, 2 * TC]) for i in range(2)]
        w2 = [sb(f"w2{i}", [P, 2, T], F16) for i in range(2)]
        wk_flat = wk_s[:, :, :, :].rearrange("p s c n -> p (s c n)").bitcast(F32)
        relu0 = [wk_flat[:, T * i:T * (i + 1)] for i in range(2)]
        sum_f = [wk_flat[:, T * (2 + i):T * (3 + i)] for i in range(2)]
        h2T = xhat2[0][:, :, :, :].rearrange("p s a b -> p s (a b)").rearrange("p s (c t) -> p s c t", c=DC)
        z_s = sb("z_s", [ZR, T], F16)
        x_rest = x_in
        x1 = wv_flat[:, 0:2 * T].rearrange("p (a b) -> p a b", b=D)
        row_a = sb("row_a", [P, 2, D])
        row_g = sb("row_g", [P, D])
        o_s = xhat2[1][:, :, :, :].rearrange("p s a b -> p (s a b)").bitcast(F32).rearrange("p (a b) -> p a b", b=D)
        wmod_s = scores[:, :, :, :].rearrange("p a b c -> p (a b c)")[:, 0:DC * 6 * D].rearrange("p (a b) -> p a b", a=DC)
        wk_f = featT
        e_flat = kexp[:, :, :, :, :].rearrange("p s a b c -> p (s a b c)").bitcast(F32)
        wq_f = e_flat[:, 0:DC * H * DH].rearrange("p (c n) -> p c n", c=DC)
        wi_f = e_flat[:, DC * H * DH:2 * DC * H * DH].rearrange("p (c n) -> p c n", c=DC)
        wo2_f = featT[:, :, :].rearrange("p a t -> p (a t)").rearrange("p (c n) -> p c n", c=FC)
        lora_b_f = work[0:ZR, :, :].rearrange("p a t -> p (a t)").rearrange("p (k f) -> p k f", k=2)
        gates_raw = row_a[0:B, :, :]
        bo_s = row_g[0:B, :]
        gate_row = xhat[0:B, 0:3, :]
        gate_sum = xhat[0:B, 3, :]
        gates = work[0:B, 0, :].rearrange("p (a d) -> p a d", d=D)
        gate_abs = work[0:B, 1, :].rearrange("p (a d) -> p a d", d=D)
        rows_dram = nc.dram_tensor("rows_scratch", (B, 3, D), F32, kind="Internal").ap()

        bank = [ctx.enter_context(nc.psum_tensor(f"bank{i}", [P, 512], F32)) for i in range(8)]
        tr16 = bank[3][:, :].bitcast(F16).rearrange("p (s t) -> p s t", s=2)

        s_small = sem("small_loaded")
        s_wk = sem("wk_loaded")
        s_wv = sem("wv_loaded")
        s_rest = [sem(f"{k}_loaded") for k in ("wq", "wi", "wo2", "lora")]
        s_pre = sem("features_loaded")
        s_idx = sem("index_loaded")
        s_x = sem("x_loaded")
        s_rowa = sem("row_a_loaded")
        s_rowg = sem("row_g_loaded")
        s_out = sem("out_stored")
        c_pool = sem("pool_constants_ready")
        c_dve = sem("dve_constants_ready")
        c_id0 = sem("ident_zeroed")
        p_exp = sem("silu_exp")
        p_dve = sem("silu_steps")
        p_mod = sem("mod_mm")
        p_modT = sem("modT_ready")
        p_r = sem("row_mm")
        p_gate = sem("gate_steps")
        p_rows = sem("rows_ready")
        p_pf = sem("pfeat_steps")
        p_lora = sem("lora_steps")
        w_hi = sem("weight_hi")
        w_up = sem("weight_scaled")
        w_lo = sem("weight_lo")
        s_stat = sem("stats_done")
        s_agg = sem("aggregated")
        s_var = sem("variance_ready")
        s_rstd = sem("rstd_ready")
        s_xhat = sem("xhat_ready")
        s_xh = sem("xhat_hi")
        s_xl = sem("xhat_lo")
        s_modc = sem("mod_current")
        s_tr = sem("hT_mm")
        s_hh = sem("hT_hi")
        s_hT = sem("hT_ready")
        s_pm = sem("proj_mm")
        s_pe = sem("proj_read_by_act")
        s_qh = sem("square_hi")
        s_pl = sem("proj_lo")
        s_sl = sem("square_lo")
        s_dd = sem("scores_mm")
        s_dg = sem("diag_mm")
        s_mx = sem("max_ready")
        s_sh = sem("shift_ready")
        s_ss = sem("scores_shifted")
        s_bm = sem("batch_max")
        s_bma = sem("batch_max_all")
        s_nr = sem("neg_ref_ready")
        s_ke = sem("key_exp")
        s_kh = sem("key_exp_hi")
        s_kl0 = sem("key_exp_lo_first")
        s_kl = sem("key_exp_lo")
        s_sum = sem("sums_mm")
        s_sume = sem("sums_ready")
        s_ft = sem("feat_mm")
        s_fte = sem("feat_ready")
        s_cx = sem("ctx_mm")
        s_cxe = sem("ctx_ready")
        s_sv = sem("v_raw_mm")
        s_sve = sem("v_raw_ready")
        s_gm = sem("gmax_ready")
        s_sc = sem("scale_ready")
        s_cur = sem("current_ready")
        s_cur_a = sem("current_steps")
        s_vc = sem("v_current_ready")
        s_bd = sem("ctx_bd_ready")
        s_kr = sem("k_row_mm")
        s_krc = sem("k_row_ready")
        s_g = sem("g_mm")
        s_gh = sem("g_hi")
        s_ge = sem("g_ready")
        s_qe = sem("query_exp")
        s_qk = sem("qk_ready")
        s_qs = sem("query_sums")
        s_qr = sem("query_rec")
        s_wf = sem("weights_float")
        s_wh = sem("weights_hi")
        s_wl = sem("weights_lo")
        s_wt = sem("weights_tr")
        s_w = sem("attw_ready")
        s_xr = sem("x_rest_ready")
        s_y = sem("y_mm")
        s_yg = sem("y_gated")
        s_yr = sem("y_read")
        s_oc = sem("x1_copied")
        s_z = sem("z_mm")
        s_zh = sem("z_hi")
        s_ze = sem("z_ready")
        s_f0 = sem("ffn_first_mm")
        s_r0 = sem("relu0_ready")
        s_f1 = sem("ffn_second_mm")
        s_r1 = sem("relu1_ready")
        s_rf = sem("relu_sum_float")
        s_rh = sem("relu_sum_hi")
        s_rs = sem("relu_sum_ready")
        s_o = sem("out_mm")
        s_og = sem("out_gated")
        s_of = sem("out_ready")

        block = ctx.enter_context(nc.Block())
        xv = x.rearrange("b (p t) d -> b p t d", t=TC)
        ov = out.rearrange("b (p t) d -> b p t d", t=TC)

        def heads(ap):
            return ap.rearrange("p (a m) -> p a m", m=M)

        def live(s, lag, att, wrap):
            return att if s >= lag else wrap

        def ffn_units(s, wrap, late):
            if s == 0:
                return [[(2, 8), (2, 9)] if late else [], [], []]
            at = [[(1, u)] for u in UNITS.get(s, ())] if wrap else []
            return at + [[]] * (3 - len(at))

        def finished(s):
            return () if s == 2 else (3, 2) if s == 3 else (2,)

        def late_weight(k):
            part = slice(k % 2, k % 2 + 1) if k < 4 else slice(FC // 2 * (k % 2), FC // 2 * (k % 2 + 1))
            src, w = ((wq_f, wq_s), (wi_f, wi_s), (wo2_f, wo2_s))[k // 2]
            return src[:, part, :], w[:, HI, part, :], w[:, LO, part, :], s_rest[k // 2]

        @block.sync
        def _(sp):
            sp.dma_start(x_in[:, :, :], xv[0]).then_inc(s_x, 16)
            sp.dma_start(idx_s[:, :], idx.rearrange("(a n) -> a n", a=1)).then_inc(s_idx, 16)
            sp.dma_start(c_s[:, :, :], cT.rearrange("(c p) b -> p c b", p=P)).then_inc(s_small, 16)
            sp.dma_start(wmod_s, wmod.rearrange("(c p) n -> p c n", p=P)).then_inc(s_small, 16)
            sp.dma_start(wk_f[:, :, :], wk.rearrange("(c p) n -> p c n", p=P)).then_inc(s_wk, 16)
            sp.wait_ge(c_pool, 1)
            sp.dma_start(pfeat_f[0:DH, 0:M], pT).then_inc(s_pre, 16)
            sp.dma_start(pfeat_f[DH:P, M:P], pT).then_inc(s_pre, 16)
            sp.dma_start(wq_f, wq.rearrange("(c p) n -> p c n", p=P)).then_inc(s_rest[0], 16)
            sp.dma_start(wi_f, wiT.rearrange("(c p) n -> p c n", p=P)).then_inc(s_rest[1], 16)
            sp.wait_ge(w_lo, 1)
            sp.dma_start(wo2_f, woT.rearrange("(c p) n -> p c n", p=P)).then_inc(s_rest[2], 16)
            sp.wait_ge(s_idx, 16)
            expert = [sp.value_load(idx_s[0:1, k:k + 1], min_val=0, max_val=EXP - 1) for k in range(TOPK)]
            lb = [lbT[bass.ds(e, 1)].rearrange("o r f -> (o r) f") for e in expert]
            for g in range(3):
                r = g * TOPK * R
                sp.dma_start(lora_b_f[r:r + R, 0, :], lb[0]).then_inc(s_rest[3], 16)
                for k in range(TOPK):
                    sp.dma_start(lora_b_f[r + k * R:r + (k + 1) * R, 1, :], lb[k]).then_inc(s_rest[3], 16)
            for k in range(TOPK):
                sp.dma_start(lora_a_f[:, :, k * R:(k + 1) * R],
                             laT[bass.ds(expert[k], 1)].rearrange("o (c p) r -> p (o c) r", p=P)).then_inc(s_rest[3], 16)
            sp.dma_start(val_s[:, :], val.rearrange("(a n) -> a n", a=1).to_broadcast([P, TOPK])).then_inc(s_rest[3], 16)
            sp.dma_start(wv_s[:, :, :], wv.rearrange("(c p) n -> p c n", p=P)).then_inc(s_wv, 16)
            sp.dma_start(wo_s[:, :, :], wo.rearrange("(c p) n -> p c n", p=P)).then_inc(s_wv, 16)
            sp.dma_start(bo_s[:, :], bo.rearrange("(a n) -> a n", a=1).to_broadcast([B, D])).then_inc(s_wv, 16)
            with sp.Fori(1, B) as b:
                sp.wait_ge(s_xhat, b)
                sp.dma_start(x_in[:, :, :], xv[b]).then_inc(s_x, 16)
            sp.wait_ge(p_rows, 1)
            sp.dma_start(rows_dram, gate_row).then_inc(s_out, 16)
            sp.wait_ge(s_out, 16)

            def load_att(i, first=False):
                sp.wait_ge(s_xhat, B) if first else sp.wait_ge(s_yr, 2 * i)
                sp.dma_start(x_in[:, :, :], xv[i]).then_inc(s_x, 16)
                sp.dma_start(row_a[:, :, :].rearrange("p a d -> p (a d)"),
                             rows_dram[bass.ds(i, 1), 0:2, :].rearrange("o a d -> o (a d)").to_broadcast([P, 2 * D])).then_inc(s_rowa, 16)

            def load_gate(j, first=False):
                if not first:
                    sp.wait_ge(s_of, 2 * j)
                sp.dma_start(row_g[:, :], rows_dram[bass.ds(j, 1), 2, :].to_broadcast([P, D])).then_inc(s_rowg, 16)

            def store(j):
                sp.wait_ge(s_of, 2 * j + 2)
                sp.dma_start(ov[j], o_s).then_inc(s_out, 16)

            load_att(0, first=True)
            load_gate(0, first=True)
            load_att(1)
            with sp.Fori(2, B) as i:
                load_att(i)
                store(i - 2)
                load_gate(i - 1)
            store(B - 2)
            load_gate(B - 1)
            store(B - 1)
            sp.wait_ge(s_out, 16 * (B + 1))

        @block.gpsimd
        def _(pool):
            pool.memset(pfeat_f[:, :], 0.0)
            pool.memset(lora_b_f, 0.0).then_inc(c_pool, 1)
            pool.memset(neg_half[:, :], -0.5)
            pool.memset(ctx_bd[:, :, :], 0.0)
            pool.memset(ident[:, :], 0.0).then_inc(c_id0, 1)
            pool.wait_ge(c_id0, 1)
            pool.affine_select(out=ident[:, :], in_=ident[:, :], compare_op=ALU.not_equal, fill=1.0,
                               base=0, pattern=[[-1, P]], channel_multiplier=1).then_inc(c_pool, 1)
            pool.wait_ge(c_pool, 2)
            pool.tensor_copy(ident16[:, :], ident[:, :]).then_inc(c_pool, 1)

            def lower(out, value, hi):
                return pool.tensor_tensor(out, value, hi, ALU.subtract)

            def ln_power(n):
                pool.wait_ge(s_var, n + 1)
                pool.tensor_tensor(rstd[:, :], var_eps[:, :], neg_half[:, :], ALU.pow).then_inc(s_rstd, 1)

            def h_lower(n, c, dst):
                pool.wait_ge(s_hh, 4 * n + 2 * c + 2)
                lower(dst[LO][c], h_f[:, c, :], dst[HI][c]).then_inc(s_hT, 1)

            def x_lower(n, par):
                pool.wait_ge(s_xh, n + 1)
                lower(xhat2[par][:, LO, :, :], xhat[:, :, :], xhat2[par][:, HI, :, :]).then_inc(s_xl, 1)

            def square_lower(n, p):
                pool.wait_ge(s_qh, n + 1)
                lower(sq[p % 2][:, LO, :], sq_f[p % 2][:, :], sq[p % 2][:, HI, :]).then_inc(s_sl, 1)

            def key_lower(u, q):
                pool.wait_ge(s_kh, 4 * u + q + 1)
                lower(kexp[:, LO, 2 * q:2 * q + 2, :, :], scores[:, 2 * q:2 * q + 2, :, :], kexp[:, HI, 2 * q:2 * q + 2, :, :]).then_inc(s_kl if q else s_kl0, 1)

            def batch_max(b):
                pool.wait_ge(s_bm, b + 1)
                pool.tensor_tensor(pool_pad[:, :], neg_half[:, 0:1], neg_half[:, 0:1], ALU.mult)
                pool.partition_all_reduce(bmax_all[:, :], bmax[:, :], P, RMAX).then_inc(s_bma, 1)

            def hT_of(b):
                return [[hT[:, b, s, c, :] for c in range(DC)] for s in range(2)]

            def keys(b, par, has_u, has_next):
                for s in range(PR):
                    if has_u and s == 0:
                        batch_max(b - 1)
                    square_lower(8 * b + s, s)
                    if has_u and s in KEY_STEPS[1:]:
                        key_lower(b - 1, KEY_STEPS.index(s))
                    if not has_u and 1 <= s < 7:
                        src, hi, lo, _ = late_weight(s - 1)
                        pool.wait_ge(w_hi, s + 1)
                        lower(lo, src, hi).then_inc(w_lo, 1)
                    if has_next and s == 3:
                        ln_power(b + 1)
                    if has_next and s in (6, 7):
                        h_lower(b + 1, s - 6, hT_of(b + 1))
                if has_next:
                    x_lower(b + 1, 1 - par)

            ln_power(0)
            h_lower(0, 0, hT_of(0))
            h_lower(0, 1, hT_of(0))
            x_lower(0, 0)
            keys(0, 0, False, True)
            with pool.Fori(0, B // 2 - 1) as h:
                keys(2 * h + 1, 1, True, True)
                keys(2 * h + 2, 0, True, True)
            keys(LAST, 1, True, False)
            batch_max(LAST)

            h2 = [[h2T[:, s, c, :] for c in range(DC)] for s in range(2)]

            def weight_float(m, p):
                pool.wait_ge(s_qr, m + 1)
                pool.tensor_tensor(heads(qk[p % 2]), heads(qk[p % 2]), qrec[p % 2][:, :].unsqueeze(2).to_broadcast([P, 2 * TC, M]),
                                   ALU.mult).then_inc(s_wf, 1)

            def weight_lower(m, p):
                pool.wait_ge(s_wh, m + 1)
                lower(w2[p % 2][:, LO, :], qk[p % 2], w2[p % 2][:, HI, :]).then_inc(s_wl, 1)

            def unit(j, u):
                f = u - 2
                if 0 <= f < FC:
                    pool.wait_ge(s_rh, 8 * j + f + 1)
                    lower(relu_sum[:, LO, f, :], sum_f[f % 2], relu_sum[:, HI, f, :]).then_inc(s_rs, 1)

            def x_plus_row(i, k):
                pool.wait_ge(s_x, 16 * (B + i))
                pool.wait_ge(s_rowa, 16 * i)
                for j in (2 * k, 2 * k + 1):
                    op = pool.tensor_tensor(x_rest[:, j, :], x_in[:, j, :], row_a[:, 1, :], ALU.add)
                op.then_inc(s_xr, 1)

            def iteration(i, att=True, wrap=True, late=True):
                for s in range(PR):
                    m = 8 * i + s
                    units = ffn_units(s, wrap, late)
                    if live(s, 2, att, wrap) and s > 0:
                        weight_lower(m - 2, (s - 2) % PR)
                    if wrap and s == 1:
                        x_plus_row(i, 0)
                    for back, u in units[0]:
                        unit(i - back, u)
                    if live(s, 2, att, wrap) and s == 0:
                        weight_lower(m - 2, (s - 2) % PR)
                    if wrap and s == 3:
                        ln_power(B + i - 1)
                    if wrap and s == 4:
                        for c in range(DC if att else 1):
                            h_lower(B + i - 1, c, h2)
                    if att:
                        square_lower(8 * B + m, s)
                    for back, u in units[1]:
                        unit(i - back, u)
                    if live(s, 1, att, wrap):
                        weight_float(m - 1, (s - 1) % PR)
                    for back, u in units[2]:
                        unit(i - back, u)
                    for q in ({0: (0,), 1: (1, 2), 2: (3,)}.get(s, ()) if not wrap else ()):
                        key_lower(LAST, q)
                    if wrap and s == 1:
                        x_plus_row(i, 1)

            iteration(0, wrap=False, late=False)
            iteration(1, late=False)
            with pool.Fori(2, B) as i:
                iteration(i)
            iteration(B, att=False)
            for u in (8, 9):
                unit(B - 1, u)

        @block.tensor
        def _(pe):
            def transpose_x(c, dst):
                for j in range(TC):
                    op = pe.transpose(dst[:, j * P:(j + 1) * P], xhat[:, j, c * P:(c + 1) * P], ident[:, :])
                op.then_inc(s_tr, 1)

            def project(n, p, b, w, banks):
                for a in range(3):
                    st, mv = PARTS[a]
                    for c in range(DC):
                        op = pe.matmul(bank[banks[0][p % 2]][:, :], w[:, st, c, p * P:(p + 1) * P], hT[:, b, mv, c, :],
                                       start=(a == 0 and c == 0), stop=(a == 2 and c == DC - 1))
                op.then_inc(s_pm, 1)

            def score(n, p, banks):
                pe.wait_ge(s_pl, n + 1)
                for j in range(TC):
                    for a in range(3):
                        st, mv = PARTS[a]
                        op = pe.matmul(bank[banks[1][p % 2]][:, j * P:(j + 1) * P], proj[p % 2][:, st, j * P:(j + 1) * P], pfeat[:, mv, :],
                                       start=(a == 0), stop=(a == 2))
                op.then_inc(s_dd, 1)

            def diag(n, p, banks, first):
                pe.wait_ge(s_sl, n + 1)
                if not first:
                    pe.wait_ge(s_sh, n)
                for j in range(TC):
                    for a in (HI, LO):
                        op = pe.matmul(bank[banks[2]][:, 2 * j:2 * j + 2], sq[p % 2][:, a, j * P:(j + 1) * P], head_half[:, :], start=(a == HI), stop=(a == LO))
                op.then_inc(s_dg, 1)

            def features(u, par, k):
                half, c = k // 2, k % 2
                if c == 0:
                    if half == 0:
                        pe.wait_ge(s_kl0, u + 1)
                    pe.wait_ge(s_kl, 3 * u + 2 * half + 1)
                if k == 0:
                    pe.wait_ge(s_xl, u + 1)
                if k > 0:
                    pe.wait_ge(s_fte, 4 * u + k)
                for a in range(3):
                    st, mv = PARTS[a]
                    for j in range(TC):
                        op = pe.matmul(bank[7][:, :], xhat2[par][:, st, j, c * P:(c + 1) * P], kexp[:, mv, 4 * half:4 * half + 4, j, :],
                                       start=(a == 0 and j == 0), stop=(a == 2 and j == TC - 1))
                op.then_inc(s_ft, 1)

            def sums(u, par):
                pe.wait_ge(s_kl, 3 * u + 3)
                for p in range(PR):
                    for a in (HI, LO):
                        for j in range(TC):
                            pe.matmul(bank[5][:, p:p + 1], kexp[:, a, p, j, :], ones[:, :], start=(a == HI and j == 0), stop=(a == LO and j == TC - 1))
                for c in range(DC):
                    for a in (HI, LO):
                        for j in range(TC):
                            op = pe.matmul(bank[5][:, PR + c:PR + c + 1], xhat2[par][:, a, j, c * P:(c + 1) * P], ones[:, :],
                                           start=(a == HI and j == 0), stop=(a == LO and j == TC - 1))
                op.then_inc(s_sum, 1)

            def contexts(u):
                pe.wait_ge(s_fte, 4 * u + 4)
                for p in range(PR):
                    if p == 4:
                        pe.wait_ge(s_sume, u + 1)
                    for c in range(DC):
                        op = pe.matmul(bank[(7, 5)[p // 4]][:, p % 4 * P:(p % 4 + 1) * P], wv_s[:, c, p * P:(p + 1) * P],
                                       featT[:, c, p * P:(p + 1) * P], start=(c == 0), stop=(c == DC - 1))
                op.then_inc(s_cx, 1)

            pe.wait_ge(c_pool, 2)
            pe.wait_ge(s_xhat, 1)
            transpose_x(0, bank[6])
            transpose_x(1, bank[7])
            pe.wait_ge(p_dve, 3)
            pe.wait_ge(s_small, 32)
            for ch in (0, 1, 2, 3, 6, 7, 8, 9):
                for c in range(DC):
                    op = pe.matmul(bank[5 if ch < 4 else 4][:, ch * B:(ch + 1) * B], wmod_s[:, c, ch * P:(ch + 1) * P], silu_c[:, c, :], start=(c == 0), stop=(c == DC - 1))
                if ch in (3, 9):
                    op.then_inc(p_mod, 1)
            for g, col in enumerate((2 * D, 5 * D)):
                for c in range(DC):
                    op = pe.matmul(bank[3][0:B, g * D:(g + 1) * D], silu_c[:, c, :], wmod_s[:, c, col:col + D], start=(c == 0), stop=(c == DC - 1))
            op.then_inc(p_mod, 1)
            pe.wait_ge(p_gate, 1)
            pe.wait_ge(w_lo, 1)
            pe.wait_ge(p_pf, 3)
            pe.wait_ge(c_dve, 2)

            def keys(b, par, has_u, has_next):
                pe.wait_ge(s_hT, 2 * (b + 1))
                for s in range(PR):
                    n = 8 * b + s
                    if has_u or s >= 2:
                        pe.wait_ge(s_pl, n - 1)
                    project(n, s, b, wk_s, KEY_BANKS)
                    if has_u or s >= 2:
                        diag(n - 2, (s - 2) % PR, KEY_BANKS, first=not has_u and s == 2)
                    if has_u or s >= 1:
                        if has_u or s >= 3:
                            pe.wait_ge(s_ss, n - 2)
                        score(n - 1, (s - 1) % PR, KEY_BANKS)
                    if has_u:
                        u = b - 1
                        if s >= 4:
                            features(u, 1 - par, s - 4)
                        if s == 7:
                            sums(u, 1 - par)
                            contexts(u)
                    if has_next and s == 5:
                        pe.wait_ge(s_xhat, b + 2)
                        transpose_x(0, bank[6])
                    if has_next and s == 6:
                        pe.wait_ge(s_hh, 4 * (b + 1) + 2)
                        transpose_x(1, bank[6])

            keys(0, 0, False, True)
            pe.wait_ge(s_wv, 48)
            with pe.Fori(0, B // 2 - 1) as h:
                keys(2 * h + 1, 1, True, True)
                keys(2 * h + 2, 0, True, True)
            keys(LAST, 1, True, False)
            pe.wait_ge(s_ss, 8 * B - 2)
            score(8 * B - 1, PR - 1, KEY_BANKS)
            diag(8 * B - 2, PR - 2, KEY_BANKS, False)
            diag(8 * B - 1, PR - 1, KEY_BANKS, False)

            def value_sums():
                pe.wait_ge(s_sume, B)
                for p in range(PR):
                    for c in range(DC):
                        op = pe.matmul(bank[6][:, p * 2 * B:(p + 1) * 2 * B], wv_s[:, c, p * P:(p + 1) * P], v_in[:, c, :, :], start=(c == 0), stop=(c == DC - 1))
                op.then_inc(s_sv, 1)

            def shift_row():
                pe.wait_ge(s_sve, 1)
                for p in range(PR):
                    op = pe.matmul(bank[6][0:B, 0:D], sa_v[:, p, :], wo_s[:, p, :], start=(p == 0), stop=(p == PR - 1))
                op.then_inc(p_r, 1)

            def keys_rest(s):
                if 2 <= s < 6:
                    features(LAST, 1, s - 2)
                if s == 4:
                    pe.wait_ge(s_krc, 2)
                    sums(LAST, 1)
                elif s == 5:
                    value_sums()
                elif s == 6:
                    shift_row()
                    contexts(LAST)

            def k_rows(i, wrap, late):
                pe.wait_ge(s_cur, i + 1)
                if wrap:
                    pe.wait_ge(s_ge, 8 * i)
                for half in range(2):
                    if late:
                        pe.wait_ge(s_rf, 8 * (i - 1) - 2 + half)
                    for q in range(4):
                        p = 4 * half + q
                        op = pe.matmul(bank[K_BANKS[half]][:, q * P:(q + 1) * P], k_cur[:, p:p + 1].to_broadcast([P, P]), ident[:, :], start=True, stop=True)
                    op.then_inc(s_kr, 1)

            def g_mm(i, k, wrap):
                if k == 0:
                    pe.wait_ge(s_bd, i + 1)
                    pe.wait_ge(s_sh, 8 * B + 8 * i + (4 if wrap else 7))
                elif k < 3:
                    if wrap:
                        pe.wait_ge(s_hh, 4 * (B + i - 1) + 2 * k)
                    else:
                        pe.wait_ge(p_rows, 1) if k == 1 else pe.wait_ge(s_cxe, B)
                else:
                    pe.wait_ge(s_ge, 8 * i + 4)
                for q in range(2):
                    p = 2 * k + q
                    op = pe.matmul(bank[G_BANKS[k]][:, q * D:(q + 1) * D], ctx_bd[:, p, :], wo_s[:, p, :], start=True, stop=True)
                op.then_inc(s_g, 1)

            def weight_transposes(m, p, first):
                pe.wait_ge(s_wl, m + 1)
                if not first:
                    pe.wait_ge(s_w, m)
                for part in range(2):
                    for j in range(TC):
                        op = pe.transpose(tr16[:, part, j * P:(j + 1) * P], w2[p % 2][:, part, j * P:(j + 1) * P], ident16[:, :])
                op.then_inc(s_wt, 1)

            def lora_in(i, att):
                pe.wait_ge(s_hT, 2 * (B + i))
                if att:
                    pe.wait_ge(s_ge, 8 * i + 2)
                for a in range(3):
                    st, mv = PARTS[a]
                    for c in range(DC):
                        op = pe.matmul(bank[Z_BANK][0:ZR, :], lora_a[:, st, c, :, :].rearrange("p g r -> p (g r)"), h2T[:, mv, c, :],
                                       start=(a == 0 and c == 0), stop=(a == 2 and c == DC - 1))
                op.then_inc(s_z, 1)

            def unit(i, u, att, late):
                if u == 0:
                    pe.wait_ge(s_ze, i)
                    if att:
                        pe.wait_ge(s_ge, 8 * i + 6)
                elif u == 1 and late:
                    pe.wait_ge(s_of, 2 * (i - 1))
                elif u == 2 and att:
                    pe.wait_ge(s_ge, 8 * i + 8)
                if u < FC:
                    if u >= 3:
                        pe.wait_ge(s_rf, 8 * (i - 1) + u - 2)
                    dst = bank[FFN_BANKS[u % 3]]
                    for a in range(3):
                        st, mv = PARTS[a]
                        for c in range(DC):
                            pe.matmul(dst[:, :], wi_s[:, st, c, u * P:(u + 1) * P], h2T[:, mv, c, :], start=(a == 0 and c == 0), stop=False)
                    pe.matmul(dst[:, :], lora_first[:, u * P:(u + 1) * P], z_s[:, :], start=False, stop=True).then_inc(s_f0, 1)
                if 1 <= u <= FC:
                    f = u - 1
                    pe.wait_ge(s_r0, 8 * (i - 1) + f + 1)
                    pe.matmul(bank[FFN_BANKS[f % 3]][:, :], lora_delta[:, f * P:(f + 1) * P], z_s[:, :], start=False, stop=True,
                              skip_group_check=True).then_inc(s_f1, 1)

            def ffn_out(i, j, last=False):
                out_bank = bank[END_BANKS[j // 2] if last else OUT_BANK]
                if j == 0 and not last:
                    pe.wait_ge(s_rf, 8 * (i - 1))
                elif j == 2 and not last:
                    pe.wait_ge(s_of, 2 * (i - 2) + 1)
                for f in range(FC):
                    if j == 0:
                        pe.wait_ge(s_rs, 8 * (i - 2) + f + 1)
                    for a in range(3):
                        st, mv = PARTS[a]
                        op = pe.matmul(out_bank[:, (j % 2) * D:(j % 2 + 1) * D], relu_sum[:, st, f, j * P:(j + 1) * P], wo2_s[:, mv, f, :],
                                       start=(f == 0 and a == 0), stop=(f == FC - 1 and a == 2))
                if j % 2:
                    op.then_inc(s_o, 1)

            def attention_out(i, j, pairs, att):
                k = j // 2
                if j == 0:
                    pe.wait_ge(s_w, 8 * i - 1) if pairs.stop < PR else pe.wait_ge(s_w, 8 * i)
                    pe.wait_ge(s_ge, 8 * i)
                if att and j % 2 == 0:
                    pe.wait_ge(s_krc, 2 * i + k + 1)
                for p in pairs:
                    for a in range(3):
                        st, mv = PARTS[a]
                        op = pe.matmul(bank[Y_BANKS[k]][:, (j % 2) * D:(j % 2 + 1) * D], attw[:, st, p, j * P:(j + 1) * P], g_s[:, mv, p, :],
                                       start=(p == 0 and a == 0), stop=(p == PR - 1 and a == 2))
                if j % 2:
                    op.then_inc(s_y, 1)

            def query_projection(i, n, p, first=False):
                pe.wait_ge(s_pl, n - 1)
                if first:
                    pe.wait_ge(s_sh, 8 * B)
                project(n, p, i, wq_s, QUERY_BANKS)

            def iteration(i, att=True, wrap=True, late=True):
                for s in range(PR):
                    m = 8 * i + s
                    n = 8 * B + m
                    units = ffn_units(s, wrap, late)
                    ready = [lag for lag in finished(s) if live(s, lag, att, wrap)]
                    if att and s == 0:
                        query_projection(i, n, s)
                    if live(s, 1, att, wrap):
                        pe.wait_ge(s_ss, n - 1)
                        score(n - 1, (s - 1) % PR, QUERY_BANKS)
                        if wrap and s == 5:
                            pe.wait_ge(s_ze, i)
                        diag(n - 1, (s - 1) % PR, QUERY_BANKS, False)
                    if wrap and s == 1:
                        attention_out(i, 0, range(PR - 1), att)
                    if s == 1 and ready:
                        weight_transposes(m - 2, (s - 2) % PR, False)
                    for back, u in units[0]:
                        unit(i + 1 - back, u, att, late)
                    if len(ready) == 2:
                        weight_transposes(m - 3, 0, not wrap)
                    if att and s > 1:
                        query_projection(i, n, s)
                    if wrap and s == 4:
                        pe.wait_ge(s_xhat, B + i)
                        transpose_x(0, bank[H2_BANKS[0]])
                        transpose_x(1, bank[H2_BANKS[1]])
                    if att and wrap and s == 4:
                        g_mm(i, 0, wrap)
                    for back, u in units[1]:
                        unit(i + 1 - back, u, att, late)
                    if att and s == 0:
                        query_projection(i, n + 1, 1, first=not wrap)
                        k_rows(i, wrap, late)
                    if late and s == 0:
                        ffn_out(i, 0)
                    if ready and s != 1:
                        weight_transposes(m - 2, (s - 2) % PR, False)
                    if late and s == 0:
                        ffn_out(i, 1)
                    for back, u in units[2]:
                        unit(i + 1 - back, u, att, late)
                    if late and s == 3:
                        ffn_out(i, 2)
                        ffn_out(i, 3)
                    if wrap and s == 1:
                        attention_out(i, 0, range(PR - 1, PR), att)
                        attention_out(i, 1, range(PR), att)
                    if wrap and s == 2:
                        attention_out(i, 2, range(PR), att)
                        attention_out(i, 3, range(PR), att)
                    if not wrap:
                        keys_rest(s)
                    if att and s == (4 if wrap else 7):
                        for k in range(1 if wrap else 0, 3):
                            g_mm(i, k, wrap)
                    if wrap and s == 4:
                        lora_in(i, att)
                    if att and s == (4 if wrap else 7):
                        g_mm(i, 3, wrap)

            pe.wait_ge(w_lo, 7)
            pe.wait_ge(p_lora, 3)
            iteration(0, wrap=False, late=False)
            iteration(1, late=False)
            with pe.Fori(2, B) as i:
                iteration(i)
            iteration(B, att=False)
            unit(B, 8, False, True)
            for j in range(TC):
                ffn_out(B + 1, j, last=True)

        @block.scalar
        def _(act):
            act.wait_ge(s_small, 32)
            act.activation(silu_a[:, :, :], c_s[:, :, :], ACT.Exp, scale=-1.0).then_inc(p_exp, 1)

            def weight_hi(src, w, loaded):
                act.wait_ge(loaded, 16)
                act.activation(w, src, ACT.Copy, scale=W_UP).then_inc(w_hi, 1)

            def h_copy(n, c, dst, src, first=False):
                if c == 0:
                    act.wait_ge(s_modc, n + 1)
                    if not first:
                        act.wait_ge(s_hT, 2 * n)
                act.wait_ge(s_tr, 2 * n + c + 1)
                act.activation(dst[HI][c], src[:, :], ACT.Identity, bias=mod_cur[:, c:c + 1], scale=mod_cur[:, 2 + c:3 + c]).then_inc(s_hh, 1)
                act.activation(h_f[:, c, :], src[:, :], ACT.Identity, bias=mod_cur[:, c:c + 1], scale=mod_cur[:, 2 + c:3 + c]).then_inc(s_hh, 1)

            def hT_of(b):
                return [[hT[:, b, s, c, :] for c in range(DC)] for s in range(2)]

            def projection(n, p, banks, early):
                src = bank[banks[0][p % 2]]
                act.wait_ge(s_pm, n + 1)
                if not early:
                    act.wait_ge(s_dd, n - 1)
                act.activation(proj[p % 2][:, HI, :], src[:, :], ACT.Copy, scale=1.0 / W_UP).then_inc(s_pe, 1)
                if not early:
                    act.wait_ge(s_sl, n - 1)
                act.activation(sq_f[p % 2][:, :], src[:, :], ACT.Square, scale=math.sqrt(SQ_UP) / W_UP).then_inc(s_pe, 1)

            def key_exp(u, q):
                if q == 0:
                    act.wait_ge(s_nr, u + 1)
                part = scores[:, 2 * q:2 * q + 2, :, :]
                act.activation(part, part, ACT.Exp, bias=neg_ref[:, :]).then_inc(s_ke, 1)
                act.wait_ge(s_ke, 4 * u + q + 1)
                act.activation(kexp[:, HI, 2 * q:2 * q + 2, :, :], part, ACT.Copy).then_inc(s_kh, 1)

            def feature_copy(u, k):
                half, c = k // 2, k % 2
                act.wait_ge(s_ft, 4 * u + k + 1)
                act.activation(featT[:, c, 512 * half:512 * (half + 1)], bank[7][:, :], ACT.Copy, scale=ca_cur[:, c:c + 1]).then_inc(s_fte, 1)

            def ctx_copy(u):
                act.wait_ge(s_cx, u + 1)
                for q in range(2):
                    for g in range(2):
                        op = act.activation(ctx_raw[g * DH:(g + 1) * DH, u, 4 * q:4 * q + 4, :],
                                            bank[(7, 5)[q]][g * DH:(g + 1) * DH, :].rearrange("p (a m) -> p a m", m=P)[:, :, g * M:(g + 1) * M], ACT.Copy)
                op.then_inc(s_cxe, 1)

            def keys(b, par, has_u, has_next):
                for s in range(PR):
                    if not has_u or s > 0:
                        projection(8 * b + s, s, KEY_BANKS, early=not has_u and s < 2)
                    if has_u and s in KEY_STEPS:
                        key_exp(b - 1, KEY_STEPS.index(s))
                    if not has_u and 1 <= s < 7:
                        src, hi, _, loaded = late_weight(s - 1)
                        act.wait_ge(loaded, 16)
                        act.activation(src, src, ACT.Copy, scale=W_UP).then_inc(w_up, 1)
                        act.wait_ge(w_up, s)
                        act.activation(hi, src, ACT.Copy).then_inc(w_hi, 1)
                    if has_u and s >= 4:
                        feature_copy(b - 1, s - 4)
                    if has_next and s in (5, 6):
                        h_copy(b + 1, s - 5, hT_of(b + 1), bank[6])
                if has_next:
                    projection(8 * (b + 1), 0, KEY_BANKS, early=False)
                if has_u:
                    ctx_copy(b - 1)

            weight_hi(wk_f[:, :, :], wk_s[:, HI, :, :], s_wk)
            h_copy(0, 0, hT_of(0), bank[6], first=True)
            h_copy(0, 1, hT_of(0), bank[7], first=True)
            keys(0, 0, False, True)
            with act.Fori(0, B // 2 - 1) as h:
                keys(2 * h + 1, 1, True, True)
                keys(2 * h + 2, 0, True, True)
            keys(LAST, 1, True, False)

            def keys_rest(s):
                if s == 0:
                    act.wait_ge(s_gm, 1)
                    act.activation(scale_all[:, :], mref[:, :], ACT.Exp, bias=gmax[:, :]).then_inc(s_sc, 1)
                for q in {0: (0, 1), 1: (2, 3)}.get(s, ()):
                    key_exp(LAST, q)
                if 2 <= s < 6:
                    feature_copy(LAST, s - 2)
                if s == 6:
                    ctx_copy(LAST)

            h2 = [[h2T[:, s, c, :] for c in range(DC)] for s in range(2)]

            def unit(i, u, spare=False):
                n = 8 * (i - 1)
                if 0 <= u - 2 < FC and not spare:
                    f = u - 2
                    act.wait_ge(s_rf, n + f + 1)
                    act.activation(relu_sum[:, HI, f, :], sum_f[f % 2], ACT.Copy).then_inc(s_rh, 1)
                if u < FC:
                    act.wait_ge(s_f0, n + u + 1)
                    if spare and u >= 2:
                        act.wait_ge(s_rf, n + u - 1)
                    act.activation(relu0[u % 2], bank[FFN_BANKS[u % 3]][:, :], ACT.Relu, scale=val_abs[:, 0:1]).then_inc(s_r0, 1)
                if 0 <= u - 1 < FC:
                    f = u - 1
                    dst = bank[FFN_BANKS[f % 3]][:, :]
                    act.wait_ge(s_f1, n + f + 1)
                    act.activation(dst, dst, ACT.Relu, scale=val_abs[:, 1:2]).then_inc(s_r1, 1)

            def keep_x1(j):
                act.wait_ge(s_out, 16 * (j + 1))
                act.activation(o_s[:, 2:4, :], x1[:, 2:4, :], ACT.Copy).then_inc(s_oc, 1)

            def weights_hi(m, p, early):
                act.wait_ge(s_wf, m + 1)
                if not early:
                    act.wait_ge(s_wt, m - 1)
                act.activation(w2[p % 2][:, HI, :], qk[p % 2], ACT.Copy).then_inc(s_wh, 1)

            def weights_copy(m, p):
                act.wait_ge(s_wt, m + 1)
                act.activation(attw[:, :, p, :], tr16, ACT.Copy).then_inc(s_w, 1)

            def g_hi(i, p):
                act.wait_ge(s_g, 4 * i + p // 2 + 1)
                act.activation(g_s[:, HI, p, :], bank[G_BANKS[p // 2]][:, (p % 2) * D:(p % 2 + 1) * D], ACT.Copy,
                               scale=k_rec[:, p:p + 1]).then_inc(s_gh, 1)

            def query_exp(n, s):
                part = qexp[(s - 1) % 2][:, :, :]
                act.wait_ge(s_ss, n)
                act.activation(part, part, ACT.Exp).then_inc(s_qe, 1)

            def iteration(i, att=True, wrap=True, late=True):
                for s in range(PR):
                    m = 8 * i + s
                    n = 8 * B + m
                    units = ffn_units(s, wrap, late)
                    ready = [lag for lag in finished(s) if live(s, lag, att, wrap)]
                    if late and s == 1:
                        keep_x1(i - 2)
                    for back, u in units[0]:
                        unit(i + 1 - back, u, spare=not att and back == 1)
                    if att and s == 1:
                        if wrap:
                            act.wait_ge(s_qk, 8 * i)
                        for half in range(2):
                            act.wait_ge(s_kr, 2 * i + half + 1)
                            act.activation(k_row[:, 512 * half:512 * (half + 1)], bank[K_BANKS[half]][:, :], ACT.Copy).then_inc(s_krc, 1)
                    if live(s, 2, att, wrap):
                        weights_hi(m - 2, (s - 2) % PR, early=not wrap and s < 4)
                    if att and s == 4:
                        projection(n, s, QUERY_BANKS, early=False)
                    if wrap and s == 4:
                        h_copy(B + i - 1, 0, h2, bank[H2_BANKS[0]])
                    if att and s == 4:
                        query_exp(n, s)
                    if wrap and s == 4:
                        h_copy(B + i - 1, 1, h2, bank[H2_BANKS[1]])
                    if len(ready) == 2:
                        act.wait_ge(s_y, 2 * i) if wrap else act.wait_ge(s_kl, 3 * B)
                        weights_copy(m - 3, 0)
                    if s == 1 and ready:
                        weights_copy(m - 2, (s - 2) % PR)
                    if att and s not in UNITS and s != 4:
                        projection(n, s, QUERY_BANKS, early=False)
                    if live(s, 1, att, wrap) and s != 4:
                        query_exp(n, s)
                    if att and wrap and s == 4:
                        for p in range(4):
                            g_hi(i, p)
                    if att and s in UNITS:
                        projection(n, s, QUERY_BANKS, early=False)
                    for back, u in units[1]:
                        unit(i + 1 - back, u, spare=not att and back == 1)
                    if ready and s != 1:
                        weights_copy(m - 2, (s - 2) % PR)
                    for back, u in units[2]:
                        unit(i + 1 - back, u, spare=not att and back == 1)
                    if not wrap:
                        keys_rest(s)
                    if att and s == (4 if wrap else 7):
                        for p in range(4 if wrap else 0, 6):
                            g_hi(i, p)
                    if wrap and s == 4:
                        act.wait_ge(s_z, i)
                        act.activation(z_s[:, :], bank[Z_BANK][0:ZR, :], ACT.Copy, scale=1.0 / W_UP).then_inc(s_zh, 1)
                    if att and s == (4 if wrap else 7):
                        g_hi(i, 6)
                        g_hi(i, 7)

            iteration(0, wrap=False, late=False)
            iteration(1, late=False)
            with act.Fori(2, B) as i:
                iteration(i)
            iteration(B, att=False)
            unit(B, FC, spare=True)
            keep_x1(B - 1)

        @block.vector
        def _(dve):
            def ln_stats(n, src, mod, first=False):
                for j in range(TC):
                    op = dve.bn_stats(stats[:, j, :], src[:, j, :])
                op.then_inc(s_stat, 1)
                if not first:
                    dve.wait_ge(s_hh, 4 * n)
                dve.wait_ge(s_stat, n + 1)
                if not first:
                    dve.tensor_copy(mod_cur[:, :], mod).then_inc(s_modc, 1)
                for j in range(TC):
                    op = dve.bn_aggr(meanvar[:, j, :], stats[:, j, :])
                op.then_inc(s_agg, 1)
                dve.wait_ge(s_agg, n + 1)
                dve.tensor_scalar(var_eps[:, :], meanvar[:, :, 1], LN_EPS, None, ALU.add).then_inc(s_var, 1)

            def ln_apply(n, src, first=False):
                if not first:
                    dve.wait_ge(s_tr, 2 * n)
                dve.wait_ge(s_rstd, n + 1)
                for j in range(TC):
                    op = dve.tensor_scalar(xhat[:, j, :], src[:, j, :], meanvar[:, j, 0:1], rstd[:, j:j + 1], ALU.subtract, ALU.mult)
                op.then_inc(s_xhat, 1)

            def xhat_hi(n, par):
                dve.wait_ge(s_xhat, n + 1)
                dve.tensor_copy(xhat2[par][:, HI, :, :], xhat[:, :, :]).then_inc(s_xh, 1)

            def weight_lo(src, w, k):
                dve.wait_ge(w_hi, k + 1)
                dve.scalar_tensor_tensor(out=w[:, LO, :, :], in0=src, scalar=W_UP, in1=w[:, HI, :, :], op0=ALU.mult, op1=ALU.subtract).then_inc(w_lo, 1)

            def projection_lo(n, p, banks, early):
                dve.wait_ge(s_pe, 2 * n + 2)
                dve.scalar_tensor_tensor(out=proj[p % 2][:, LO, :], in0=bank[banks[0][p % 2]][:, :], scalar=1.0 / W_UP, in1=proj[p % 2][:, HI, :],
                                         op0=ALU.mult, op1=ALU.subtract).then_inc(s_pl, 1)
                if not early:
                    dve.wait_ge(s_dg, n - 1)
                dve.tensor_copy(sq[p % 2][:, HI, :], sq_f[p % 2][:, :]).then_inc(s_qh, 1)

            def score_max(n, p, banks):
                dve.wait_ge(s_dd, n + 1)
                dve.tensor_reduce(mx[:, p, :], heads(bank[banks[1][p % 2]][:, :]), AX.X, ALU.max).then_inc(s_mx, 1)

            def shifted_scores(n, p, dst, banks, query):
                dg = bank[banks[2]][:, 0:2 * TC]
                dve.wait_ge(s_dg, n + 1)
                if query:
                    dve.wait_ge(s_mx, n + 1)
                    dve.tensor_tensor(shift[p % 2][:, :], dg, mx[:, p, :], ALU.add).then_inc(s_sh, 1)
                else:
                    dve.tensor_copy(shift[p % 2][:, :], dg).then_inc(s_sh, 1)
                dve.wait_ge(s_sh, n + 1)
                dve.tensor_tensor(dst.rearrange("p t (a m) -> p (t a) m", m=M), heads(bank[banks[1][p % 2]][:, :]),
                                  shift[p % 2][:, :].unsqueeze(2).to_broadcast([P, 2 * TC, M]), ALU.subtract).then_inc(s_ss, 1)

            def batch_max(b):
                dve.wait_ge(s_mx, 8 * b + 8)
                dve.tensor_reduce(bmax[:, :], mx[:, :, :].rearrange("p a b -> p (a b)"), AX.X, ALU.max).then_inc(s_bm, 1)

            def reference_max(u):
                dve.wait_ge(s_bma, u + 1)
                dve.tensor_copy(ca_cur[:, :], modT[:, u, 2:4])
                dve.tensor_copy(mref[:, bass.ds(u, 1)], bmax_all[:, :])
                dve.tensor_scalar(neg_ref[:, :], bmax_all[:, :], -1.0, KEY_SHIFT, ALU.mult, ALU.add).then_inc(s_nr, 1)

            def sums_copy(u):
                dve.wait_ge(s_sum, u + 1)
                dve.tensor_copy(k_raw[:, u, :], bank[5][:, 0:PR])
                at = v_in[:, :, 0, bass.ds(u, 1)]
                dve.tensor_tensor(at, bank[5][:, PR:PR + DC].unsqueeze(2), ca_cur[:, :].unsqueeze(2), ALU.mult).then_inc(s_sume, 1)

            dve.memset(ones[:, :], 1.0)
            dve.memset(head_half[:, :], 0.0)
            dve.memset(lora_sign[:, :], W_UP).then_inc(c_dve, 1)
            dve.wait_ge(c_dve, 1)
            for g in range(2):
                dve.memset(head_half[g * DH:(g + 1) * DH, g:g + 1], 0.5 * DN * DN / SQ_UP)
            for g in range(3):
                op = dve.memset(lora_sign[g * TOPK * R:g * TOPK * R + R, :], -W_UP)
            op.then_inc(c_dve, 1)
            dve.wait_ge(s_x, 16)
            ln_stats(0, x_in, None, first=True)
            ln_apply(0, x_in, first=True)
            dve.wait_ge(p_exp, 1)
            dve.tensor_scalar(silu_b[:, :, :], silu_a[:, :, :], 1.0, None, ALU.add).then_inc(p_dve, 1)
            dve.wait_ge(p_dve, 1)
            dve.reciprocal(silu_a[:, :, :], silu_b[:, :, :]).then_inc(p_dve, 1)
            dve.wait_ge(p_dve, 2)
            dve.tensor_tensor(silu_c[:, :, :], c_s[:, :, :], silu_a[:, :, :], ALU.mult).then_inc(p_dve, 1)
            xhat_hi(0, 0)

            def mod_columns(k):
                mod_ps = bank[5 - k][:, 48 * k:48 * k + 32].rearrange("p (k b) -> p b k", b=B)
                dve.wait_ge(p_mod, k + 1)
                dve.tensor_copy(modT[:, :, 6 * k:6 * k + 2], mod_ps[:, :, 0:2])
                dve.tensor_scalar(modT[:, :, 6 * k + 2:6 * k + 4], mod_ps[:, :, 2:4], 1.0, None, ALU.add).then_inc(p_modT, 1)
                dve.wait_ge(p_modT, k + 1)

            mod_columns(0)
            dve.tensor_copy(mod_cur[:, :], modT[:, 0, 0:4]).then_inc(s_modc, 1)
            dve.tensor_copy(v_in[:, :, 1, :], modT[:, :, 0:2].rearrange("p b c -> p c b"))
            weight_lo(wk_f[:, :, :], wk_s, 0)
            mod_columns(1)
            dve.wait_ge(p_mod, 3)
            dve.tensor_copy(gates_raw[:, :, :], bank[3][0:B, :].rearrange("p (a d) -> p a d", a=2)).then_inc(p_gate, 1)
            dve.wait_ge(s_pre, 32)
            dve.tensor_scalar(pfeat_f[:, :], pfeat_f[:, :], DN, None, ALU.mult).then_inc(p_pf, 1)
            dve.wait_ge(p_pf, 1)
            dve.tensor_copy(pfeat[:, HI, :], pfeat_f[:, :]).then_inc(p_pf, 1)
            dve.wait_ge(p_pf, 2)
            dve.tensor_tensor(pfeat[:, LO, :], pfeat_f[:, :], pfeat[:, HI, :], ALU.subtract).then_inc(p_pf, 1)

            def lora_parts():
                dve.wait_ge(s_rest[3], 16 * 12)
                dve.wait_ge(c_dve, 2)
                dve.tensor_scalar(val_neg[:, :], val_s[:, :], -1.0 / W_UP, None, ALU.mult)
                dve.tensor_scalar(val_sign[:, :], val_s[:, :], 0.0, 2.0, ALU.is_ge, ALU.mult)
                dve.tensor_scalar(lora_first[:, :], lora_b_f[:, 0, :], W_UP, None, ALU.mult)
                dve.tensor_scalar(lora_delta[:, :], lora_b_f[:, 1, :], lora_sign[:, 0:1], None, ALU.mult)
                for g in range(3):
                    op = dve.tensor_scalar(lora_a[:, HI, :, g, :], lora_a_f[:, :, :], W_UP, None, ALU.mult)
                op.then_inc(p_lora, 1)
                dve.wait_ge(p_lora, 1)
                dve.scalar_tensor_tensor(out=val_abs[:, :], in0=val_s[:, :], scalar=1.0 / W_UP, in1=val_neg[:, :], op0=ALU.mult, op1=ALU.max)
                dve.tensor_scalar(val_sign[:, :], val_sign[:, :], -1.0, None, ALU.add)
                r = 2 * TOPK * R
                dve.scalar_tensor_tensor(out=lora_first[r:ZR, :], in0=lora_b_f[r:ZR, 0, :], scalar=W_UP, in1=lora_first[r:ZR, :], op0=ALU.mult, op1=ALU.subtract)
                dve.scalar_tensor_tensor(out=lora_delta[r:ZR, :], in0=lora_b_f[r:ZR, 1, :], scalar=lora_sign[r:ZR, 0:1], in1=lora_delta[r:ZR, :], op0=ALU.mult, op1=ALU.subtract)
                for g in range(3):
                    op = dve.scalar_tensor_tensor(out=lora_a[:, LO, :, g, :], in0=lora_a_f[:, :, :], scalar=W_UP, in1=lora_a[:, HI, :, g, :], op0=ALU.mult, op1=ALU.subtract)
                op.then_inc(p_lora, 1)
                dve.wait_ge(p_lora, 2)
                dve.tensor_tensor(val_pair[:, :], val_sign[:, 0:1], val_sign[:, 1:2], ALU.mult).then_inc(p_lora, 1)

            def gate_values():
                dve.wait_ge(p_gate, 1)
                dve.tensor_scalar(gates, gates_raw[:, :, :], -1.0, None, ALU.mult).then_inc(p_gate, 1)
                dve.wait_ge(p_gate, 2)
                dve.tensor_tensor(gate_abs, gates_raw[:, :, :], gates, ALU.max).then_inc(p_gate, 1)
                dve.wait_ge(p_gate, 3)
                dve.tensor_scalar(gates, gates_raw[:, :, :], 0.0, 2.0, ALU.is_ge, ALU.mult)
                dve.tensor_scalar(gate_abs, gate_abs, 0.25, None, ALU.max).then_inc(p_gate, 1)
                dve.wait_ge(p_gate, 4)
                dve.scalar_tensor_tensor(out=gates_raw[:, :, :], in0=gates, scalar=-1.0, in1=gate_abs, op0=ALU.add, op1=ALU.mult).then_inc(p_gate, 1)
                dve.wait_ge(p_gate, 5)

            def keys(b, par, has_u, has_next):
                for s in range(PR):
                    n = 8 * b + s
                    if has_u and s < 2 or s >= 2 and True:
                        if has_u and s >= 2:
                            dve.wait_ge(s_kl0, b) if s < 4 else dve.wait_ge(s_kl, 3 * (b - 1) + (s - 2) // 2)
                        shifted_scores(n - 2, (s - 2) % PR, scores[:, (s - 2) % PR, :, :], KEY_BANKS, False)
                    if has_u and s == 0:
                        score_max(n - 1, PR - 1, KEY_BANKS)
                        batch_max(b - 1)
                    projection_lo(n, s, KEY_BANKS, early=not has_u and s < 2)
                    if has_u and s == 0:
                        reference_max(b - 1)
                    if s >= 1:
                        if has_u and s == 1:
                            dve.wait_ge(s_bm, b)
                        score_max(n - 1, (s - 1) % PR, KEY_BANKS)
                    if has_u and s == 1:
                        dve.wait_ge(s_kh, 4 * (b - 1) + 1)
                        dve.tensor_tensor(kexp[:, LO, 0:2, :, :], scores[:, 0:2, :, :], kexp[:, HI, 0:2, :, :], ALU.subtract).then_inc(s_kl0, 1)
                    if s >= 2 and not (True):
                        if has_u and s >= 2:
                            dve.wait_ge(s_kl0, b) if s < 4 else dve.wait_ge(s_kl, 3 * (b - 1) + (s - 2) // 2)
                        shifted_scores(n - 2, (s - 2) % PR, scores[:, (s - 2) % PR, :, :], KEY_BANKS, False)
                    if has_next and s == 3:
                        dve.wait_ge(s_x, 16 * (b + 2))
                        ln_stats(b + 1, x_in, modT[:, b + 1, 0:4])
                    if has_next and s == 4:
                        dve.wait_ge(s_xl, b + 1)
                        ln_apply(b + 1, x_in)
                if has_u:
                    sums_copy(b - 1)
                if has_next:
                    xhat_hi(b + 1, 1 - par)

            keys(0, 0, False, True)
            lora_parts()
            gate_values()
            with dve.Fori(0, B // 2 - 1) as h:
                keys(2 * h + 1, 1, True, True)
                keys(2 * h + 2, 0, True, True)
            keys(LAST, 1, True, False)
            score_max(8 * B - 1, PR - 1, KEY_BANKS)
            batch_max(LAST)
            for p in (PR - 2, PR - 1):
                shifted_scores(8 * (B - 1) + p, p, scores[:, p, :, :], KEY_BANKS, False)
            reference_max(LAST)
            dve.wait_ge(s_nr, B)
            dve.tensor_reduce(gmax[:, :], mref[:, :], AX.X, ALU.max, negate=True).then_inc(s_gm, 1)

            def keys_rest(s):
                if s == 5:
                    sums_copy(LAST)
                    dve.tensor_scalar(gate_row[:, 0, :], gates_raw[:, 0, :], 1.0 / ATT_UP, None, ALU.mult)
                    dve.tensor_scalar(gate_row[:, 2, :], gates_raw[:, 1, :], val_sign[0:B, 0:1], 1.0 / W_UP, ALU.mult, ALU.mult)
                elif s == 6:
                    dve.wait_ge(s_sv, 1)
                    v_ps = bank[6][:, 0:2 * B * PR].rearrange("p (a s b) -> p s a b", s=2, b=B)
                    dve.tensor_copy(v_raw[:, :, :].rearrange("p b a -> p a b"), v_ps[:, 0, :, :])
                    dve.tensor_copy(sa_v[:, :, :], v_ps[:, 1, :, :]).then_inc(s_sve, 1)
                elif s == 7:
                    dve.wait_ge(p_r, 1)
                    dve.wait_ge(s_wv, 48)
                    dve.tensor_tensor(gate_sum, bank[6][0:B, 0:D], bo_s[:, :], ALU.add).then_inc(p_gate, 1)
                    dve.wait_ge(p_gate, 6)
                    dve.tensor_tensor(gate_row[:, 1, :], gate_sum, gates_raw[:, 0, :], ALU.mult).then_inc(p_rows, 1)

            def current_k(i):
                dve.wait_ge(s_cur_a, 2 * i + 1)
                dve.tensor_copy(scale_cur[:, :], scale_all[:, bass.ds(i, 1)])
                dve.tensor_copy(k_cur[:, :], k_raw[:, i, :]).then_inc(s_cur_a, 1)
                dve.wait_ge(s_cur_a, 2 * i + 2)
                dve.tensor_scalar(k_cur[:, :], k_cur[:, :], scale_cur[:, 0:1], T * EPS, ALU.mult, ALU.add).then_inc(s_cur_a, 1)
                dve.wait_ge(s_cur_a, 2 * i + 3)
                dve.reciprocal(k_rec[:, :], k_cur[:, :]).then_inc(s_cur, 1)

            def current_contexts(i, first):
                if first:
                    dve.wait_ge(s_sve, 1)
                dve.tensor_scalar(v_cur[:, :], v_raw[:, i, :], EPS, None, ALU.mult).then_inc(s_vc, 1)
                dve.wait_ge(s_vc, i + 1)
                for g in range(2):
                    rows = slice(g * DH, (g + 1) * DH)
                    op = dve.scalar_tensor_tensor(out=ctx_bd[rows, :, g * M:(g + 1) * M], in0=ctx_raw[rows, i, :, :], scalar=scale_cur[rows, 0:1],
                                                  in1=v_cur[rows, :].unsqueeze(2).to_broadcast([DH, PR, M]), op0=ALU.mult, op1=ALU.add)
                op.then_inc(s_bd, 1)

            def query_weights(i, m, p, early):
                dve.wait_ge(s_qe, m + 1)
                if p == 0:
                    dve.wait_ge(s_krc, 2 * i + 2)
                if not early:
                    dve.wait_ge(s_wl, m - 1)
                dve.scalar_tensor_tensor(out=qk[p % 2].rearrange("p (a b) -> p a b", b=P), in0=qexp[p % 2][:, :, :], scalar=EPS,
                                         in1=k_row[:, p * P:(p + 1) * P].unsqueeze(1).to_broadcast([P, TC, P]), op0=ALU.add, op1=ALU.mult).then_inc(s_qk, 1)
                dve.wait_ge(s_qk, m + 1)
                dve.tensor_reduce(qsum[p % 2][:, :], heads(qk[p % 2]), AX.X, ALU.add).then_inc(s_qs, 1)
                dve.wait_ge(s_qs, 2 * m + 1)
                dve.tensor_scalar(qsum[p % 2][:, :], qsum[p % 2][:, :], 1.0 / ATT_UP, None, ALU.mult).then_inc(s_qs, 1)
                dve.wait_ge(s_qs, 2 * m + 2)
                dve.reciprocal(qrec[p % 2][:, :], qsum[p % 2][:, :]).then_inc(s_qr, 1)

            def out_rows(j, k, last=False):
                rows = bank[END_BANKS[k] if last else OUT_BANK][:, :].rearrange("p (a d) -> p a d", d=D)
                if k == 0:
                    dve.wait_ge(s_rowg, 16 * (j + 1))
                    dve.wait_ge(s_out, 16 * (j + 1))
                dve.wait_ge(s_o, 2 * j + k + 1)
                dve.tensor_tensor(rows, rows, row_g[:, :].unsqueeze(1).to_broadcast([P, 2, D]), ALU.mult).then_inc(s_og, 1)
                dve.wait_ge(s_og, 2 * j + k + 1)
                rest = x1[:, 0:2, :]
                if k == 1:
                    dve.wait_ge(s_oc, j + 1)
                    rest = o_s[:, 2:4, :]
                dve.tensor_tensor(o_s[:, 2 * k:2 * k + 2, :], rows, rest, ALU.add).then_inc(s_of, 1)

            def y_rows(j, k, late):
                rows = bank[Y_BANKS[k]][:, :].rearrange("p (a d) -> p a d", d=D)
                if k == 0:
                    dve.wait_ge(s_rowa, 16 * (j + 1))
                    dve.wait_ge(s_xr, 2 * j + 2)
                if late:
                    dve.wait_ge(s_of, 2 * j - 1) if k == 0 else dve.wait_ge(s_oc, j)
                dve.wait_ge(s_y, 2 * j + k + 1)
                dve.tensor_tensor(rows, rows, row_a[:, 0, :].unsqueeze(1).to_broadcast([P, 2, D]), ALU.mult).then_inc(s_yg, 1)
                dve.wait_ge(s_yg, 2 * j + k + 1)
                dve.tensor_tensor(x1[:, 2 * k:2 * k + 2, :], rows, x_rest[:, 2 * k:2 * k + 2, :], ALU.add).then_inc(s_yr, 1)

            def unit(i, u, spare=False):
                f = u - 1
                if 0 <= f < FC:
                    n = 8 * (i - 1) + f
                    dve.wait_ge(s_r1, n + 1)
                    if f >= 2:
                        dve.wait_ge(s_rs, n - 1)
                    dve.scalar_tensor_tensor(out=sum_f[f % 2], in0=bank[FFN_BANKS[f % 3]][:, :], scalar=val_pair[:, 0:1], in1=relu0[f % 2],
                                             op0=ALU.mult, op1=ALU.add).then_inc(s_rf, 1)
                    if spare:
                        dve.wait_ge(s_rf, n + 1)
                        dve.tensor_copy(relu_sum[:, HI, f, :], sum_f[f % 2]).then_inc(s_rh, 1)

            def g_lo(i, p):
                dve.wait_ge(s_gh, 8 * i + 2 * (p // 2) + 2)
                dve.scalar_tensor_tensor(out=g_s[:, LO, p, :], in0=bank[G_BANKS[p // 2]][:, (p % 2) * D:(p % 2 + 1) * D],
                                         scalar=k_rec[:, p:p + 1], in1=g_s[:, HI, p, :], op0=ALU.mult, op1=ALU.subtract).then_inc(s_ge, 1)

            def iteration(i, att=True, wrap=True, late=True, ahead=True):
                for s in range(PR):
                    m = 8 * i + s
                    n = 8 * B + m
                    units = ffn_units(s, wrap, late)
                    if not wrap:
                        keys_rest(s)
                    for back, u in (units[0] if s == 0 else []):
                        unit(i + 1 - back, u, spare=not att and back == 1)
                    if wrap and s == 3:
                        y_rows(i - 1, 1, late)
                    if late and s == 5:
                        out_rows(i - 2, 1)
                    if live(s, 1, att, wrap):
                        score_max(n - 1, (s - 1) % PR, QUERY_BANKS)
                        if wrap or s >= 3:
                            dve.wait_ge(s_qk, m - 2)
                        shifted_scores(n - 1, (s - 1) % PR, qexp[(s - 1) % 2][:, :, :], QUERY_BANKS, True)
                    if late and s == 1:
                        out_rows(i - 2, 0)
                    if wrap and s == 2:
                        y_rows(i - 1, 0, late)
                    if wrap and s == 3:
                        dve.wait_ge(s_yr, 2 * i)
                        ln_stats(B + i - 1, x1, modT[:, i - 1, 6:10])
                    for back, u in (units[0] if s > 0 else []):
                        unit(i + 1 - back, u, spare=not att and back == 1)
                    if att:
                        projection_lo(n, s, QUERY_BANKS, False)
                    if not wrap and s == 0:
                        dve.wait_ge(s_sc, 1)
                        dve.tensor_scalar(scale_all[:, :], scale_all[:, :], 2.0 ** -KEY_UP, None, ALU.mult).then_inc(s_cur_a, 1)
                        current_k(i)
                    if ahead and wrap and s == 7:
                        current_k(i + 1)
                    for back, u in units[1]:
                        unit(i + 1 - back, u, spare=not att and back == 1)
                    if live(s, 1, att, wrap):
                        query_weights(i, m - 1, (s - 1) % PR, early=not wrap and s < 3)
                    if wrap and s == 3:
                        ln_apply(B + i - 1, x1)
                    for back, u in units[2]:
                        unit(i + 1 - back, u, spare=not att and back == 1)
                    if att and s == (2 if wrap else 6):
                        current_contexts(i, first=not wrap)
                    if att and s == (4 if wrap else 7):
                        for p in range(6):
                            g_lo(i, p)
                    if not att and s == 4:
                        dve.wait_ge(s_hh, 4 * (B + i))
                        dve.wait_ge(s_hT, 2 * (B + i) - 1)
                        dve.tensor_tensor(h2T[:, LO, 1, :], h_f[:, 1, :], h2T[:, HI, 1, :], ALU.subtract).then_inc(s_hT, 1)
                    if wrap and s == 4:
                        r = TOPK * R
                        dve.wait_ge(s_zh, i)
                        dve.scalar_tensor_tensor(out=z_s[r:2 * r, :], in0=bank[Z_BANK][r:2 * r, :], scalar=1.0 / W_UP, in1=z_s[r:2 * r, :],
                                                 op0=ALU.mult, op1=ALU.subtract).then_inc(s_ze, 1)
                    if att and s == (4 if wrap else 7):
                        g_lo(i, 6)
                        g_lo(i, 7)
                    if not wrap and s == 7:
                        current_k(i + 1)

            iteration(0, wrap=False, late=False)
            iteration(1, late=False)
            with dve.Fori(2, LAST) as i:
                iteration(i)
            iteration(LAST, ahead=False)
            iteration(B, att=False, ahead=False)
            unit(B, FC, spare=True)
            out_rows(B - 1, 0, last=True)
            out_rows(B - 1, 1, last=True)


_INS = ["L0_attn_x", "L0_attn_Wq", "L0_attn_Wk", "L0_attn_Wv", "L0_attn_Wo", "L0_attn_bo"]


def kernel(**inputs):
    import numpy as np
    import concourse.bacc as bacc
    from concourse.bass_utils import run_bass_kernel_spmd

    f = "L0_ffn_"
    arrays = {name: np.asarray(inputs[name]) for name in _INS}
    arrays["P_t"] = np.asarray(inputs["L0_attn_P"]).T
    arrays["wi_t"] = np.asarray(inputs[f + "wi_w"]).T
    arrays["wo_t"] = np.asarray(inputs[f + "wo_w"]).T
    arrays["lora_a_t"] = np.asarray(inputs[f + "lora_As"]).transpose(0, 2, 1)
    arrays["lora_b_t"] = np.asarray(inputs[f + "lora_Bs"]).transpose(0, 2, 1)
    arrays["index"] = np.asarray(inputs[f + "top_k_indices"])
    arrays["value"] = np.asarray(inputs[f + "top_k_values"])
    arrays["c_t"] = np.asarray(inputs["L0_c"]).T
    arrays["wmod"] = np.asarray(inputs["L0_wmod"])
    arrays = {"in_" + k: np.ascontiguousarray(a) for k, a in arrays.items()}
    nc = bacc.Bacc("TRN2", target_bir_lowering=False, num_devices=1)
    args = [nc.dram_tensor(k, a.shape, mybir.dt.from_np(a.dtype), kind="ExternalInput").ap() for k, a in arrays.items()]
    args.append(nc.dram_tensor("out_x", (B, T, D), F32, kind="ExternalOutput").ap())
    build(nc, *args)
    return run_bass_kernel_spmd(nc, [arrays], core_ids=[0]).results[0]["out_x"]
```
